# Optimizing a Trainium2 kernel written in Bass

```python
import numpy as np
import jax
import jax.numpy as jnp

def _softmax(x, axis=-1):
    return jax.nn.softmax(x, axis=axis)

def _gelu(x):
    return jax.nn.gelu(x, approximate=True)

def _silu(x):
    return jax.nn.silu(x)

def _sigmoid(x):
    return jax.nn.sigmoid(x)

def _layernorm(x, axis=-1, eps=1e-05):
    m = jnp.mean(x, axis=axis, keepdims=True)
    v = jnp.var(x, axis=axis, keepdims=True)
    return (x - m) / jnp.sqrt(v + eps)

def _scatter_add(tgt, idx, src, axis=0):
    return tgt.at[idx].add(src)

def _segment_sum(src, seg, n):
    return jax.ops.segment_sum(src, seg, n)
kernel_name = 'mk_perceiver_d2_seqx_r2_2bd3a8'

def setup_inputs(seed: int=0):
    np.random.seed(seed)
    _w = jnp.asarray

    def _rec_inputs():
        import jax
        import jax.numpy as jnp
        _rk = jax.random.key(seed)
        x = 0.002226 + 0.9996 * jax.random.normal(jax.random.fold_in(_rk, 1), (4, 128, 512), jnp.float32)
        _lenS = 128 - jax.random.randint(jax.random.fold_in(_rk, 7), (4,), 0, max(1, 128 // 4) + 1, jnp.int32)
        _lenS2 = 2048 - jax.random.randint(jax.random.fold_in(_rk, 8), (4,), 0, max(1, 2048 // 4) + 1, jnp.int32)
        _ctx_1024P = jax.random.normal(jax.random.fold_in(_rk, 11), (4, 16, 512), jnp.float32)
        _ctx_1024c = jax.random.dirichlet(jax.random.fold_in(_rk, 511), 0.3 * jnp.ones((16,), jnp.float32), (4, 2048))
        _ctx_1024t = jnp.einsum('bsk,bkd->bsd', _ctx_1024c, _ctx_1024P)
        _ctx_1024t = _ctx_1024t * jax.lax.rsqrt(jnp.mean(jnp.square(_ctx_1024t)) + 1e-12) * 0.953939
        ctx_1024 = -7.10856e-05 + 0.999911 * (_ctx_1024t + 0.3 * jax.random.normal(jax.random.fold_in(_rk, 611), (4, 2048, 512), jnp.float32))
        _validS = jnp.arange(128)[None, :] < _lenS[:, None]
        _validS2 = jnp.arange(2048)[None, :] < _lenS2[:, None]
        _causal = jnp.tril(jnp.ones((128, 128), dtype=bool))
        mask_BxS2_bk0 = jnp.logical_not(jnp.broadcast_to(_validS2[:, :], (4, 2048)))
        return (x, ctx_1024, mask_BxS2_bk0)
    x, ctx_1024, mask_BxS2_bk0 = _rec_inputs()

    def _L0_xattn_setup():
        import jax, jax.numpy as jnp
        import numpy as np
        DIM, DIM_HEAD, HEADS, SCALE = (512, 64, 8, 8.0)
        INNER = DIM_HEAD * HEADS
        LN_EPS = 1e-05
        L2_EPS = 1e-12

        def layer_norm(x, w, b):
            mu = jnp.mean(x, axis=-1, keepdims=True)
            var = jnp.mean(jnp.square(x - mu), axis=-1, keepdims=True)
            return (x - mu) * jax.lax.rsqrt(var + LN_EPS) * w + b

        def l2norm(t):
            n = jnp.sqrt(jnp.sum(jnp.square(t), axis=-1, keepdims=True))
            return t / jnp.maximum(n, L2_EPS)
        key = jax.random.key(seed)
        ks = jax.random.split(key, 8)
        b, n, m = (8, 4096, 64)
        x = jax.random.normal(ks[0], (b, n, DIM), dtype=jnp.float32)
        latents = jax.random.normal(ks[1], (b, m, DIM), dtype=jnp.float32)
        mask = jax.random.randint(ks[2], (b, n), 0, 2) > 0
        Wq = jax.random.normal(ks[3], (DIM, INNER), dtype=jnp.float32) * DIM ** (-0.5)
        Wkv = jax.random.normal(ks[4], (DIM, 2 * INNER), dtype=jnp.float32) * DIM ** (-0.5)
        Wo = jax.random.normal(ks[5], (INNER, DIM), dtype=jnp.float32) * INNER ** (-0.5)
        return {'x': x, 'latents': latents, 'mask': mask, 'ln_x_w': jnp.ones((DIM,)), 'ln_x_b': jnp.zeros((DIM,)), 'ln_l_w': jnp.ones((DIM,)), 'ln_l_b': jnp.zeros((DIM,)), 'Wq': Wq, 'Wkv': Wkv, 'q_scale': jnp.ones((DIM_HEAD,)), 'k_scale': jnp.ones((DIM_HEAD,)), 'Wo': Wo, 'ln_o_w': jnp.ones((DIM,)), 'ln_o_b': jnp.zeros((DIM,))}
    _L0_xattn_all = _L0_xattn_setup()
    _L0_xattn_in = {k: v for k, v in _L0_xattn_all.items() if k in ('ln_x_w', 'ln_x_b', 'ln_l_w', 'ln_l_b', 'Wq', 'Wkv', 'q_scale', 'k_scale', 'Wo', 'ln_o_w', 'ln_o_b')}
    del _L0_xattn_all

    def _L0_attn_setup():
        import jax, jax.numpy as jnp
        import numpy as np
        EPS = 1e-06

        def _rmsnorm(x, w):
            dt = x.dtype
            xf = x.astype(jnp.float32)
            var = jnp.mean(xf * xf, axis=-1, keepdims=True)
            xf = xf * jax.lax.rsqrt(var + EPS)
            return xf.astype(dt) * w
        key = jax.random.key(seed)
        ks = jax.random.split(key, 4)
        B, N, C = (4, 1024, 512)
        H = 16
        D = C // H
        x = jax.random.normal(ks[0], (B, N, C), dtype=jnp.float32)
        W_qkv = jax.random.normal(ks[1], (C, 3 * C), dtype=jnp.float32) * (1.0 / np.sqrt(C))
        b_qkv = jnp.zeros((3 * C,), dtype=jnp.float32)
        W_proj = jax.random.normal(ks[2], (C, C), dtype=jnp.float32) * (1.0 / np.sqrt(C))
        b_proj = jnp.zeros((C,), dtype=jnp.float32)
        qn_w = jnp.ones((D,), dtype=jnp.float32)
        kn_w = jnp.ones((D,), dtype=jnp.float32)
        return {'x': x, 'W_qkv': W_qkv, 'b_qkv': b_qkv, 'W_proj': W_proj, 'b_proj': b_proj, 'qn_w': qn_w, 'kn_w': kn_w}
    _L0_attn_all = _L0_attn_setup()
    _L0_attn_in = {k: v for k, v in _L0_attn_all.items() if k in ('W_qkv', 'b_qkv', 'W_proj', 'b_proj', 'qn_w', 'kn_w')}
    del _L0_attn_all

    def _L0_ffn_setup():
        import jax, jax.numpy as jnp
        import numpy as np
        DIM = 512

        def _reference_tuple_inner(x, W_r, W_k, W_v, mu_r, mu_k):
            B, T, C = x.shape
            x_prev = jnp.concatenate([jnp.zeros((B, 1, C), x.dtype), x[:, :-1, :]], axis=1)
            xr = mu_r * x + (1.0 - mu_r) * x_prev
            xk = mu_k * x + (1.0 - mu_k) * x_prev
            r = jax.nn.sigmoid(jnp.einsum('btc,dc->btd', xr, W_r))
            k = jnp.einsum('btc,dc->btd', xk, W_k)
            k_act = jnp.square(jax.nn.relu(k))
            out = r * jnp.einsum('btc,dc->btd', k_act, W_v)
            new_state = x[:, -1, :]
            return (out, new_state)
        key = jax.random.key(seed)
        ks = jax.random.split(key, 6)
        B, T, C = (8, 1024, DIM)
        x = jax.random.normal(ks[0], (B, T, C), dtype=jnp.float32)
        s = 1.0 / np.sqrt(C)
        W_r = jax.random.uniform(ks[1], (C, C), jnp.float32, -s, s)
        W_k = jax.random.uniform(ks[2], (C, C), jnp.float32, -s, s)
        W_v = jax.random.uniform(ks[3], (C, C), jnp.float32, -s, s)
        mu_r = jax.random.uniform(ks[4], (C,), jnp.float32)
        mu_k = jax.random.uniform(ks[5], (C,), jnp.float32)
        return {'x': x, 'W_r': W_r, 'W_k': W_k, 'W_v': W_v, 'mu_r': mu_r, 'mu_k': mu_k}
    _L0_ffn_all = _L0_ffn_setup()
    _L0_ffn_in = {k: v for k, v in _L0_ffn_all.items() if k in ('W_r', 'W_k', 'W_v', 'mu_r', 'mu_k')}
    del _L0_ffn_all

    def _L1_xattn_setup():
        import jax, jax.numpy as jnp
        import numpy as np
        D_MODEL = 512
        N_HEADS = 16
        HEAD_DIM = D_MODEL // N_HEADS
        key = jax.random.key(seed)
        ks = jax.random.split(key, 6)
        B, T, S = (4, 512, 1024)
        scale = 1.0 / np.sqrt(D_MODEL)
        return {'query': jax.random.normal(ks[0], (B, T, D_MODEL), jnp.float32), 'key_value': jax.random.normal(ks[1], (B, S, D_MODEL), jnp.float32), 'wq': jax.random.normal(ks[2], (D_MODEL, D_MODEL), jnp.float32) * scale, 'wk': jax.random.normal(ks[3], (D_MODEL, D_MODEL), jnp.float32) * scale, 'wv': jax.random.normal(ks[4], (D_MODEL, D_MODEL), jnp.float32) * scale, 'wo': jax.random.normal(ks[5], (D_MODEL, D_MODEL), jnp.float32) * scale}
    _L1_xattn_all = _L1_xattn_setup()
    _L1_xattn_in = {k: v for k, v in _L1_xattn_all.items() if k in ('wq', 'wk', 'wv', 'wo')}
    del _L1_xattn_all

    def _L1_attn_setup():
        import jax, jax.numpy as jnp
        import numpy as np
        N_HEAD = 16
        EPS = 1e-05
        ROPE_BASE = 10000.0
        key = jax.random.key(seed)
        ks = jax.random.split(key, 6)
        B, T, C = (2, 1024, 512)
        s = 0.02
        return {'x': jax.random.normal(ks[0], (B, T, C), dtype=jnp.float32), 'wq': jax.random.normal(ks[1], (C, C), dtype=jnp.float32) * s, 'wk': jax.random.normal(ks[2], (C, C), dtype=jnp.float32) * s, 'wv': jax.random.normal(ks[3], (C, C), dtype=jnp.float32) * s, 'wproj': jax.random.normal(ks[4], (C, C), dtype=jnp.float32) * s, 'g_rms': jnp.ones((C // N_HEAD,), dtype=jnp.float32)}
    _L1_attn_all = _L1_attn_setup()
    _L1_attn_in = {k: v for k, v in _L1_attn_all.items() if k in ('wq', 'wk', 'wv', 'wproj', 'g_rms')}
    del _L1_attn_all

    def _L1_ffn_setup():
        import jax, jax.numpy as jnp
        import numpy as np
        B, S, H, E, DFF = (4, 2048, 512, 8, 2048)
        key = jax.random.key(seed)
        k0, k1, k2, k3 = jax.random.split(key, 4)
        hidden_states = jax.random.normal(k0, (B, S, H), dtype=jnp.float32)
        gate_w = jax.random.normal(k1, (E, H), dtype=jnp.float32) * 0.02
        w1 = jax.random.normal(k2, (E, H, DFF), dtype=jnp.float32) * 0.02
        b1 = jnp.zeros((E, DFF), dtype=jnp.float32)
        w2 = jax.random.normal(k3, (E, DFF, H), dtype=jnp.float32) * 0.02
        b2 = jnp.zeros((E, H), dtype=jnp.float32)
        return {'hidden_states': hidden_states, 'gate_w': gate_w, 'w1': w1, 'b1': b1, 'w2': w2, 'b2': b2}
    _L1_ffn_all = _L1_ffn_setup()
    _L1_ffn_in = {k: v for k, v in _L1_ffn_all.items() if k in ('gate_w', 'w1', 'b1', 'w2', 'b2')}
    del _L1_ffn_all
    return {'x': x, 'ctx_1024': ctx_1024, 'mask_BxS2_bk0': mask_BxS2_bk0, 'L0_xattn_ln_x_w': _L0_xattn_in['ln_x_w'], 'L0_xattn_ln_x_b': _L0_xattn_in['ln_x_b'], 'L0_xattn_ln_l_w': _L0_xattn_in['ln_l_w'], 'L0_xattn_ln_l_b': _L0_xattn_in['ln_l_b'], 'L0_xattn_Wq': _L0_xattn_in['Wq'], 'L0_xattn_Wkv': _L0_xattn_in['Wkv'], 'L0_xattn_q_scale': _L0_xattn_in['q_scale'], 'L0_xattn_k_scale': _L0_xattn_in['k_scale'], 'L0_xattn_Wo': _L0_xattn_in['Wo'], 'L0_xattn_ln_o_w': _L0_xattn_in['ln_o_w'], 'L0_xattn_ln_o_b': _L0_xattn_in['ln_o_b'], 'L0_attn_W_qkv': _L0_attn_in['W_qkv'], 'L0_attn_b_qkv': _L0_attn_in['b_qkv'], 'L0_attn_W_proj': _L0_attn_in['W_proj'], 'L0_attn_b_proj': _L0_attn_in['b_proj'], 'L0_attn_qn_w': _L0_attn_in['qn_w'], 'L0_attn_kn_w': _L0_attn_in['kn_w'], 'L0_ffn_W_r': _L0_ffn_in['W_r'], 'L0_ffn_W_k': _L0_ffn_in['W_k'], 'L0_ffn_W_v': _L0_ffn_in['W_v'], 'L0_ffn_mu_r': _L0_ffn_in['mu_r'], 'L0_ffn_mu_k': _L0_ffn_in['mu_k'], 'L1_xattn_wq': _L1_xattn_in['wq'], 'L1_xattn_wk': _L1_xattn_in['wk'], 'L1_xattn_wv': _L1_xattn_in['wv'], 'L1_xattn_wo': _L1_xattn_in['wo'], 'L1_attn_wq': _L1_attn_in['wq'], 'L1_attn_wk': _L1_attn_in['wk'], 'L1_attn_wv': _L1_attn_in['wv'], 'L1_attn_wproj': _L1_attn_in['wproj'], 'L1_attn_g_rms': _L1_attn_in['g_rms'], 'L1_ffn_gate_w': _L1_ffn_in['gate_w'], 'L1_ffn_w1': _L1_ffn_in['w1'], 'L1_ffn_b1': _L1_ffn_in['b1'], 'L1_ffn_w2': _L1_ffn_in['w2'], 'L1_ffn_b2': _L1_ffn_in['b2']}

def reference(x, ctx_1024, mask_BxS2_bk0, L0_xattn_ln_x_w, L0_xattn_ln_x_b, L0_xattn_ln_l_w, L0_xattn_ln_l_b, L0_xattn_Wq, L0_xattn_Wkv, L0_xattn_q_scale, L0_xattn_k_scale, L0_xattn_Wo, L0_xattn_ln_o_w, L0_xattn_ln_o_b, L0_attn_W_qkv, L0_attn_b_qkv, L0_attn_W_proj, L0_attn_b_proj, L0_attn_qn_w, L0_attn_kn_w, L0_ffn_W_r, L0_ffn_W_k, L0_ffn_W_v, L0_ffn_mu_r, L0_ffn_mu_k, L1_xattn_wq, L1_xattn_wk, L1_xattn_wv, L1_xattn_wo, L1_attn_wq, L1_attn_wk, L1_attn_wv, L1_attn_wproj, L1_attn_g_rms, L1_ffn_gate_w, L1_ffn_w1, L1_ffn_b1, L1_ffn_w2, L1_ffn_b2):
    import jax
    import jax.numpy as jnp

    def _L0_xattn_ref(x, latents, mask, ln_x_w, ln_x_b, ln_l_w, ln_l_b, Wq, Wkv, q_scale, k_scale, Wo, ln_o_w, ln_o_b):
        import jax, jax.numpy as jnp
        import numpy as np
        DIM, DIM_HEAD, HEADS, SCALE = (512, 64, 8, 8.0)
        INNER = DIM_HEAD * HEADS
        LN_EPS = 1e-05
        L2_EPS = 1e-12

        def layer_norm(x, w, b):
            mu = jnp.mean(x, axis=-1, keepdims=True)
            var = jnp.mean(jnp.square(x - mu), axis=-1, keepdims=True)
            return (x - mu) * jax.lax.rsqrt(var + LN_EPS) * w + b

        def l2norm(t):
            n = jnp.sqrt(jnp.sum(jnp.square(t), axis=-1, keepdims=True))
            return t / jnp.maximum(n, L2_EPS)
        b, n, _ = x.shape
        m = latents.shape[1]
        x = layer_norm(x, ln_x_w, ln_x_b)
        latents = layer_norm(latents, ln_l_w, ln_l_b)
        q = latents @ Wq
        kv_input = jnp.concatenate([x, latents], axis=1)
        kv = kv_input @ Wkv
        k, v = jnp.split(kv, 2, axis=-1)

        def to_heads(t):
            return t.reshape(t.shape[0], t.shape[1], HEADS, DIM_HEAD).transpose(0, 2, 1, 3)
        q, k, v = map(to_heads, (q, k, v))
        q = l2norm(q) * q_scale
        k = l2norm(k) * k_scale
        sim = jnp.einsum('bhid,bhjd->bhij', q, k) * SCALE
        full_mask = jnp.concatenate([mask, jnp.ones((b, m), dtype=bool)], axis=1)[:, None, None, :]
        max_neg = -jnp.finfo(sim.dtype).max
        sim = jnp.where(full_mask, sim, max_neg)
        attn = jax.nn.softmax(sim.astype(jnp.float32), axis=-1).astype(sim.dtype)
        out = jnp.einsum('bhij,bhjd->bhid', attn, v)
        out = out.transpose(0, 2, 1, 3).reshape(b, m, INNER)
        return layer_norm(out @ Wo, ln_o_w, ln_o_b)

    def _L0_attn_ref(x, W_qkv, b_qkv, W_proj, b_proj, qn_w, kn_w):
        import jax, jax.numpy as jnp
        import numpy as np
        EPS = 1e-06

        def _rmsnorm(x, w):
            dt = x.dtype
            xf = x.astype(jnp.float32)
            var = jnp.mean(xf * xf, axis=-1, keepdims=True)
            xf = xf * jax.lax.rsqrt(var + EPS)
            return xf.astype(dt) * w
        B, N, C = x.shape
        H = 16
        D = C // H
        qkv = jnp.einsum('bnc,cd->bnd', x, W_qkv) + b_qkv
        qkv = qkv.reshape(B, N, 3, H, D)
        q = qkv[:, :, 0].transpose(0, 2, 1, 3)
        k = qkv[:, :, 1].transpose(0, 2, 1, 3)
        v = qkv[:, :, 2].transpose(0, 2, 1, 3)
        q = _rmsnorm(q, qn_w)
        k = _rmsnorm(k, kn_w)
        scale = D ** (-0.5)
        attn = jnp.einsum('bhqd,bhkd->bhqk', q, k) * scale
        attn = jax.nn.softmax(attn, axis=-1)
        out = jnp.einsum('bhqk,bhkd->bhqd', attn, v)
        out = out.transpose(0, 2, 1, 3).reshape(B, N, C)
        out = jnp.einsum('bnc,cd->bnd', out, W_proj) + b_proj
        return out

    def _L0_ffn_ref(x, W_r, W_k, W_v, mu_r, mu_k):
        import jax, jax.numpy as jnp
        import numpy as np
        DIM = 512

        def _reference_tuple_inner(x, W_r, W_k, W_v, mu_r, mu_k):
            B, T, C = x.shape
            x_prev = jnp.concatenate([jnp.zeros((B, 1, C), x.dtype), x[:, :-1, :]], axis=1)
            xr = mu_r * x + (1.0 - mu_r) * x_prev
            xk = mu_k * x + (1.0 - mu_k) * x_prev
            r = jax.nn.sigmoid(jnp.einsum('btc,dc->btd', xr, W_r))
            k = jnp.einsum('btc,dc->btd', xk, W_k)
            k_act = jnp.square(jax.nn.relu(k))
            out = r * jnp.einsum('btc,dc->btd', k_act, W_v)
            new_state = x[:, -1, :]
            return (out, new_state)
        return _reference_tuple_inner(x, W_r, W_k, W_v, mu_r, mu_k)[0]

    def _L1_xattn_ref(query, key_value, wq, wk, wv, wo):
        import jax, jax.numpy as jnp
        import numpy as np
        D_MODEL = 512
        N_HEADS = 16
        HEAD_DIM = D_MODEL // N_HEADS
        B, T, _ = query.shape
        S = key_value.shape[1]
        q = (query @ wq.T).reshape(B, T, N_HEADS, HEAD_DIM)
        k = (key_value @ wk.T).reshape(B, S, N_HEADS, HEAD_DIM)
        v = (key_value @ wv.T).reshape(B, S, N_HEADS, HEAD_DIM)
        scale = HEAD_DIM ** (-0.5)
        attn = jnp.einsum('bthd,bshd->bhts', q, k) * scale
        attn = jax.nn.softmax(attn, axis=-1)
        out = jnp.einsum('bhts,bshd->bthd', attn, v).reshape(B, T, N_HEADS * HEAD_DIM)
        return out @ wo.T

    def _L1_attn_ref(x, wq, wk, wv, wproj, g_rms):
        import jax, jax.numpy as jnp
        import numpy as np
        N_HEAD = 16
        EPS = 1e-05
        ROPE_BASE = 10000.0
        B, T, C = x.shape
        H = N_HEAD
        hd = C // H
        q = (x @ wq.T).reshape(B, T, H, hd)
        k = (x @ wk.T).reshape(B, T, H, hd)
        v = (x @ wv.T).reshape(B, T, H, hd)

        def rms(t):
            var = jnp.mean(t * t, axis=-1, keepdims=True) + EPS
            return g_rms * (t * jax.lax.rsqrt(var))
        q, k = (rms(q), rms(k))
        inv_freq = 1.0 / ROPE_BASE ** (jnp.arange(0, hd, 2, dtype=jnp.float32) / hd)
        freqs = jnp.outer(jnp.arange(T, dtype=jnp.float32), inv_freq)
        cos = jnp.cos(freqs).astype(jnp.bfloat16).astype(jnp.float32)[None, :, None, :]
        sin = jnp.sin(freqs).astype(jnp.bfloat16).astype(jnp.float32)[None, :, None, :]

        def rope(u):
            d = hd // 2
            u1, u2 = (u[..., :d], u[..., d:])
            return jnp.concatenate([u1 * cos + u2 * sin, -u1 * sin + u2 * cos], axis=-1)
        q, k = (rope(q), rope(k))
        qh = q.transpose(0, 2, 1, 3)
        kh = k.transpose(0, 2, 1, 3)
        vh = v.transpose(0, 2, 1, 3)
        scale = 1.0 / jnp.sqrt(jnp.float32(hd))
        scores = jnp.einsum('bhtd,bhsd->bhts', qh, kh) * scale + 1.0
        attn = jax.nn.softmax(scores, axis=-1)
        y = jnp.einsum('bhts,bhsd->bhtd', attn, vh)
        y = y.transpose(0, 2, 1, 3).reshape(B, T, C)
        return y @ wproj.T

    def _L1_ffn_ref(hidden_states, gate_w, w1, b1, w2, b2):
        import jax, jax.numpy as jnp
        import numpy as np
        B, S, H, E, DFF = (4, 2048, 512, 8, 2048)
        b, s, h = hidden_states.shape
        x = hidden_states.reshape(-1, h)
        gate_logits = x @ gate_w.T
        gate_probs = jax.nn.softmax(gate_logits, axis=-1)
        expert_idx = jnp.argmax(gate_probs, axis=-1)
        expert_w = jnp.take_along_axis(gate_probs, expert_idx[:, None], axis=1)[:, 0]
        out = jnp.zeros_like(x)
        n_experts = w1.shape[0]
        for e in range(n_experts):
            ye = jax.nn.relu(x @ w1[e] + b1[e]) @ w2[e] + b2[e]
            sel = (expert_idx == e)[:, None]
            out = out + jnp.where(sel, ye * expert_w[:, None], 0.0)
        return out.reshape(b, s, h)
    x = x + _L0_xattn_ref(ctx_1024, _layernorm(x, axis=-1), mask_BxS2_bk0, L0_xattn_ln_x_w, L0_xattn_ln_x_b, L0_xattn_ln_l_w, L0_xattn_ln_l_b, L0_xattn_Wq, L0_xattn_Wkv, L0_xattn_q_scale, L0_xattn_k_scale, L0_xattn_Wo, L0_xattn_ln_o_w, L0_xattn_ln_o_b)
    x = x + _L0_attn_ref(_layernorm(x, axis=-1), L0_attn_W_qkv, L0_attn_b_qkv, L0_attn_W_proj, L0_attn_b_proj, L0_attn_qn_w, L0_attn_kn_w)
    x = x + _L0_ffn_ref(_layernorm(x, axis=-1), L0_ffn_W_r, L0_ffn_W_k, L0_ffn_W_v, L0_ffn_mu_r, L0_ffn_mu_k)
    x = x + _L1_xattn_ref(_layernorm(x, axis=-1), ctx_1024, L1_xattn_wq, L1_xattn_wk, L1_xattn_wv, L1_xattn_wo)
    x = x + _L1_attn_ref(_layernorm(x, axis=-1), L1_attn_wq, L1_attn_wk, L1_attn_wv, L1_attn_wproj, L1_attn_g_rms)
    x = x + _L1_ffn_ref(_layernorm(x, axis=-1), L1_ffn_gate_w, L1_ffn_w1, L1_ffn_b1, L1_ffn_w2, L1_ffn_b2)
    return x

_drawn_inputs = setup_inputs


def setup_inputs(seed=0):
    import zlib

    import numpy as np

    out = dict(_drawn_inputs(seed))
    spreads = {'L0_xattn_ln_x_w': (1.0, 0.2),
     'L0_xattn_ln_x_b': (0.0, 0.1),
     'L0_xattn_ln_l_w': (1.0, 0.2),
     'L0_xattn_ln_l_b': (0.0, 0.1),
     'L0_xattn_q_scale': (1.0, 0.2),
     'L0_xattn_k_scale': (1.0, 0.2),
     'L0_xattn_ln_o_w': (1.0, 0.2),
     'L0_xattn_ln_o_b': (0.0, 0.1),
     'L0_attn_b_qkv': (0.0, 0.1),
     'L0_attn_b_proj': (0.0, 0.1),
     'L0_attn_qn_w': (1.0, 0.6),
     'L0_attn_kn_w': (1.0, 0.6),
     'L1_attn_g_rms': (1.0, 0.6),
     'L1_ffn_b1': (0.0, 0.8),
     'L1_ffn_b2': (0.0, 0.557)}
    factors = {'L0_ffn_W_r': 2.991, 'L0_ffn_mu_r': 8.0, 'L1_attn_wq': 5.82, 'L1_attn_wk': 5.912}
    for name, (base, spread) in spreads.items():
        noise = np.random.default_rng([zlib.crc32(name.encode()), seed]).standard_normal(out[name].shape)
        drawn = base * np.exp(spread * noise) if base else spread * noise
        out[name] = jnp.asarray(drawn.astype(out[name].dtype))
    for name, factor in factors.items():
        out[name] = (out[name] * factor).astype(out[name].dtype)
    return out
```

```python
import numpy as np
import concourse.bass as bass
from concourse import mybir
from contextlib import ExitStack

f32 = mybir.dt.float32
f32r = mybir.dt.float32r
bf16 = mybir.dt.bfloat16
u8 = mybir.dt.uint8
i32 = mybir.dt.int32
ALU = mybir.AluOpType
ACT = mybir.ActivationFunctionType
AX = mybir.AxisListType

P = 128
B, N, D = 4, 128, 512
S = 2048
KT = D // P
T = B * N
CT = S // P
LN_EPS = 1e-5
NEG = -1.0e30
GROUPS = D // P


class Cross:

    def __init__(self, layer, heads, latent_keys):
        self.layer, self.H = layer, heads
        self.d = D // heads
        self.hpg = heads // GROUPS
        self.NT = CT + (1 if latent_keys else 0)
        self.keys = self.NT * P
        self.halves = [(0, 1024), (1024, self.keys)]
        self.NQ = -(-self.NT // 4)
        self.by_act, self.by_dve = ((0, 1, 2, 3), ()) if self.NQ == 4 else ((0, 2), (1, 3, 4))
        self.nA, self.nD = len(self.by_act), len(self.by_dve)
        self.splits = 4 if layer == 0 else 8

    def turned_bank(self, q):
        return 4 + q % 3 if self.NQ == 4 else 5 + q % 2

    def before(self, q):
        n = 3 if self.NQ == 4 else 2
        if q >= n:
            return 0, q - n
        return 1, max(r for r in range(self.NQ) if self.turned_bank(r) == self.turned_bank(q))

    def quad(self, q):
        return range(4 * q, min(4 * q + 4, self.NT))


HEADS, HD = 16, 32
E, F = 8, 2048
CH = F // 512
FT = F // P
TMAX = T // P + E - 1
X0 = Cross(0, 8, True)
X1 = Cross(1, 16, False)


def tile_steps(eng, nt, body):
    for s in (-2, -1, 0):
        body(s, s)
    with eng.Fori(0, 6) as j:
        for u in (1, 2):
            body(j * 2 + u, u)
    for s in range(13, nt + 1):
        body(s, s)


def head_steps(eng, hpg, body):
    for u in range(hpg):
        body(0, u, u == 0)
    with eng.Fori(1, GROUPS) as g:
        for u in range(hpg):
            body(g, u, False)


def perceiver(nc, a, out):
    top = ExitStack()
    with top:
        def sb(name, shape, dt=f32, ctx=top):
            return ctx.enter_context(nc.sbuf_tensor(name, shape, dt))

        def sem(name):
            return top.enter_context(nc.semaphore(name))

        x_dram = nc.dram_tensor("x_spill", [B, N, D], f32).ap()

        z = sb("z", [P, B, D])
        zT = sb("zT", [P, KT, B, N + 1])
        QT = sb("QT", [P, GROUPS, T])
        ident = sb("ident", [P, P])
        rmask = {4: sb("rmask4", [P, 4]), 2: sb("rmask2", [P, 2])}
        eps = sb("eps", [P, 1])
        st = sb("st", [P, B, 6])
        mv = sb("mv", [P, B, 2])
        sd = sb("sd", [P, B])
        rstd = sb("rstd", [P, B])
        ps = top.enter_context(nc.psum_tensor("ps", [P, 8, 512], f32))

        def bank(k, w=512):
            return ps[:, k, 0:w]

        cross = ExitStack()
        WKh = sb("WKh", [P, KT, D], f32r, cross)
        WKl = sb("WKl", [P, KT, D], f32r, cross)
        WVh = sb("WVh", [P, KT, D], f32r, cross)
        WVl = sb("WVl", [P, KT, D], f32r, cross)
        KTh = sb("KTh", [P, GROUPS, X0.keys], f32r, cross)
        KTl = sb("KTl", [P, GROUPS, X0.keys], f32r, cross)
        zh = sb("zh", [P, 2, KT, P], f32r, cross)
        zl = sb("zl", [P, 2, KT, P], f32r, cross)
        Qmh = sb("Qmh", [P, 2, P], f32r, cross)
        Qml = sb("Qml", [P, 2, P], f32r, cross)
        V = sb("V", [P, X0.NT * D], f32, cross)
        SM = sb("SM", [P, 2 * X0.keys], f32, cross)
        PT = sb("PT", [P, 4, 512], f32, cross)
        lnw = sb("lnw", [P, D], f32, cross)
        lnb = sb("lnb", [P, D], f32, cross)
        mask8 = sb("mask8", [P, S], u8, cross)
        mbias = sb("mbias", [P, X0.keys], bf16, cross)
        rs = sb("rs", [P, 2], f32, cross)
        rinv = sb("rinv", [P, 2], f32, cross)
        pmax = sb("pmax", [P, 8], f32, cross)
        nb = sb("nb", [P, 2], f32, cross)
        xst = sb("xst", [P, 2, 6], f32, cross)
        xmv = sb("xmv", [P, 2, 2], f32, cross)
        xsd = sb("xsd", [P, 2], f32, cross)
        xrs = sb("xrs", [P, 2], f32, cross)
        kss = sb("kss", [P, 8], f32, cross)
        knm = sb("knm", [P, 8], f32, cross)
        krn = sb("krn", [P, 8], f32, cross)
        cross.close()
        Vt = V[:, :].rearrange("p (t n) -> p t n", n=D)
        SMv = SM[:, :].rearrange("p (u n) -> p u n", u=2)
        tilebuf = SM[:, 0:8 * D].rearrange("p (t n) -> p t n", n=D)
        xin = [tilebuf[:, k, :] for k in (0, 1)]
        zt = [tilebuf[:, k, :] for k in (2, 3)]
        kn = [tilebuf[:, k, :] for k in (4, 5)]
        ksq = tilebuf[:, 6, :]
        kvw = SM[:, 0:KT * 1024].rearrange("p (k n) -> p k n", k=KT)
        kv_st = [SM[:, n * 2048:(n + 1) * 2048].rearrange("p (k n) -> p k n", k=KT) for n in (0, 1)]
        def vbuf(k):
            return V[:, k * 2048:(k + 1) * 2048]
        wq_st = vbuf(0).rearrange("p (k n) -> p k n", k=KT)
        wqT = vbuf(1).rearrange("p (k n) -> p k n", k=KT)
        x_st = vbuf(2).rearrange("p (b n) -> p b n", b=B)
        lnw2 = V[:, 6144:6656]
        lnb2 = V[:, 6656:7168]
        qsc = V[:, 7168:7232]
        ksc = V[:, 7232:7296]
        y_st = vbuf(1).rearrange("p (b n) -> p b n", b=B)
        ssb = V[:, 7296:7296 + 32].rearrange("p (b h) -> p b h", b=B)
        nrm = V[:, 7328:7328 + 32].rearrange("p (b h) -> p b h", b=B)
        mid = ExitStack()
        x = sb("x", [P, B, D], f32, mid)
        Wqkv = sb("Wqkv", [P, KT, 3 * D], f32, mid)
        Wp = sb("Wp", [P, KT, D], f32, mid)
        wst = sb("wst", [P, 3, KT, D], f32, mid)
        wffT = sb("wffT", [P, 3, KT, D], f32, mid)
        qkv = sb("qkv", [P, B, 3 * D], f32, mid)
        Qm = sb("Qm", [P, HEADS, N], f32, mid)
        KTm = sb("KTm", [P, GROUPS, T], f32, mid)
        Pm = sb("Pm", [P, HEADS * N], f32, mid)
        PTm = sb("PTm", [P, HEADS * N], f32, mid)
        bqkv = sb("bqkv", [P, 3 * D], f32, mid)
        bproj = sb("bproj", [P, D], f32, mid)
        gains = sb("gains", [P, 2, HD], f32, mid)
        rope_t = sb("rope_t", [P, 3, HD // 2], f32, mid)
        hss = sb("hss", [P, B, 2 * HEADS], f32, mid)
        hrs = sb("hrs", [P, B, 2 * HEADS], f32, mid)
        mx = sb("mx", [P, HEADS], f32, mid)
        hsum = sb("hsum", [P, HEADS], f32, mid)
        mu = sb("mu", [P, 2, KT], f32, mid)
        omu = sb("omu", [P, 2, KT], f32, mid)
        hsq = sb("hsq", [P, 2 * D], f32, mid)
        mid.close()
        moe = ExitStack()
        sb("x_keep", [P, B, D], f32, moe)
        w1r = sb("w1r", [P, CH, KT, 512], f32, moe)
        w2r = sb("w2r", [P, CH, KT, 512], f32, moe)
        zmh = sb("zmh", [P, B, D], f32r, moe)
        zml = sb("zml", [P, B, D], f32r, moe)
        Dm = sb("Dm", [P, B, P], f32r, moe)
        DT = sb("DT", [P, B, P], f32r, moe)
        xeT = sb("xeT", [P, KT, P], f32, moe)
        hT = sb("hT", [P, 2, KT, P], f32, moe)
        ysb = sb("ysb", [P, D], f32, moe)
        yh = sb("yh", [P, D], f32r, moe)
        yl = sb("yl", [P, D], f32r, moe)
        b2r = sb("b2r", [P, D], f32, moe)
        b1n = sb("b1n", [P, P], f32, moe)
        b1T = sb("b1T", [P, P], f32, moe)
        gwn = sb("gwn", [E, D], f32, moe)
        gwT = sb("gwT", [P, KT, E], f32, moe)
        upper = sb("upper", [P, P], f32, moe)
        ones = sb("ones", [P, P], f32, moe)
        slots = sb("slots", [P, P], f32, moe)
        order = sb("order", [P, E], f32, moe)
        turns = sb("turns", [P, TMAX], f32, moe)
        lg = sb("lg", [P, B, E], f32, moe)
        lm = sb("lm", [P, B], f32, moe)
        oh = sb("oh", [P, B, E], f32, moe)
        cand = sb("cand", [P, B, E], f32, moe)
        ex = sb("ex", [P, B, E], f32, moe)
        gate = sb("gate", [P, B], f32, moe)
        pos = sb("pos", [P, B], f32, moe)
        nblk = sb("nblk", [P, E], f32, moe)
        cmp8 = sb("cmp8", [P, E], f32, moe)
        last = sb("last", [P, E], f32, moe)
        first = sb("first", [P, E], f32, moe)
        cmpt = sb("cmpt", [P, TMAX, E], f32, moe)
        tabf = sb("tabf", [P, TMAX + 1], f32, moe)
        tab = sb("tab", [P, TMAX + 1], i32, moe)
        moe.close()
        ffbuf = qkv[:, :, :].rearrange("p b n -> p (b n)").rearrange("p (w k t) -> p w k t", w=3, k=KT)
        xr, xk, kact = (ffbuf[:, w] for w in range(3))
        rgate = Pm[:, :].rearrange("p (b n) -> p b n", b=B)

        s_c = sem("consts")
        class Signals(dict):

            def __init__(self, part):
                self.part = part

            def __missing__(self, name):
                self[name] = sem(f"{self.part}_{name}")
                return self[name]
        xs = {0: Signals("x0"), 1: Signals("x1")}
        xc = Signals("xc")
        tiles, heads_ = B * X0.NT, B * X0.H
        first_adds = dict(x_ld0=B * CT // 2 * 16, x_ld1=B * CT // 2 * 16, t_done=B * CT, zh_ready=tiles, zl_ready=tiles, k_done=tiles, v_done=tiles,
                          kn_ready=tiles, kt_done=tiles, kh_ready=tiles, kl_ready=tiles, v_ready=tiles, qm_ready=heads_, s_done=2 * heads_,
                          s_taken=2 * heads_, nb_ready=heads_, exp_done=heads_, pt_done=heads_ * X0.NQ, ev_a=heads_ * X0.nA, ev_d=heads_ * X0.nD,
                          av_done=heads_ * X0.NQ, o_done=heads_, ao_done=B + 1)

        def at(X, name, v):
            return xc[name], v + X.layer * first_adds[name]
        outs = sem("outs")
        ln = Signals("ln")
        ms = Signals("self")
        per = dict(qkv_pe=12, qkv_out=12, sq=4, ss=5, nm=1, qk_ready=4, qkt_pe=8, qt_out=4, kt_out=4, qm=4, s_pe=4, s_out=4, e_out=4,
                   pt_pe=16, pt_a=8, pt_d=8, av_pe=4, ao=4, aot_pe=4, aot_a=2, aot_d=2, y_pe=4, x_att=4)
        fs = Signals("ff")
        ws = Signals("selfw")
        es = Signals("moe")
        mi = {0: Signals("in0"), 1: Signals("in1")}
        spill = sem("spill")

        block = top.enter_context(nc.Block())

        @block.sync
        def _(sp):
            s = xs[0]
            sp.dma_start(x_st, a["x"].rearrange("b n d -> n b d")).then_inc(s["x_in"], 16)
            for dst, src in ((lnw2, a["L0_xattn_ln_l_w"]), (lnb2, a["L0_xattn_ln_l_b"]), (qsc, a["L0_xattn_q_scale"]),
                             (ksc, a["L0_xattn_k_scale"]), (lnw[:, :], a["L0_xattn_ln_x_w"]), (lnb[:, :], a["L0_xattn_ln_x_b"])):
                sp.dma_start(dst, src.rearrange("(o n) -> o n", o=1).partition_broadcast(P)).then_inc(s["x_in"], 16)
            sp.dma_start(wq_st, a["L0_xattn_Wq"].rearrange("(k p) n -> p k n", p=P)).then_inc(s["w_in"], 16)
            sp.dma_start(kvw, a["L0_xattn_Wkv"].rearrange("(k p) n -> p k n", p=P)).then_inc(s["w_in"], 16)

            def context(X, s):
                ctx = a["ctx_1024"].rearrange("b s d -> (b s) d")
                with sp.Fori(0, B) as b:
                    row = sp.snap(b * S)
                    sp.wait_ge(*at(X, "ao_done", b + 1))
                    sp.wait_ge(s["w_split"], X.splits)


                    def load(i, rep):
                        tile = ctx[bass.ds(sp.snap(row + i * P), P), :]
                        if rep >= 2:
                            if X.layer == 0:
                                sp.wait_ge(s["z_norm"], b * CT + i - 1)
                            else:
                                sp.wait_ge(*at(X, "t_done", b * CT + i - 1))
                        sp.dma_start(xin[rep % 2], tile).then_inc(xc[f"x_ld{rep % 2}"], 16)
                    load(0, 0)
                    load(1, 1)
                    with sp.Fori(1, CT // 2) as j:
                        load(j * 2, 2)
                        load(j * 2 + 1, 3)

            def project_in(X, s, wo):
                sp.wait_ge(*at(X, "ao_done", B + 1))
                sp.dma_start(wq_st, wo).then_inc(s["wo_in"], 16)
                if X.layer == 0:
                    sp.dma_start(lnw2, a["L0_xattn_ln_o_w"].rearrange("(o n) -> o n", o=1).partition_broadcast(P)).then_inc(s["wo_in"], 16)
                    sp.dma_start(lnb2, a["L0_xattn_ln_o_b"].rearrange("(o n) -> o n", o=1).partition_broadcast(P)).then_inc(s["wo_in"], 16)
                    sp.dma_start(x_st, a["x"].rearrange("b n d -> n b d")).then_inc(s["wo_in"], 16)
            context(X0, s)
            project_in(X0, s, a["L0_xattn_Wo"].rearrange("(k p) n -> p k n", p=P))

            def row(v):
                return v.rearrange("(o n) -> o n", o=1).partition_broadcast(P)

            def native(w):
                return w.rearrange("(t p) n -> p t n", p=P)

            m = mi[0]
            sp.wait_ge(xs[0]["x_done"], B)
            sp.dma_start(Wqkv[:, :, :], native(a["L0_attn_W_qkv"])).then_inc(m["w_in"], 16)
            sp.dma_start(Wp[:, :, :], native(a["L0_attn_W_proj"])).then_inc(m["w_in"], 16)
            sp.dma_start(bqkv[:, :], row(a["L0_attn_b_qkv"])).then_inc(m["p_in"], 16)
            sp.dma_start(bproj[:, :], row(a["L0_attn_b_proj"])).then_inc(m["p_in"], 16)
            sp.dma_start(gains[:, 0, :], row(a["L0_attn_qn_w"])).then_inc(m["p_in"], 16)
            sp.dma_start(gains[:, 1, :], row(a["L0_attn_kn_w"])).then_inc(m["p_in"], 16)
            for n, w in enumerate(("L0_ffn_W_r", "L0_ffn_W_k", "L0_ffn_W_v")):
                sp.dma_start(wst[:, n], native(a[w])).then_inc(fs["w_in"], 16)
            for n, w in enumerate(("L0_ffn_mu_r", "L0_ffn_mu_k")):
                sp.dma_start(mu[:, n, :], a[w].rearrange("(k p) -> p k", p=P), allow_slow_non_contiguous=True).then_inc(fs["w_in"], 16)
            s = xs[1]
            sp.wait_ge(fs["x_ff"], B)
            sp.dma_start(x_dram.rearrange("b n d -> n b d"), x[:, :, :]).then_inc(spill, 16)
            sp.wait_ge(spill, 16)
            sp.wait_ge(ln["z"], 3 * B)
            sp.dma_start(wq_st, native(a["L1_xattn_wq"])).then_inc(s["w_in"], 16)
            for n, w in enumerate(("L1_xattn_wk", "L1_xattn_wv")):
                sp.dma_start(kv_st[n], native(a[w])).then_inc(s["w_in"], 16)
            context(X1, s)
            sp.wait_ge(*at(X1, "ao_done", B + 1))
            sp.dma_start(wq_st, native(a["L1_xattn_wo"])).then_inc(s["wo_in"], 16)
            sp.dma_start(x_st, x_dram.rearrange("b n d -> n b d")).then_inc(s["wo_in"], 16)
            m = mi[1]
            sp.wait_ge(xs[1]["x_done"], B)
            for n, w in enumerate(("L1_attn_wq", "L1_attn_wk", "L1_attn_wv")):
                sp.dma_start(wst[:, n], native(a[w])).then_inc(ws["w_in"], 16)
            sp.dma_start(wffT[:, 0], native(a["L1_attn_wproj"])).then_inc(ws["w_in"], 16)
            sp.dma_start(gains[:, 0, :], row(a["L1_attn_g_rms"])).then_inc(m["p_in"], 16)
            sp.dma_start(gains[:, 1, :], row(a["L1_attn_g_rms"])).then_inc(m["p_in"], 16)
            sp.dma_start(rope_t[:, :, :], a["rope"]).then_inc(m["p_in"], 16)
            sp.wait_ge(es["ring_free"], 1)
            sp.dma_start(gwn[:, :], a["L1_ffn_gate_w"]).then_inc(es["g_in"], 16)
            sp.dma_start(b1n[:, :], a["L1_ffn_b1"].rearrange("e (f p) -> (e f) p", p=P)).then_inc(es["g_in"], 16)
            sp.wait_ge(es["table"], 1)
            blocks = sp.value_load(tab[0:1, TMAX:TMAX + 1], min_val=1, max_val=TMAX)
            w1 = a["L1_ffn_w1"].rearrange("e (k p) f -> e p k f", p=P)
            w2 = a["L1_ffn_w2"].rearrange("e (f p) n -> e p f n", p=P)
            with sp.Fori(0, blocks) as t:
                e = sp.value_load(tab[0:1, bass.ds(t, 1)], min_val=0, max_val=E - 1)
                for c in range(CH):
                    sp.wait_ge(es["ring_free"], t * CH + c + 1)
                    sp.dma_start(w1r[:, c], w1[e, :, :, c * 512:(c + 1) * 512]).then_inc(es[f"w1_in{c}"], 16)
                    sp.dma_start(w2r[:, c], w2[e, :, c * KT:(c + 1) * KT, :]).then_inc(es[f"w2_in{c}"], 16)
                sp.wait_ge(es["y_out"], t + 1)
                sp.dma_start(b2r[:, :], a["L1_ffn_b2"][e, :].rearrange("(o n) -> o n", o=1).partition_broadcast(P)).then_inc(es["b2_in"], 16)
            sp.wait_ge(es["x_moe"], blocks * B)
            sp.dma_start(out.rearrange("b n d -> n b d"), x[:, :, :]).then_inc(outs, 16)
            sp.wait_ge(outs, 16)

        @block.gpsimd
        def _(pool):
            pool.memset(ident[:, :], 0.0).then_inc(s_c, 1)
            pool.memset(rmask[4][:, :], 1.0).then_inc(s_c, 1)
            pool.memset(rmask[2][:, :], 1.0).then_inc(s_c, 1)
            pool.memset(eps[:, :], LN_EPS).then_inc(s_c, 1)
            pool.memset(zT[:, :, :, :], 0.0).then_inc(s_c, 1)
            pool.wait_ge(s_c, 5)
            pool.affine_select(out=ident[:, :], in_=ident[:, :], compare_op=ALU.not_equal, fill=1.0, base=0,
                               pattern=[[-1, P]], channel_multiplier=1).then_inc(s_c, 1)
            n = 6
            for hpg in (4, 2):
                w = P // hpg
                m = rmask[hpg][:, :]
                pool.affine_select(out=m, in_=m, compare_op=ALU.is_ge, fill=0.0, base=0,
                                   pattern=[[-w, hpg]], channel_multiplier=1).then_inc(s_c, 1)
                n += 1
                pool.wait_ge(s_c, n)
                pool.affine_select(out=m, in_=m, compare_op=ALU.is_ge, fill=0.0, base=w - 1,
                                   pattern=[[w, hpg]], channel_multiplier=-1).then_inc(s_c, 1)
                n += 1
            pool.wait_ge(s_c, n)

            s = xs[0]
            with pool.Fori(0, B) as b:
                with pool.Fori(0, CT // 2) as j:
                    for u in (0, 1):
                        i = b * CT + j * 2 + u
                        pool.wait_ge(s["z_norm"], i + 1)
                        pool.tensor_tensor(zt[u], zt[u], lnw[:, :], ALU.mult).then_inc(s["z_ready"], 1)
                        pool.wait_ge(s["z_ready"], i * 2 + 1)
                        pool.tensor_tensor(zt[u], zt[u], lnb[:, :], ALU.add).then_inc(s["z_ready"], 1)
            pool.wait_ge(es["ring_free"], 1)
            pool.memset(ones[:, :], 1.0).then_inc(es["c"], 1)
            pool.memset(upper[:, :], 1.0).then_inc(es["c"], 1)
            pool.iota(slots[:, :], [[1, P]], base=0, channel_multiplier=0, allow_small_or_imprecise_dtypes=True).then_inc(es["c"], 1)
            pool.iota(order[:, :], [[-1, E]], base=E, channel_multiplier=0, allow_small_or_imprecise_dtypes=True).then_inc(es["c"], 1)
            pool.iota(turns[:, :], [[1, TMAX]], base=0, channel_multiplier=0, allow_small_or_imprecise_dtypes=True).then_inc(es["c"], 1)
            pool.wait_ge(es["c"], 5)
            pool.affine_select(out=upper[:, :], in_=upper[:, :], compare_op=ALU.is_gt, fill=0.0, base=0,
                               pattern=[[1, P]], channel_multiplier=-1).then_inc(es["c"], 1)

        @block.scalar
        def _(act):
            def deviation(s, base=0):
                act.wait_ge(s["v"], base + 1)
                act.activation(sd[:, :], mv[:, :, 1], ACT.Sqrt, bias=eps[:, :]).then_inc(s["sd"], 1)

            s = xs[0]
            act.wait_ge(s_c, 10)
            act.wait_ge(s["w_in"], 32)
            act.activation(WKh[:, :, :], kvw[:, :, 0:D], ACT.Copy).then_inc(s["w_split"], 1)
            act.activation(WVh[:, :, :], kvw[:, :, D:2 * D], ACT.Copy).then_inc(s["w_split"], 1)
            deviation(s)
            deviation(s, 1)
            for b in (0, 2):
                act.wait_ge(s["zt_pe"], b + 1)
                act.activation(zT[:, :, b, 1:N + 1], bank(b).rearrange("p (k n) -> p k n", k=KT), ACT.Copy).then_inc(s["zt_ready"], 1)
            for b in range(B):
                act.wait_ge(s["q_pe"], b + 1)
                act.activation(y_st[:, b, :], bank(4 + b), ACT.Square).then_inc(s["q_sq"], 1)
            act.wait_ge(s["q_ss"], 1)
            act.activation(nrm, ssb, ACT.Sqrt).then_inc(s["q_nm"], 1)
            for b in (0, 2):
                act.wait_ge(s["qt_pe"], b + 1)
                act.activation(QT[:, :, b * N:(b + 1) * N], bank(b).rearrange("p (k n) -> p k n", k=KT), ACT.Copy).then_inc(s["qt_ready"], 1)

            def attend(X, s, scale):
                masks = a["mask_BxS2_bk0"].rearrange("b s -> (b s)").bitcast(u8)
                with act.Fori(0, B) as b:
                    act.wait_ge(*at(X, "ao_done", b + 1))
                    if X.layer == 0:
                        act.dma_start(mask8[:, :], masks[bass.ds(b * S, S)].rearrange("(o n) -> o n", o=1).partition_broadcast(P)).then_inc(s["mask_in"], 16)

                    def step(i, rep):
                        t = rep + 1
                        if 0 <= t < X.NT:
                            if t == CT:
                                if rep >= 1:
                                    act.wait_ge(*at(X, "v_done", b * X.NT + i))
                                act.activation(zh[:, t % 2], zT[:, :, b, 1:N + 1], ACT.Copy).then_inc(xc["zh_ready"], 1)
                            else:
                                act.wait_ge(*at(X, "t_done", b * CT + i + 2))
                                if rep >= 1:
                                    act.wait_ge(*at(X, "v_done", b * X.NT + i))
                                act.activation(zh[:, t % 2], bank(t % 2).rearrange("p (k n) -> p k n", k=KT), ACT.Copy).then_inc(xc["zh_ready"], 1)
                        if X.layer == 0 and 0 <= rep + 2 < CT:
                            act.wait_ge(s["st_ready"], b * CT + i + 3)
                            act.activation(xsd[:, rep % 2:rep % 2 + 1], xmv[:, rep % 2, 1:2], ACT.Sqrt, bias=eps[:, :]).then_inc(s["sd_ready"], 1)
                        if 0 <= rep < X.NT:
                            p = rep % 2
                            act.wait_ge(*at(X, "k_done", b * X.NT + i + 1))
                            if X.layer == 0:
                                act.activation(ksq, bank(2 + p), ACT.Square).then_inc(s["sq_ready"], 1)
                                act.wait_ge(s["ss_ready"], b * X.NT + i + 1)
                                act.activation(knm[:, :], kss[:, :], ACT.Sqrt).then_inc(s["nm_ready"], 1)
                            else:
                                if rep >= 2:
                                    act.wait_ge(*at(X, "kt_done", b * X.NT + i - 1))
                                act.activation(kn[p], bank(2 + p), ACT.Copy).then_inc(xc["kn_ready"], 1)
                            act.wait_ge(*at(X, "v_done", b * X.NT + i + 1))
                            act.activation(Vt[:, i, :], bank(4 + p), ACT.Copy).then_inc(xc["v_ready"], 1)
                        if 0 <= rep - 1 < X.NT:
                            p = (rep - 1) % 2
                            act.wait_ge(*at(X, "kt_done", b * X.NT + i))
                            act.activation(KTh[:, :, bass.ts(i - 1, P)], bank(6 + p).rearrange("p (k n) -> p k n", k=KT), ACT.Copy).then_inc(xc["kh_ready"], 1)
                    tile_steps(act, X.NT, step)

                    def copy(hn, q, first):
                        act.wait_ge(*at(X, "pt_done", hn * X.NQ + q + 1))
                        if not first:
                            act.wait_ge(*at(X, "av_done", hn * X.NQ if q == 0 and X.NQ == 5 else (hn - 1) * X.NQ + q + 1))
                        act.activation(PT[:, q, :], bank(X.turned_bank(q)), ACT.Copy).then_inc(xc["ev_a"], 1)

                    def head(g, u, first):
                        hn = b * X.H + g * X.hpg + u
                        if not first:
                            for q in X.by_act:
                                copy(hn - 1, q, isinstance(g, int) and g == 0 and u == 1)
                        p = u % 2
                        act.wait_ge(*at(X, "nb_ready", hn + 1))
                        act.activation(SMv[:, p, 0:X.keys], SMv[:, p, 0:X.keys], ACT.Exp, scale=scale, bias=nb[:, p:p + 1],
                                       accum_out=rs[:, p:p + 1]).then_inc(xc["exp_done"], 1)
                    head_steps(act, X.hpg, head)
                    for q in X.by_act:
                        copy(b * X.H + X.H - 1, q, False)
            attend(X0, s, 8.0)

            def project_out(s):
                for b in (0, 2):
                    act.wait_ge(s["aot_pe"], b + 1)
                    act.activation(zT[:, :, b, 1:N + 1], bank(b).rearrange("p (k n) -> p k n", k=KT), ACT.Copy).then_inc(s["aot_ready"], 1)
            project_out(s)
            deviation(s, 2)

            def layer_norm(u):
                act.wait_ge(ln["v"], u + 1)
                act.activation(sd[:, :], mv[:, :, 1], ACT.Sqrt, bias=eps[:, :]).then_inc(ln["sd"], 1)
                for b in (0, 2):
                    act.wait_ge(ln["zt_pe"], u * B + b + 1)
                    act.activation(zT[:, :, b, 1:N + 1], bank(b).rearrange("p (k n) -> p k n", k=KT), ACT.Copy).then_inc(ln["zt_a"], 1)

            def self_attention(layer):
                def own(name, v):
                    return ms[name], v + layer * per[name]
                layer_norm(3 * layer)
                if layer == 1:
                    for j in range(3 * B):
                        act.wait_ge(*own("qkv_pe", j + 1))
                        act.activation(qkv[:, j // 3, (j % 3) * D:(j % 3 + 1) * D], bank(j % 8), ACT.Copy).then_inc(ms["qkv_out"], 1)
                for b in range(B):
                    act.wait_ge(*own("qkv_out", 3 * b + 2))
                    if b:
                        act.wait_ge(*own("ss", b))
                    act.activation(hsq[:, :], qkv[:, b, 0:2 * D], ACT.Square).then_inc(ms["sq"], 1)
                act.wait_ge(*own("ss", B + 1))
                act.activation(hrs[:, :, :], hss[:, :, :], ACT.Sqrt).then_inc(ms["nm"], 1)
                for b in range(B):
                    act.wait_ge(*own("qkt_pe", 2 * b + 1))
                    act.activation(QT[:, :, b * N:(b + 1) * N], bank(2 * b).rearrange("p (k n) -> p k n", k=KT), ACT.Copy).then_inc(ms["qt_out"], 1)
                for b in range(B):
                    act.wait_ge(*own("s_out", b + 1))
                    act.activation(Pm[:, :], Pm[:, :], ACT.Exp, bias=float(layer)).then_inc(ms["e_out"], 1)
                    for q in (0, 2):
                        act.wait_ge(*own("pt_pe", 4 * b + q + 1))
                        if b:
                            act.wait_ge(*own("av_pe", b))
                        act.activation(PTm[:, q * 512:(q + 1) * 512], bank(4 + (4 * b + q) % 3), ACT.Copy).then_inc(ms["pt_a"], 1)
                for b in (0, 2):
                    act.wait_ge(*own("aot_pe", b + 1))
                    act.activation(zT[:, :, b, 1:N + 1], bank(b).rearrange("p (k n) -> p k n", k=KT), ACT.Copy).then_inc(ms["aot_a"], 1)

            self_attention(0)
            for j in range(0, 3 * KT, 2):
                act.wait_ge(fs["wt_pe"], j + 1)
                act.activation(wffT[:, j // KT, j % KT, :], bank(j % 8), ACT.Copy).then_inc(fs["wt_a"], 1)
            layer_norm(1)
            for b in range(B):
                act.wait_ge(fs["r_pe"], b + 1)
                act.activation(rgate[:, b, :], bank(b), ACT.Sigmoid).then_inc(fs["r_out"], 1)
            for n in range(KT):
                act.wait_ge(fs["k_pe"], n + 1)
                act.activation(kact[:, n, :], bank(4 + n), ACT.Relu).then_inc(fs["k_relu"], 1)
            s = xs[1]
            layer_norm(2)
            for j in range(3 * KT):
                w, k = j // KT, j % KT
                act.wait_ge(s["w_tr"], j + 1)
                act.activation((wqT, WKh, WVh)[w][:, k, :], bank((4 + j) % 8), ACT.Copy).then_inc(s["w_hi"], 1)
            for n in range(0, KT, 2):
                act.wait_ge(s["qt_pe"], n + 1)
                act.activation(QT[:, n, :], bank(n), ACT.Copy).then_inc(s["qt_ready"], 1)
            attend(X1, s, HD ** -0.5)
            project_out(s)
            for k in range(0, KT, 2):
                act.wait_ge(s["wo_tr"], k + 1)
                act.activation(wqT[:, k, :], bank(4 + k), ACT.Copy).then_inc(s["wo_a"], 1)
            for j in range(0, 4 * KT, 2):
                w, k = j // KT, j % KT
                act.wait_ge(ws["tr"], j + 1)
                act.activation(Wqkv[:, k, w * D:(w + 1) * D] if w < 3 else Wp[:, k, :], bank(j % 8), ACT.Copy).then_inc(ws["a"], 1)
            self_attention(1)
            layer_norm(4)
            act.wait_ge(ln["z"], 5 * B)
            act.activation(zmh[:, :, :], z[:, :, :], ACT.Copy).then_inc(es["zh"], 1)
            act.wait_ge(es["b_pe"], 1)
            act.activation(gwT[:, :, :], ps[:, 5, 0:KT * E].rearrange("p (k e) -> p k e", k=KT), ACT.Copy).then_inc(es["g_t"], 1)
            act.activation(b1T[:, :], ps[:, 5, P:2 * P], ACT.Copy).then_inc(es["g_t"], 1)
            act.wait_ge(es["ex_in"], 1)
            act.activation(ex[:, :, :], ex[:, :, :], ACT.Exp).then_inc(es["ex_out"], 1)
            act.wait_ge(es["table"], 1)
            blocks = act.value_load(tab[0:1, TMAX:TMAX + 1], min_val=1, max_val=TMAX)
            act.wait_ge(es["gather"], 1)
            act.activation(xeT[:, :, :], bank(0).rearrange("p (k n) -> p k n", k=KT), ACT.Copy).then_inc(es["xe"], 1)
            with act.Fori(0, blocks) as t:
                e = act.value_load(tab[0:1, bass.ds(t, 1)], min_val=0, max_val=E - 1)
                for c in range(CH):
                    act.wait_ge(es["up"], t * CH + c + 1)
                    for f in range(KT):
                        act.activation(hT[:, c % 2, f, :], ps[:, 2 + c % 2, f * P:(f + 1) * P], ACT.Relu,
                                       bias=b1T[:, bass.ds(e * FT + (c * KT + f), 1)]).then_inc(es["h"], 1)
                act.wait_ge(es["y_out"], t + 2)
                act.activation(yh[:, :], ysb[:, :], ACT.Copy).then_inc(es["yh"], 1)
                act.wait_ge(es["gather"], t + 2)
                act.activation(xeT[:, :, :], bank(0).rearrange("p (k n) -> p k n", k=KT), ACT.Copy).then_inc(es["xe"], 1)

        @block.vector
        def _(dve):
            def normalise(s, src, dst, base):
                for b in range(B):
                    dve.bn_stats(st[:, b, :], src(b))
                dve.drain()
                for b in range(B):
                    i = dve.bn_aggr(mv[:, b, :], st[:, b, :])
                i.then_inc(s["v"], 1)
                dve.wait_ge(s["sd"], base + 1)
                dve.reciprocal(rstd[:, :], sd[:, :])
                dve.drain()
                for b in range(B):
                    i = dve.tensor_scalar(dst(b), src(b), mv[:, b, 0:1], rstd[:, b:b + 1], ALU.subtract, ALU.mult)
                    yield b, i

            s = xs[0]
            dve.wait_ge(s_c, 10)
            dve.wait_ge(s["x_in"], 7 * 16)
            for _b in normalise(s, lambda b: x_st[:, b, :], lambda b: z[:, b, :], 0):
                pass
            dve.drain()
            for _b in normalise(s, lambda b: z[:, b, :], lambda b: z[:, b, :], 1):
                pass
            dve.drain()
            for b in range(B):
                dve.tensor_tensor(z[:, b, :], z[:, b, :], lnw2, ALU.mult)
                dve.drain()
                dve.tensor_tensor(z[:, b, :], z[:, b, :], lnb2, ALU.add).then_inc(s["ln_z"], 1)
            dve.wait_ge(s["w_in"], 32)
            dve.wait_ge(s["w_split"], 2)
            dve.tensor_tensor(WKl[:, :, :], kvw[:, :, 0:D], WKh[:, :, :].bitcast(f32), ALU.subtract).then_inc(s["w_split"], 1)
            dve.tensor_tensor(WVl[:, :, :], kvw[:, :, D:2 * D], WVh[:, :, :].bitcast(f32), ALU.subtract).then_inc(s["w_split"], 1)
            for b in (1, 3):
                dve.wait_ge(s["zt_pe"], b + 1)
                dve.tensor_copy(zT[:, :, b, 1:N + 1], bank(b).rearrange("p (k n) -> p k n", k=KT)).then_inc(s["zt_ready"], 1)
            dve.tensor_tensor(qsc, qsc, ksc, ALU.mult)
            dve.wait_ge(s["q_sq"], B)
            for b in range(B):
                i = dve.tensor_reduce(ssb[:, b, :], y_st[:, b, :].rearrange("p (h d) -> p h d", h=X0.H), AX.X, ALU.add)
            i.then_inc(s["q_ss"], 1)
            dve.wait_ge(s["q_nm"], 1)
            dve.tensor_scalar(nrm, nrm, 1e-12, None, ALU.max)
            dve.drain()
            dve.reciprocal(ssb, nrm)
            dve.drain()
            for b in range(B):
                q3 = z[:, b, :].rearrange("p (h d) -> p h d", h=X0.H)
                dve.tensor_tensor(q3, bank(4 + b).rearrange("p (h d) -> p h d", h=X0.H),
                                  ssb[:, b, :].unsqueeze(2).to_broadcast([P, X0.H, X0.d]), ALU.mult)
                dve.drain()
                dve.tensor_tensor(q3, q3, qsc.unsqueeze(1).to_broadcast([P, X0.H, X0.d]), ALU.mult).then_inc(s["q_ready"], 1)
            for b in (1, 3):
                dve.wait_ge(s["qt_pe"], b + 1)
                dve.tensor_copy(QT[:, :, b * N:(b + 1) * N], bank(b).rearrange("p (k n) -> p k n", k=KT)).then_inc(s["qt_ready"], 1)

            def attend(X, s, scale):
                dve.memset(pmax[:, 4:5], 0.0).then_inc(xc["ao_done"], 1)
                with dve.Fori(0, B) as b:
                    if X.layer == 0:
                        dve.wait_ge(s["mask_in"], b * 16 + 16)
                        dve.tensor_scalar(mbias[:, 0:S], mask8[:, :], -1.0, -NEG, ALU.add, ALU.mult)
                        dve.memset(mbias[:, S:X.keys], 0.0)

                    def step(i, rep):
                        if X.layer == 0 and 0 <= rep + 2 < CT:
                            p = rep % 2
                            dve.wait_ge(*at(X, f"x_ld{p}", b * (CT // 2 * 16) + (i - p + 2) * 8 + 16))
                            dve.bn_stats(xst[:, p, :], xin[p])
                            dve.drain()
                            dve.bn_aggr(xmv[:, p, :], xst[:, p, :]).then_inc(s["st_ready"], 1)
                        t = rep + 1
                        if 0 <= t < X.NT:
                            dve.wait_ge(*at(X, "zh_ready", b * X.NT + i + 2))
                            src = zT[:, :, b, 1:N + 1] if t == CT else bank(t % 2).rearrange("p (k n) -> p k n", k=KT)
                            dve.tensor_tensor(zl[:, t % 2], src, zh[:, t % 2].bitcast(f32), ALU.subtract).then_inc(xc["zl_ready"], 1)
                        if X.layer == 0 and 0 <= rep + 2 < CT:
                            dve.wait_ge(s["sd_ready"], b * CT + i + 3)
                            dve.reciprocal(xrs[:, p:p + 1], xsd[:, p:p + 1])
                            dve.drain()
                            if rep >= 0:
                                dve.wait_ge(*at(X, "t_done", b * CT + i + 1))
                            dve.tensor_scalar(zt[p], xin[p], xmv[:, p, 0:1], xrs[:, p:p + 1], ALU.subtract, ALU.mult).then_inc(s["z_norm"], 1)
                        if X.layer == 0 and 0 <= rep < X.NT:
                            p = rep % 2
                            dve.wait_ge(s["sq_ready"], b * X.NT + i + 1)
                            dve.tensor_reduce(kss[:, :], ksq.rearrange("p (h d) -> p h d", h=X.H), AX.X, ALU.add).then_inc(s["ss_ready"], 1)
                            dve.wait_ge(s["nm_ready"], b * X.NT + i + 1)
                            dve.tensor_scalar(knm[:, :], knm[:, :], 1e-12, None, ALU.max)
                            dve.drain()
                            dve.reciprocal(krn[:, :], knm[:, :])
                            dve.drain()
                            if rep >= 2:
                                dve.wait_ge(*at(X, "kt_done", b * X.NT + i - 1))
                            dve.tensor_tensor(kn[p].rearrange("p (h d) -> p h d", h=X.H), bank(2 + p).rearrange("p (h d) -> p h d", h=X.H),
                                              krn[:, :].unsqueeze(2).to_broadcast([P, X.H, X.d]), ALU.mult).then_inc(xc["kn_ready"], 1)
                        if 0 <= rep - 1 < X.NT:
                            p = (rep - 1) % 2
                            dve.wait_ge(*at(X, "kh_ready", b * X.NT + i))
                            dve.tensor_tensor(KTl[:, :, bass.ts(i - 1, P)], bank(6 + p).rearrange("p (k n) -> p k n", k=KT),
                                              KTh[:, :, bass.ts(i - 1, P)].bitcast(f32), ALU.subtract).then_inc(xc["kl_ready"], 1)
                    tile_steps(dve, X.NT, step)

                    def copy(hn, q, first):
                        w = P * len(X.quad(q))
                        dve.wait_ge(*at(X, "pt_done", hn * X.NQ + q + 1))
                        if q == 4:
                            dve.wait_ge(*at(X, "av_done", hn * X.NQ + 1))
                        elif not first:
                            dve.wait_ge(*at(X, "av_done", (hn - 1) * X.NQ + q + 1))
                        dve.tensor_copy(PT[:, q % 4, 0:w], bank(X.turned_bank(q), w)).then_inc(xc["ev_d"], 1)

                    def output(g, u):
                        h = g * X.hpg + u
                        p = u % 2
                        dve.wait_ge(*at(X, "av_done", (b * X.H + h + 1) * X.NQ))
                        dve.reciprocal(rinv[:, p:p + 1], rs[:, p:p + 1])
                        dve.drain()
                        dve.tensor_scalar(z[:, b, bass.ds(h * X.d, X.d)], ps[:, 7, u * P + u * X.d:u * P + (u + 1) * X.d],
                                          rinv[:, p:p + 1], None, ALU.mult).then_inc(xc["o_done"], 1)

                    def head(g, u, first):
                        hn = b * X.H + g * X.hpg + u
                        p = u % 2
                        second = isinstance(g, int) and g == 0 and u == 1
                        if not (first or second):
                            dve.wait_ge(*at(X, "s_done", hn * 2 - 2))
                        q = QT[:, g, bass.ts(b, N)]
                        row = rmask[X.hpg][:, u:u + 1]
                        dve.tensor_scalar(Qmh[:, p, :], q, row, None, ALU.mult)
                        dve.drain()
                        dve.scalar_tensor_tensor(Qml[:, p, :], q, row, Qmh[:, p, :].bitcast(f32), ALU.mult, ALU.subtract).then_inc(xc["qm_ready"], 1)
                        for k, (lo, hi) in enumerate(X.halves):
                            if k == 1 and X.NQ == 5 and not first:
                                copy(hn - 1, 1, second)
                            dve.wait_ge(*at(X, "s_done", hn * 2 + k + 1))
                            if k == 0 and not (first or second):
                                dve.wait_ge(*at(X, "pt_done", (hn - 1) * X.NQ))
                            src = ps[:, lo // 512:5, :].rearrange("p k n -> p (k n)")[:, 0:hi - lo]
                            m = pmax[:, 2 * p + k:2 * p + k + 1]
                            dve.memset(pmax[:, 4 + 2 * p + k:5 + 2 * p + k], 0.0)
                            if X.layer == 0:
                                dve.tensor_tensor_reduce(out=SMv[:, p, lo:hi], in0=src, in1=mbias[:, lo:hi], scale=1.0, scalar=-3.0e38,
                                                         op0=ALU.add, op1=ALU.max, accum_out=m).then_inc(xc["s_taken"], 1)
                            else:
                                dve.tensor_scalar(SMv[:, p, lo:hi], src, 1.0, None, ALU.mult, ALU.max, accum_out=m).then_inc(xc["s_taken"], 1)
                            if k == 0 and not (first or second):
                                output(*((g, u - 2) if u >= 2 else (g - 1, X.hpg + u - 2)))
                        dve.drain()
                        dve.tensor_scalar(nb[:, p:p + 1], pmax[:, 2 * p:2 * p + 1], pmax[:, 2 * p + 1:2 * p + 2], -scale, ALU.max, ALU.mult).then_inc(xc["nb_ready"], 1)
                        if not first:
                            for q in X.by_dve:
                                if q > 1 or X.NQ == 4:
                                    copy(hn - 1, q, second)
                    head_steps(dve, X.hpg, head)
                    output(GROUPS - 1, X.hpg - 2)
                    for q in X.by_dve:
                        copy(b * X.H + X.H - 1, q, False)
                    output(GROUPS - 1, X.hpg - 1)
                    dve.memset(pmax[:, 4:5], 0.0).then_inc(xc["ao_done"], 1)
            attend(X0, s, 8.0)

            def project_out(s):
                for b in (1, 3):
                    dve.wait_ge(s["aot_pe"], b + 1)
                    dve.tensor_copy(zT[:, :, b, 1:N + 1], bank(b).rearrange("p (k n) -> p k n", k=KT)).then_inc(s["aot_ready"], 1)
            project_out(s)
            dve.wait_ge(s["wo_in"], 64)
            dve.wait_ge(s["y_pe"], B)
            for b, i in normalise(s, lambda b: bank(4 + b), lambda b: y_st[:, b, :], 2):
                pass
            dve.drain()
            for b in range(B):
                dve.tensor_tensor(y_st[:, b, :], y_st[:, b, :], lnw2, ALU.mult)
                dve.drain()
                dve.tensor_tensor(y_st[:, b, :], y_st[:, b, :], lnb2, ALU.add)
                dve.drain()
                dve.tensor_tensor(x[:, b, :], y_st[:, b, :], x_st[:, b, :], ALU.add).then_inc(s["x_done"], 1)

            def layer_norm(u):
                dve.drain()
                for b, i in normalise(ln, lambda b: x[:, b, :], lambda b: z[:, b, :], u):
                    i.then_inc(ln["z"], 1)
                for b in (1, 3):
                    dve.wait_ge(ln["zt_pe"], u * B + b + 1)
                    dve.tensor_copy(zT[:, :, b, 1:N + 1], bank(b).rearrange("p (k n) -> p k n", k=KT)).then_inc(ln["zt_d"], 1)

            def heads(t, h):
                return t.rearrange("p (h d) -> p h d", h=h)

            def self_attention(layer, eps_, shift):
                def own(name, v):
                    return ms[name], v + layer * per[name]
                scale = HD ** -0.5
                layer_norm(3 * layer)
                dve.wait_ge(mi[layer]["p_in"], (4 if layer == 0 else 3) * 16)
                if layer == 0:
                    for j in range(3 * B):
                        dve.wait_ge(*own("qkv_pe", j + 1))
                        cols = slice((j % 3) * D, (j % 3 + 1) * D)
                        dve.tensor_tensor(qkv[:, j // 3, cols], bank(j % 8), bqkv[:, cols], ALU.add).then_inc(ms["qkv_out"], 1)
                for b in range(B):
                    dve.wait_ge(*own("sq", b + 1))
                    dve.tensor_reduce(hss[:, b, :], heads(hsq[:, :], 2 * HEADS), AX.X, ALU.add).then_inc(ms["ss"], 1)
                dve.drain()
                dve.tensor_scalar(hss[:, :, :], hss[:, :, :], 1.0 / HD, eps_, ALU.mult, ALU.add).then_inc(ms["ss"], 1)
                dve.wait_ge(*own("nm", 1))
                dve.reciprocal(hss[:, :, :], hrs[:, :, :])
                dve.drain()
                for b in range(B):
                    t = qkv[:, b, 0:2 * D]
                    dve.tensor_tensor(heads(t, 2 * HEADS), heads(t, 2 * HEADS), hss[:, b, :].unsqueeze(2).to_broadcast([P, 2 * HEADS, HD]), ALU.mult)
                    dve.drain()
                    t4 = t.rearrange("p (w h d) -> p w h d", w=2, h=HEADS)
                    i = dve.tensor_tensor(t4, t4, gains[:, :, :].unsqueeze(2).to_broadcast([P, 2, HEADS, HD]), ALU.mult)
                    if layer == 1:
                        dve.drain()
                        u = t.rearrange("p (h a d) -> p h a d", h=2 * HEADS, a=2)
                        v = hsq[:, :].rearrange("p (h a d) -> p h a d", h=2 * HEADS, a=2)
                        for half in (0, 1):
                            dve.tensor_tensor(v[:, :, half, :], u[:, :, 1 - half, :], rope_t[:, 1 + half, :].unsqueeze(1).to_broadcast([P, 2 * HEADS, HD // 2]), ALU.mult)
                        dve.drain()
                        w = t.rearrange("p (h d) -> p h d", d=HD // 2)
                        dve.tensor_tensor(w, w, rope_t[:, 0, :].unsqueeze(1).to_broadcast([P, 4 * HEADS, HD // 2]), ALU.mult)
                        dve.drain()
                        i = dve.tensor_tensor(t, t, hsq[:, :], ALU.add)
                    i.then_inc(ms["qk_ready"], 1)
                for b in range(B):
                    dve.wait_ge(*own("qkt_pe", 2 * b + 2))
                    dve.tensor_copy(KTm[:, :, b * N:(b + 1) * N], bank(2 * b + 1).rearrange("p (k n) -> p k n", k=KT)).then_inc(ms["kt_out"], 1)
                Qm4 = Qm[:, :, :].rearrange("p (g j) n -> p g j n", g=GROUPS)
                S3 = ps[:, 0:4, :].rearrange("p k n -> p (k n)").rearrange("p (h n) -> p h n", h=HEADS)
                P3 = Pm[:, :].rearrange("p (h n) -> p h n", h=HEADS)

                def masked_queries(b):
                    dve.wait_ge(*own("qt_out", b + 1))
                    if b:
                        dve.wait_ge(*own("s_pe", b))
                    for j in range(HEADS // GROUPS):
                        i = dve.tensor_scalar(Qm4[:, :, j, :], QT[:, :, b * N:(b + 1) * N], rmask[4][:, j:j + 1], None, ALU.mult)
                    i.then_inc(ms["qm"], 1)
                masked_queries(0)
                for b in range(B):
                    dve.wait_ge(*own("s_pe", b + 1))
                    dve.tensor_reduce(mx[:, :], S3, AX.X, ALU.max)
                    dve.drain()
                    dve.tensor_scalar(mx[:, :], mx[:, :], scale, shift, ALU.mult, ALU.add)
                    dve.drain()
                    if b:
                        dve.wait_ge(*own("pt_pe", 4 * b))
                    dve.scalar_tensor_tensor(P3, S3, scale, mx[:, :].unsqueeze(2).to_broadcast([P, HEADS, N]), ALU.mult, ALU.subtract).then_inc(ms["s_out"], 1)
                    if b + 1 < B:
                        masked_queries(b + 1)
                    dve.wait_ge(*own("e_out", b + 1))
                    dve.tensor_reduce(hsum[:, :], P3, AX.X, ALU.add)
                    for q in (1, 3):
                        dve.wait_ge(*own("pt_pe", 4 * b + q + 1))
                        if b:
                            dve.wait_ge(*own("av_pe", b))
                        dve.tensor_copy(PTm[:, q * 512:(q + 1) * 512], bank(4 + (4 * b + q) % 3)).then_inc(ms["pt_d"], 1)
                    dve.drain()
                    dve.reciprocal(hsum[:, :], hsum[:, :])
                    dve.drain()
                    dve.wait_ge(*own("av_pe", b + 1))
                    dve.tensor_tensor(heads(z[:, b, :], HEADS), heads(bank(7), HEADS), hsum[:, :].unsqueeze(2).to_broadcast([P, HEADS, HD]), ALU.mult).then_inc(ms["ao"], 1)
                for b in (1, 3):
                    dve.wait_ge(*own("aot_pe", b + 1))
                    dve.tensor_copy(zT[:, :, b, 1:N + 1], bank(b).rearrange("p (k n) -> p k n", k=KT)).then_inc(ms["aot_d"], 1)
                for b in range(B):
                    dve.wait_ge(*own("y_pe", b + 1))
                    i = dve.tensor_tensor(x[:, b, :], x[:, b, :], bank(4 + b), ALU.add)
                    if layer == 0:
                        dve.drain()
                        i = dve.tensor_tensor(x[:, b, :], x[:, b, :], bproj[:, :], ALU.add)
                    i.then_inc(ms["x_att"], 1)

            self_attention(0, 1e-6, 0.0)
            for j in range(1, 3 * KT, 2):
                dve.wait_ge(fs["wt_pe"], j + 1)
                dve.tensor_copy(wffT[:, j // KT, j % KT, :], bank(j % 8)).then_inc(fs["wt_d"], 1)
            layer_norm(1)
            dve.wait_ge(fs["w_in"], 80)
            dve.tensor_scalar(omu[:, :, :], mu[:, :, :], -1.0, 1.0, ALU.mult, ALU.add)
            dve.wait_ge(ln["zt_a"], 4)
            dve.drain()
            for n, dst in enumerate((xr, xk)):
                for k in range(KT):
                    to = dst[:, k, :].rearrange("p (b n) -> p b n", b=B)
                    dve.tensor_scalar(to, zT[:, k, :, 0:N], omu[:, n, k:k + 1], None, ALU.mult)
                dve.drain()
                for k in range(KT):
                    to = dst[:, k, :].rearrange("p (b n) -> p b n", b=B)
                    i = dve.scalar_tensor_tensor(to, zT[:, k, :, 1:N + 1], mu[:, n, k:k + 1], to, ALU.mult, ALU.add)
                i.then_inc(fs["mix"], 1)
            for n in range(KT):
                dve.wait_ge(fs["k_relu"], n + 1)
                dve.tensor_tensor(kact[:, n, :], kact[:, n, :], kact[:, n, :], ALU.mult).then_inc(fs["k_out"], 1)
            dve.wait_ge(fs["r_out"], B)
            for b in range(B):
                dve.wait_ge(fs["v_pe"], b + 1)
                dve.tensor_tensor(rgate[:, b, :], rgate[:, b, :], bank(b), ALU.mult)
                dve.drain()
                dve.tensor_tensor(x[:, b, :], x[:, b, :], rgate[:, b, :], ALU.add).then_inc(fs["x_ff"], 1)
            s = xs[1]
            layer_norm(2)
            for j in range(KT, 3 * KT):
                w, k = j // KT, j % KT
                hi, lo = ((WKh, WKl), (WVh, WVl))[w - 1]
                dve.wait_ge(s["w_hi"], j + 1)
                dve.tensor_tensor(lo[:, k, :], bank((4 + j) % 8), hi[:, k, :].bitcast(f32), ALU.subtract).then_inc(s["w_split"], 1)
            for n in range(1, KT, 2):
                dve.wait_ge(s["qt_pe"], n + 1)
                dve.tensor_copy(QT[:, n, :], bank(n)).then_inc(s["qt_ready"], 1)
            attend(X1, s, HD ** -0.5)
            project_out(s)
            for k in range(1, KT, 2):
                dve.wait_ge(s["wo_tr"], k + 1)
                dve.tensor_copy(wqT[:, k, :], bank(4 + k)).then_inc(s["wo_d"], 1)
            for b in range(B):
                dve.wait_ge(s["y_pe"], b + 1)
                dve.tensor_tensor(x[:, b, :], bank(b), x_st[:, b, :], ALU.add).then_inc(s["x_done"], 1)
            for j in range(1, 4 * KT, 2):
                w, k = j // KT, j % KT
                dve.wait_ge(ws["tr"], j + 1)
                dve.tensor_copy(Wqkv[:, k, w * D:(w + 1) * D] if w < 3 else Wp[:, k, :], bank(j % 8)).then_inc(ws["d"], 1)
            self_attention(1, 1e-5, 1.0)
            layer_norm(4)
            dve.wait_ge(es["zh"], 1)
            dve.tensor_tensor(zml[:, :, :], z[:, :, :], zmh[:, :, :].bitcast(f32), ALU.subtract).then_inc(es["zl"], 1)
            dve.wait_ge(es["c"], 6)
            dve.wait_ge(es["logits"], 1)
            dve.tensor_copy(lg[:, :, :], ps[:, 4, 0:B * E].rearrange("p (b e) -> p b e", b=B))
            dve.drain()

            def wide(v):
                return v.unsqueeze(2).to_broadcast([P, B, E])

            def over(v):
                return v.unsqueeze(1).to_broadcast([P, B, E])
            dve.tensor_reduce(lm[:, :], lg[:, :, :], AX.X, ALU.max)
            dve.drain()
            dve.tensor_tensor(ex[:, :, :], lg[:, :, :], wide(lm[:, :]), ALU.subtract).then_inc(es["ex_in"], 1)
            dve.tensor_tensor(cand[:, :, :], lg[:, :, :], wide(lm[:, :]), ALU.is_equal)
            dve.drain()
            dve.tensor_tensor(cand[:, :, :], cand[:, :, :], over(order[:, :]), ALU.mult)
            dve.drain()
            dve.tensor_reduce(lm[:, :], cand[:, :, :], AX.X, ALU.max)
            dve.drain()
            dve.tensor_tensor(oh[:, :, :], cand[:, :, :], wide(lm[:, :]), ALU.is_equal).then_inc(es["oh"], 1)
            dve.wait_ge(es["ex_out"], 1)
            dve.tensor_reduce(gate[:, :], ex[:, :, :], AX.X, ALU.add)
            dve.drain()
            dve.reciprocal(gate[:, :], gate[:, :]).then_inc(es["y_out"], 1)
            dve.wait_ge(es["ranks"], 1)
            count = ps[:, 6, B * E:(B + 1) * E]
            dve.tensor_scalar(nblk[:, :], count, 0.0, None, ALU.is_gt)
            for j in range(1, T // P):
                dve.drain()
                dve.tensor_scalar(cmp8[:, :], count, float(j * P), None, ALU.is_gt)
                dve.drain()
                dve.tensor_tensor(nblk[:, :], nblk[:, :], cmp8[:, :], ALU.add)
            dve.drain()
            dve.tensor_copy(last[:, :], nblk[:, :])
            for j in range(1, E):
                dve.drain()
                dve.tensor_tensor(last[:, j:j + 1], last[:, j:j + 1], last[:, j - 1:j], ALU.add)
            dve.drain()
            dve.tensor_tensor(first[:, :], last[:, :], nblk[:, :], ALU.subtract)
            dve.tensor_tensor(cmpt[:, :, :], last[:, :].unsqueeze(1).to_broadcast([P, TMAX, E]), turns[:, :].unsqueeze(2).to_broadcast([P, TMAX, E]), ALU.is_le)
            dve.drain()
            dve.tensor_reduce(tabf[:, 0:TMAX], cmpt[:, :, :], AX.X, ALU.add)
            dve.tensor_scalar(first[:, :], first[:, :], float(P), None, ALU.mult)
            dve.tensor_copy(tabf[:, TMAX:TMAX + 1], last[:, E - 1:E])
            dve.drain()
            dve.tensor_scalar(tabf[:, 0:TMAX], tabf[:, 0:TMAX], float(E - 1), None, ALU.min)
            dve.drain()
            dve.tensor_copy(tab[:, :], tabf[:, :]).then_inc(es["table"], 1)
            dve.tensor_tensor(cand[:, :, :], ps[:, 6, 0:B * E].rearrange("p (b e) -> p b e", b=B), over(first[:, :]), ALU.add)
            dve.drain()
            dve.tensor_tensor(cand[:, :, :], cand[:, :, :], oh[:, :, :], ALU.mult)
            dve.drain()
            dve.tensor_reduce(pos[:, :], cand[:, :, :], AX.X, ALU.add)
            dve.drain()
            dve.wait_ge(es["table"], 1)
            blocks = dve.value_load(tab[0:1, TMAX:TMAX + 1], min_val=1, max_val=TMAX)

            def dispatch():
                for b in range(B):
                    i = dve.tensor_scalar(Dm[:, b, :], slots[:, :], pos[:, b:b + 1], None, ALU.is_equal)
                i.then_inc(es["dm"], 1)
                dve.drain()
                dve.tensor_scalar(pos[:, :], pos[:, :], -float(P), None, ALU.add)
                dve.drain()
            dispatch()
            with dve.Fori(0, blocks) as t:
                dve.wait_ge(es["dt_pe"], t + 1)
                dve.tensor_copy(DT[:, :, :], bank(1).rearrange("p (b n) -> p b n", b=B)).then_inc(es["dt"], 1)
                dispatch()
                dve.wait_ge(es["ring_free"], t * CH + 2 * CH)
                dve.wait_ge(es["b2_in"], t * 16 + 16)
                dve.tensor_tensor(ysb[:, :], bank(4), b2r[:, :], ALU.add).then_inc(es["y_out"], 1)
                dve.wait_ge(es["yh"], t + 1)
                dve.tensor_tensor(yl[:, :], ysb[:, :], yh[:, :].bitcast(f32), ALU.subtract).then_inc(es["yl"], 1)
                for b in range(B):
                    dve.wait_ge(es["mixed"], t * B + b + 1)
                    dve.scalar_tensor_tensor(x[:, b, :], bank(5 + b % 3), gate[:, b:b + 1], x[:, b, :], ALU.mult, ALU.add).then_inc(es["x_moe"], 1)

        @block.tensor
        def _(pe):
            def transpose4(dst, src):
                for k in range(KT):
                    i = pe.transpose(dst[:, k * P:(k + 1) * P], src[:, k * P:(k + 1) * P], ident[:, :])
                return i

            def product(dst, lhs, rhs):
                for k in range(KT):
                    i = pe.matmul(dst, lhs(k), rhs(k), start=(k == 0), stop=(k == KT - 1))
                return i

            s = xs[0]
            pe.wait_ge(s_c, 10)
            for b in range(B):
                pe.wait_ge(s["ln_z"], b + 1)
                transpose4(bank(b), z[:, b, :]).then_inc(s["zt_pe"], 1)
            pe.wait_ge(s["w_in"], 32)
            pe.wait_ge(s["zt_ready"], B)
            for b in range(B):
                product(bank(4 + b), lambda k: zT[:, k, b, 1:N + 1], lambda k: wq_st[:, k, :]).then_inc(s["q_pe"], 1)
            for b in range(B):
                pe.wait_ge(s["q_ready"], b + 1)
                transpose4(bank(b), z[:, b, :]).then_inc(s["qt_pe"], 1)

            def attend(X, s):
                pe.wait_ge(s["w_split"], X.splits)
                pe.wait_ge(s["qt_ready"], B)
                with pe.Fori(0, B) as b:
                    pe.wait_ge(*at(X, "ao_done", b + 1))

                    def step(i, rep):
                        t = rep + 1
                        if 0 <= t < CT:
                            if X.layer == 0:
                                pe.wait_ge(s["z_ready"], (b * CT + i + 2) * 2)
                                src = zt[t % 2]
                            else:
                                pe.wait_ge(*at(X, f"x_ld{t % 2}", b * (CT // 2 * 16) + (i + 1 - t % 2) * 8 + 16))
                                src = xin[t % 2]
                            if t >= 2:
                                pe.wait_ge(*at(X, "zl_ready", b * X.NT + i))
                            transpose4(bank(t % 2), src).then_inc(xc["t_done"], 1)
                        if 0 <= rep < X.NT:
                            p = rep % 2
                            n = b * X.NT + i
                            pe.wait_ge(*at(X, "zl_ready", n + 1))
                            if rep >= 2:
                                pe.wait_ge(*at(X, "kn_ready", n - 1))
                            for k in range(KT):
                                pe.matmul(bank(2 + p), zh[:, p, k, :], WKh[:, k, :], start=(k == 0), stop=False)
                                pe.matmul(bank(2 + p), zh[:, p, k, :], WKl[:, k, :], start=False, stop=False)
                                m = pe.matmul(bank(2 + p), zl[:, p, k, :], WKh[:, k, :], start=False, stop=(k == KT - 1))
                            m.then_inc(xc["k_done"], 1)
                            if rep >= 2:
                                pe.wait_ge(*at(X, "v_ready", n - 1))
                            for k in range(KT):
                                pe.matmul(bank(4 + p), zh[:, p, k, :], WVh[:, k, :], start=(k == 0), stop=False)
                                pe.matmul(bank(4 + p), zh[:, p, k, :], WVl[:, k, :], start=False, stop=False)
                                m = pe.matmul(bank(4 + p), zl[:, p, k, :], WVh[:, k, :], start=False, stop=(k == KT - 1))
                            m.then_inc(xc["v_done"], 1)
                        if 0 <= rep - 1 < X.NT:
                            p = (rep - 1) % 2
                            pe.wait_ge(*at(X, "kn_ready", b * X.NT + i))
                            if rep - 1 >= 2:
                                pe.wait_ge(*at(X, "kl_ready", b * X.NT + i - 2))
                            transpose4(bank(6 + p), kn[p]).then_inc(xc["kt_done"], 1)
                    tile_steps(pe, X.NT, step)
                    pe.wait_ge(*at(X, "kl_ready", b * X.NT + X.NT))
                    pe.wait_ge(*at(X, "v_ready", b * X.NT + X.NT))

                    def copied(hn, q):
                        if q in X.by_act:
                            pe.wait_ge(*at(X, "ev_a", hn * X.nA + X.by_act.index(q) + 1))
                        else:
                            pe.wait_ge(*at(X, "ev_d", hn * X.nD + X.by_dve.index(q) + 1))

                    def turn(h, u, q, first):
                        hn = b * X.H + h
                        if q == 0:
                            pe.wait_ge(*at(X, "exp_done", hn + 1))
                        back, r = X.before(q)
                        if not (first and back):
                            copied(hn - back, r)
                        for n, kt in enumerate(X.quad(q)):
                            i = pe.transpose(ps[:, X.turned_bank(q), n * P:(n + 1) * P], SMv[:, u % 2, kt * P:(kt + 1) * P], ident[:, :])
                        i.then_inc(xc["pt_done"], 1)

                    def add(g, u, q, first):
                        hn = b * X.H + g * X.hpg + u
                        if q == 0 and not first:
                            pe.wait_ge(*at(X, "o_done", hn))
                        copied(hn, q)
                        for n, kt in enumerate(X.quad(q)):
                            i = pe.matmul(bank(7)[:, u * P:(u + 1) * P], PT[:, q % 4, n * P:(n + 1) * P], Vt[:, kt, bass.ds(g * P, P)],
                                          start=(kt == 0), stop=(kt == X.NT - 1))
                        i.then_inc(xc["av_done"], 1)

                    def score(g, u, c, first):
                        hn = b * X.H + g * X.hpg + u
                        p = u % 2
                        k = c // 2 if c < 4 else 1
                        if c == 0:
                            pe.wait_ge(*at(X, "qm_ready", hn + 1))
                        if c in (0, 2) and not first:
                            pe.wait_ge(*at(X, "s_taken", hn * 2 - 1 + k))
                        lo = c * 512
                        w = min(512, X.keys - lo)
                        o = bank(c, w)
                        pe.matmul(o, Qmh[:, p, :], KTh[:, g, lo:lo + w], start=True, stop=False)
                        pe.matmul(o, Qmh[:, p, :], KTl[:, g, lo:lo + w], start=False, stop=False)
                        i = pe.matmul(o, Qml[:, p, :], KTh[:, g, lo:lo + w], start=False, stop=True)
                        if c == 1 or lo + w == X.keys:
                            i.then_inc(xc["s_done"], 1)

                    plan = ("S0 S1 T0 S2 T1 S3 T2 A0 T3 A1 A2 A3" if X.NQ == 4 else "S0 S1 T0 S2 T1 S3 S4 T2 A0 T3 A1 T4 A2 A3 A4").split()

                    def head(g, u, first):
                        gg, uu = (g, u - 1) if u else (g - 1, X.hpg - 1)
                        for what, q in plan:
                            q = int(q)
                            if what == "S":
                                score(g, u, q, first)
                            elif first:
                                continue
                            elif what == "T":
                                turn(gg * X.hpg + uu, uu, q, isinstance(g, int) and g == 0 and u == 1)
                            else:
                                add(gg, uu, q, isinstance(g, int) and g == 0 and u == 1)
                    head_steps(pe, X.hpg, head)
                    for what, q in plan:
                        if what == "T":
                            turn(X.H - 1, X.hpg - 1, int(q), False)
                        elif what == "A":
                            add(GROUPS - 1, X.hpg - 1, int(q), False)
            attend(X0, s)

            def project_out(s, wo):
                for b in range(B):
                    pe.wait_ge(*at(X0, "ao_done", B + 1))
                    transpose4(bank(b), z[:, b, :]).then_inc(s["aot_pe"], 1)
                pe.wait_ge(s["aot_ready"], B)
                for b in range(B):
                    product(bank(4 + b), lambda k: zT[:, k, b, 1:N + 1], lambda k: wo[:, k, :]).then_inc(s["y_pe"], 1)
            pe.wait_ge(s["wo_in"], 64)
            project_out(s, wq_st)

            def layer_norm(u):
                for b in range(B):
                    pe.wait_ge(ln["z"], u * B + b + 1)
                    transpose4(bank(b), z[:, b, :]).then_inc(ln["zt_pe"], 1)
                pe.wait_ge(ln["zt_a"], u * 2 + 2)
                pe.wait_ge(ln["zt_d"], u * 2 + 2)

            def tokens(b):
                return lambda k: zT[:, k, b, 1:N + 1]

            def self_attention(layer):
                def own(name, v):
                    return ms[name], v + layer * per[name]
                layer_norm(3 * layer)
                for j in range(3 * B):
                    if j >= 8:
                        pe.wait_ge(*own("qkv_out", j - 7))
                    cols = slice((j % 3) * D, (j % 3 + 1) * D)
                    product(bank(j % 8), tokens(j // 3), lambda k: Wqkv[:, k, cols]).then_inc(ms["qkv_pe"], 1)
                pe.wait_ge(*own("qkv_out", 3 * B))
                for b in range(B):
                    pe.wait_ge(*own("qk_ready", b + 1))
                    transpose4(bank(2 * b), qkv[:, b, 0:D]).then_inc(ms["qkt_pe"], 1)
                    transpose4(bank(2 * b + 1), qkv[:, b, D:2 * D]).then_inc(ms["qkt_pe"], 1)
                pe.wait_ge(*own("qt_out", B))
                pe.wait_ge(*own("kt_out", B))

                def scores(b):
                    pe.wait_ge(*own("qm", b + 1))
                    if b:
                        pe.wait_ge(*own("s_out", b))
                    for h in range(HEADS):
                        i = pe.matmul(ps[:, h // 4, (h % 4) * N:(h % 4 + 1) * N], Qm[:, h, :], KTm[:, h // 4, b * N:(b + 1) * N], start=True, stop=True)
                    i.then_inc(ms["s_pe"], 1)

                def copied(n):
                    if n % 2 == 0:
                        pe.wait_ge(*own("pt_a", n // 2 + 1))
                    else:
                        pe.wait_ge(*own("pt_d", n // 2 + 1))
                scores(0)
                for b in range(B):
                    if b + 1 < B:
                        scores(b + 1)
                    pe.wait_ge(*own("e_out", b + 1))
                    for q in range(4):
                        n = 4 * b + q
                        if n >= 3:
                            copied(n - 3)
                        for j in range(4):
                            h = 4 * q + j
                            i = pe.transpose(ps[:, 4 + n % 3, j * N:(j + 1) * N], Pm[:, h * N:(h + 1) * N], ident[:, :])
                        i.then_inc(ms["pt_pe"], 1)
                    if b:
                        pe.wait_ge(*own("ao", b))
                    for q in range(4):
                        copied(4 * b + q)
                        for j in range(4):
                            h = 4 * q + j
                            i = pe.matmul(ps[:, 7, h * HD:(h + 1) * HD], PTm[:, h * N:(h + 1) * N], qkv[:, b, 2 * D + h * HD:2 * D + (h + 1) * HD], start=True, stop=True)
                    i.then_inc(ms["av_pe"], 1)
                for b in range(B):
                    pe.wait_ge(*own("ao", B))
                    transpose4(bank(b), z[:, b, :]).then_inc(ms["aot_pe"], 1)
                pe.wait_ge(*own("aot_a", 2))
                pe.wait_ge(*own("aot_d", 2))
                for b in range(B):
                    product(bank(4 + b), tokens(b), lambda k: Wp[:, k, :]).then_inc(ms["y_pe"], 1)

            pe.wait_ge(mi[0]["w_in"], 32)
            self_attention(0)
            pe.wait_ge(fs["w_in"], 80)
            pe.wait_ge(ms["x_att"], B)
            for j in range(3 * KT):
                w, k = j // KT, j % KT
                if j >= 8:
                    pe.wait_ge(fs["wt_a" if j % 2 == 0 else "wt_d"], (j - 8) // 2 + 1)
                for t in range(KT):
                    i = pe.transpose(ps[:, j % 8, t * P:(t + 1) * P], wst[:, w, t, k * P:(k + 1) * P], ident[:, :])
                i.then_inc(fs["wt_pe"], 1)
            pe.wait_ge(fs["wt_a"], 6)
            pe.wait_ge(fs["wt_d"], 6)
            layer_norm(1)
            pe.wait_ge(fs["mix"], 1)
            for b in range(B):
                product(bank(b), lambda k: xr[:, k, b * N:(b + 1) * N], lambda k: wffT[:, 0, k, :]).then_inc(fs["r_pe"], 1)
            pe.wait_ge(fs["mix"], 2)
            for n in range(KT):
                product(bank(4 + n), lambda k: wffT[:, 1, k, n * P:(n + 1) * P], lambda k: xk[:, k, :]).then_inc(fs["k_pe"], 1)
            pe.wait_ge(fs["r_out"], B)
            pe.wait_ge(fs["k_out"], KT)
            for b in range(B):
                product(bank(b), lambda k: kact[:, k, b * N:(b + 1) * N], lambda k: wffT[:, 2, k, :]).then_inc(fs["v_pe"], 1)

            def turn_weight(dst, w, k):
                for t in range(KT):
                    i = pe.transpose(dst[:, t * P:(t + 1) * P], w[:, t, k * P:(k + 1) * P], ident[:, :])
                return i
            s = xs[1]
            layer_norm(2)
            pe.wait_ge(s["w_in"], 48)
            for j in range(3 * KT):
                w, k = j // KT, j % KT
                if j >= 8:
                    pe.wait_ge(s["w_hi"], j - 7)
                turn_weight(bank((4 + j) % 8), (wq_st, kv_st[0], kv_st[1])[w], k).then_inc(s["w_tr"], 1)
            pe.wait_ge(s["w_hi"], KT)
            pe.wait_ge(s["w_split"], 4)
            for n in range(KT):
                product(bank(n), lambda k: wqT[:, k, n * P:(n + 1) * P], lambda k: zT[:, k, :, 1:N + 1]).then_inc(s["qt_pe"], 1)
            attend(X1, s)
            for b in range(B):
                pe.wait_ge(*at(X1, "ao_done", B + 1))
                transpose4(bank(b), z[:, b, :]).then_inc(s["aot_pe"], 1)
            pe.wait_ge(s["wo_in"], 32)
            for k in range(KT):
                turn_weight(bank(4 + k), wq_st, k).then_inc(s["wo_tr"], 1)
            pe.wait_ge(s["aot_ready"], B)
            pe.wait_ge(s["wo_a"], 2)
            pe.wait_ge(s["wo_d"], 2)
            for b in range(B):
                product(bank(b), tokens(b), lambda k: wqT[:, k, :]).then_inc(s["y_pe"], 1)
            pe.wait_ge(ws["w_in"], 64)
            for j in range(4 * KT):
                w, k = j // KT, j % KT
                if j >= 8:
                    pe.wait_ge(ws["a" if j % 2 == 0 else "d"], (j - 8) // 2 + 1)
                turn_weight(bank(j % 8), wst[:, w] if w < 3 else wffT[:, 0], k).then_inc(ws["tr"], 1)
            pe.wait_ge(ws["a"], 8)
            pe.wait_ge(ws["d"], 8)
            self_attention(1)
            layer_norm(4)
            pe.wait_ge(es["zh"], 1)
            for c in range(CH):
                i = pe.transpose(ps[:, 7, 0:P], ident[:, :], ident[:, :])
                i.then_inc(es["ring_free"], 1)
            pe.wait_ge(es["g_in"], 32)
            for k in range(KT):
                pe.transpose(ps[:, 5, k * E:(k + 1) * E], gwn[:, k * P:(k + 1) * P], ident[0:E, 0:E])
            pe.transpose(ps[:, 5, P:2 * P], b1n[:, :], ident[:, :]).then_inc(es["b_pe"], 1)
            pe.wait_ge(es["g_t"], 2)
            for b in range(B):
                i = product(ps[:, 4, b * E:(b + 1) * E], tokens(b), lambda k: gwT[:, k, :])
            i.then_inc(es["logits"], 1)
            pe.wait_ge(es["c"], 6)
            pe.wait_ge(es["oh"], 1)
            for b in range(B + 1):
                o = ps[:, 6, b * E:(b + 1) * E]
                for j in range(b):
                    i = pe.matmul(o, ones[:, :], oh[:, j, :], start=(j == 0), stop=(j == b - 1 and b == B))
                if b < B:
                    i = pe.matmul(o, upper[:, :], oh[:, b, :], start=(b == 0), stop=True)
            i.then_inc(es["ranks"], 1)
            pe.wait_ge(es["table"], 1)
            blocks = pe.value_load(tab[0:1, TMAX:TMAX + 1], min_val=1, max_val=TMAX)
            pe.wait_ge(es["zl"], 1)

            def gather():
                for k in range(KT):
                    o = ps[:, 0, k * P:(k + 1) * P]
                    for b in range(B):
                        pe.matmul(o, zmh[:, b, k * P:(k + 1) * P], Dm[:, b, :], start=(b == 0), stop=False)
                        i = pe.matmul(o, zml[:, b, k * P:(k + 1) * P], Dm[:, b, :], start=False, stop=(b == B - 1))
                i.then_inc(es["gather"], 1)
            pe.wait_ge(es["dm"], 1)
            gather()
            with pe.Fori(0, blocks) as t:
                def up(c):
                    pe.wait_ge(es[f"w1_in{c}"], t * 16 + 16)
                    for f in range(KT):
                        i = product(ps[:, 2 + c % 2, f * P:(f + 1) * P], lambda k: w1r[:, c, k, f * P:(f + 1) * P], lambda k: xeT[:, k, :])
                    i.then_inc(es["up"], 1)

                def down(c):
                    pe.wait_ge(es[f"w2_in{c}"], t * 16 + 16)
                    pe.wait_ge(es["h"], t * FT + (c + 1) * KT)
                    for f in range(KT):
                        i = pe.matmul(bank(4), hT[:, c % 2, f, :], w2r[:, c, f, :], start=(c == 0 and f == 0), stop=(c == CH - 1 and f == KT - 1))
                    i.then_inc(es["ring_free"], 1)
                pe.wait_ge(es["xe"], t + 1)
                up(0)
                for b in range(B):
                    i = pe.transpose(ps[:, 1, b * P:(b + 1) * P], Dm[:, b, :].bitcast(f32), ident[:, :])
                i.then_inc(es["dt_pe"], 1)
                for c in range(1, CH):
                    up(c)
                    down(c - 1)
                down(CH - 1)
                pe.wait_ge(es["dm"], t + 2)
                gather()
                pe.wait_ge(es["dt"], t + 1)
                pe.wait_ge(es["yl"], t + 1)
                for b in range(B):
                    if b == 3:
                        pe.wait_ge(es["x_moe"], t * B + 1)
                    pe.matmul(bank(5 + b % 3), DT[:, b, :], yh[:, :], start=True, stop=False)
                    pe.matmul(bank(5 + b % 3), DT[:, b, :], yl[:, :], start=False, stop=True).then_inc(es["mixed"], 1)


def kernel(**inputs):
    import numpy as _np
    import concourse.bacc as _bacc
    from concourse import mybir as _mybir
    from concourse.bass_utils import run_bass_kernel_spmd as _run

    nc = _bacc.Bacc("TRN2", target_bir_lowering=False, num_devices=1)
    arrays, args = {}, {}
    for name, value in inputs.items():
        v = _np.ascontiguousarray(value)
        if v.dtype == _np.bool_:
            v = v.view(_np.int32)
        arrays[f"in_{name}"] = v
        args[name] = nc.dram_tensor(f"in_{name}", v.shape, _mybir.dt.from_np(v.dtype), kind="ExternalInput").ap()
    angles = _np.outer(_np.arange(N, dtype=_np.float32), (1.0 / 10000.0 ** (_np.arange(0, HD, 2, dtype=_np.float32) / HD)).astype(_np.float32))
    table = _np.stack([_np.cos(angles), _np.sin(angles), -_np.sin(angles)], axis=1).astype(_np.float32)
    bits = table.view(_np.uint32)
    table = ((bits + 0x7FFF + ((bits >> 16) & 1)) & _np.uint32(0xFFFF0000)).view(_np.float32)
    arrays["rope_table"] = table
    args["rope"] = nc.dram_tensor("rope_table", table.shape, _mybir.dt.float32, kind="ExternalInput").ap()
    res = nc.dram_tensor("out_x", (B, N, D), _mybir.dt.float32, kind="ExternalOutput").ap()
    perceiver(nc, args, res)
    r = _run(nc, [arrays], core_ids=[0])
    return r.results[0]["out_x"]
```

```python
import numpy as np
import concourse.bass as bass
from concourse import mybir
from contextlib import ExitStack

f32 = mybir.dt.float32
f32r = mybir.dt.float32r
bf16 = mybir.dt.bfloat16
u8 = mybir.dt.uint8
i32 = mybir.dt.int32
ALU = mybir.AluOpType
ACT = mybir.ActivationFunctionType
AX = mybir.AxisListType

P = 128
B, N, D = 4, 128, 512
S = 2048
KT = D // P
T = B * N
CT = S // P
LN_EPS = 1e-5
NEG = -1.0e30
GROUPS = D // P


class Cross:

    def __init__(self, layer, heads, latent_keys):
        self.layer, self.H = layer, heads
        self.d = D // heads
        self.hpg = heads // GROUPS
        self.NT = CT + (1 if latent_keys else 0)
        self.keys = self.NT * P
        self.halves = [(0, 1024), (1024, self.keys)]
        self.NQ = -(-self.NT // 4)
        self.by_act, self.by_dve = ((0, 1, 2, 3), ()) if self.NQ == 4 else ((0, 2), (1, 3, 4))
        self.nA, self.nD = len(self.by_act), len(self.by_dve)
        self.splits = 4 if layer == 0 else 8

    def turned_bank(self, q):
        return 4 + q % 3 if self.NQ == 4 else 5 + q % 2

    def before(self, q):
        n = 3 if self.NQ == 4 else 2
        if q >= n:
            return 0, q - n
        return 1, max(r for r in range(self.NQ) if self.turned_bank(r) == self.turned_bank(q))

    def quad(self, q):
        return range(4 * q, min(4 * q + 4, self.NT))


HEADS, HD = 16, 32
E, F = 8, 2048
CH = F // 512
FT = F // P
TMAX = T // P + E - 1
X0 = Cross(0, 8, True)
X1 = Cross(1, 16, False)


def tile_steps(eng, nt, body):
    for s in (-2, -1, 0):
        body(s, s)
    with eng.Fori(0, 6) as j:
        for u in (1, 2):
            body(j * 2 + u, u)
    for s in range(13, nt + 1):
        body(s, s)


def head_steps(eng, hpg, body):
    for u in range(hpg):
        body(0, u, u == 0)
    with eng.Fori(1, GROUPS) as g:
        for u in range(hpg):
            body(g, u, False)


def perceiver(nc, a, out):
    top = ExitStack()
    with top:
        def sb(name, shape, dt=f32, ctx=top):
            return ctx.enter_context(nc.sbuf_tensor(name, shape, dt))

        def sem(name):
            return top.enter_context(nc.semaphore(name))

        x_dram = nc.dram_tensor("x_spill", [B, N, D], f32).ap()

        z = sb("z", [P, B, D])
        zT = sb("zT", [P, KT, B, N + 1])
        QT = sb("QT", [P, GROUPS, T])
        ident = sb("ident", [P, P])
        rmask = {4: sb("rmask4", [P, 4]), 2: sb("rmask2", [P, 2])}
        eps = sb("eps", [P, 1])
        st = sb("st", [P, B, 6])
        mv = sb("mv", [P, B, 2])
        sd = sb("sd", [P, B])
        rstd = sb("rstd", [P, B])
        y_rstd = sb("y_rstd", [P, B])
        ps = top.enter_context(nc.psum_tensor("ps", [P, 8, 512], f32))

        def bank(k, w=512):
            return ps[:, k, 0:w]

        cross = ExitStack()
        WKh = sb("WKh", [P, KT, D], f32r, cross)
        WKl = sb("WKl", [P, KT, D], f32r, cross)
        WVh = sb("WVh", [P, KT, D], f32r, cross)
        WVl = sb("WVl", [P, KT, D], f32r, cross)
        KTh = sb("KTh", [P, GROUPS, X0.keys], f32r, cross)
        KTl = sb("KTl", [P, GROUPS, X0.keys], f32r, cross)
        zhl = sb("zhl", [P, 2, 2, KT, P], f32r, cross)
        zh, zl = zhl[:, 0], zhl[:, 1]
        Qmh = sb("Qmh", [P, 2, P], f32r, cross)
        Qml = sb("Qml", [P, 2, P], f32r, cross)
        V = sb("V", [P, X0.NT * D], f32, cross)
        SM = sb("SM", [P, 2 * X0.keys], f32, cross)
        PT = sb("PT", [P, 4, 512], f32, cross)
        lnw = sb("lnw", [P, D], f32, cross)
        lnb = sb("lnb", [P, D], f32, cross)
        mask8 = sb("mask8", [P, S], u8, cross)
        mbias = sb("mbias", [P, X0.keys], bf16, cross)
        rs = sb("rs", [P, 2], f32, cross)
        rinv = sb("rinv", [P, 2], f32, cross)
        pmax = sb("pmax", [P, 8], f32, cross)
        nb = sb("nb", [P, 2], f32, cross)
        xst = sb("xst", [P, 2, 6], f32, cross)
        xmv = sb("xmv", [P, 2, 2], f32, cross)
        xsd = sb("xsd", [P, 2], f32, cross)
        xrs = sb("xrs", [P, 2], f32, cross)
        kss = sb("kss", [P, 8], f32, cross)
        knm = sb("knm", [P, 8], f32, cross)
        krn = sb("krn", [P, 8], f32, cross)
        cross.close()
        Vt = V[:, :].rearrange("p (t n) -> p t n", n=D)
        SMv = SM[:, :].rearrange("p (u n) -> p u n", u=2)
        tilebuf = SM[:, 0:8 * D].rearrange("p (t n) -> p t n", n=D)
        xin = [tilebuf[:, k, :] for k in (0, 1)]
        zt = [tilebuf[:, k, :] for k in (2, 3)]
        kn = [tilebuf[:, k, :] for k in (4, 5)]
        ksq = tilebuf[:, 6, :]
        kvw = SM[:, 0:KT * 1024].rearrange("p (k n) -> p k n", k=KT)
        def vbuf(k):
            return V[:, k * 2048:(k + 1) * 2048]
        wq_st = vbuf(0).rearrange("p (k n) -> p k n", k=KT)
        wqT = vbuf(1).rearrange("p (k n) -> p k n", k=KT)
        x_st = vbuf(2).rearrange("p (b n) -> p b n", b=B)
        lnw2 = V[:, 6144:6656]
        lnb2 = V[:, 6656:7168]
        qsc = V[:, 7168:7232]
        ksc = V[:, 7232:7296]
        y_st = vbuf(1).rearrange("p (b n) -> p b n", b=B)
        ssb = V[:, 7296:7296 + 32].rearrange("p (b h) -> p b h", b=B)
        nrm = V[:, 7328:7328 + 32].rearrange("p (b h) -> p b h", b=B)
        mid = ExitStack()
        x = sb("x", [P, B, D], f32, mid)
        Wqkv = sb("Wqkv", [P, KT, 3 * D], f32, mid)
        Wp = sb("Wp", [P, KT, D], f32, mid)
        wst = sb("wst", [P, 3, KT, D], f32, mid)
        wffT = sb("wffT", [P, 3, KT, D], f32, mid)
        qkv = sb("qkv", [P, B, 3 * D], f32, mid)
        Qm = sb("Qm", [P, 2, HEADS, N], f32, mid)
        KTm = sb("KTm", [P, GROUPS, T], f32, mid)
        Pm = sb("Pm", [P, HEADS * N], f32, mid)
        PTm = sb("PTm", [P, HEADS * N], f32, mid)
        bqkv = sb("bqkv", [P, 3 * D], f32, mid)
        bproj = sb("bproj", [P, D], f32, mid)
        gains = sb("gains", [P, 2, HD], f32, mid)
        rope_t = sb("rope_t", [P, 3, HD // 2], f32, mid)
        hss = sb("hss", [P, B, 2 * HEADS], f32, mid)
        hrs = sb("hrs", [P, B, 2 * HEADS], f32, mid)
        mx = sb("mx", [P, HEADS], f32, mid)
        hsum = sb("hsum", [P, 2, HEADS], f32, mid)
        mu = sb("mu", [P, 2, KT], f32, mid)
        omu = sb("omu", [P, 2, KT], f32, mid)
        hsq = sb("hsq", [P, 2 * D], f32, mid)
        hrot = sb("hrot", [P, 2 * D], f32, mid)
        rope_g = sb("rope_g", [P, 2, 2, HD // 2], f32, mid)
        mid.close()
        wo_st = x[:, :, :]
        before = 4 * KT * D + 2 * GROUPS * X0.keys - (B * D + 10 * KT * D)
        assert 0 <= before <= B * 3 * D - B * D
        x_res = qkv[:, :, :].rearrange("p b n -> p (b n)")[:, before:before + B * D].rearrange("p (b n) -> p b n", b=B)
        WqkvT = wst[:, :, :, :].rearrange("p w k n -> p (w k n)").rearrange("p (k n) -> p k n", k=KT)
        qkv_st = Wqkv[:, :, :].rearrange("p k n -> p (k n)").rearrange("p (w k n) -> p w k n", w=3, k=KT)
        moe = ExitStack()
        sb("x_keep", [P, B, D], f32, moe)
        w1r = sb("w1r", [P, CH, KT, 512], f32, moe)
        w2r = sb("w2r", [P, CH, KT, 512], f32, moe)
        zmh = sb("zmh", [P, B, D], f32r, moe)
        zml = sb("zml", [P, B, D], f32r, moe)
        Dm = sb("Dm", [P, B, P], f32r, moe)
        DT = sb("DT", [P, B, P], f32r, moe)
        xeT = sb("xeT", [P, KT, P], f32, moe)
        hT = sb("hT", [P, 2, KT, P], f32, moe)
        ysb = sb("ysb", [P, D], f32, moe)
        yh = sb("yh", [P, D], f32r, moe)
        yl = sb("yl", [P, D], f32r, moe)
        b2r = sb("b2r", [P, D], f32, moe)
        b1n = sb("b1n", [P, P], f32, moe)
        b1T = sb("b1T", [P, P], f32, moe)
        gwn = sb("gwn", [E, D], f32, moe)
        gwT = sb("gwT", [P, KT, E], f32, moe)
        upper = sb("upper", [P, P], f32, moe)
        ones = sb("ones", [P, P], f32, moe)
        slots = sb("slots", [P, P], f32, moe)
        order = sb("order", [P, E], f32, moe)
        turns = sb("turns", [P, TMAX], f32, moe)
        lg = sb("lg", [P, B, E], f32, moe)
        lm = sb("lm", [P, B], f32, moe)
        oh = sb("oh", [P, B, E], f32, moe)
        cand = sb("cand", [P, B, E], f32, moe)
        ex = sb("ex", [P, B, E], f32, moe)
        gate = sb("gate", [P, B], f32, moe)
        pos = sb("pos", [P, B], f32, moe)
        nblk = sb("nblk", [P, E], f32, moe)
        cmp8 = sb("cmp8", [P, E], f32, moe)
        last = sb("last", [P, E], f32, moe)
        first = sb("first", [P, E], f32, moe)
        cmpt = sb("cmpt", [P, TMAX, E], f32, moe)
        tabf = sb("tabf", [P, TMAX + 1], f32, moe)
        tab = sb("tab", [P, TMAX + 1], i32, moe)
        moe.close()
        ffbuf = qkv[:, :, :].rearrange("p b n -> p (b n)").rearrange("p (w k t) -> p w k t", w=3, k=KT)
        xr, xk, kact = (ffbuf[:, w] for w in range(3))
        rgate = Pm[:, :].rearrange("p (b n) -> p b n", b=B)

        s_c = sem("consts")
        class Signals(dict):

            def __init__(self, part):
                self.part = part

            def __missing__(self, name):
                self[name] = sem(f"{self.part}_{name}")
                return self[name]
        xs = {0: Signals("x0"), 1: Signals("x1")}
        xc = Signals("xc")
        tiles, heads_ = B * X0.NT, B * X0.H
        first_adds = dict(x_ld0=B * CT // 2 * 16, x_ld1=B * CT // 2 * 16, t_done=B * CT, zh_ready=tiles, zl_ready=tiles, k_done=tiles, v_done=tiles,
                          kn_ready=tiles, kt_done=tiles, kh_ready=tiles, kl_ready=tiles, v_ready=tiles, qm_ready=heads_, s_done=2 * heads_,
                          s_taken=2 * heads_, nb_ready=heads_, exp_done=heads_, pt_done=heads_ * X0.NQ, ev_a=heads_ * X0.nA, ev_d=heads_ * X0.nD,
                          av_done=heads_ * X0.NQ, o_done=heads_, ao_done=B + 1)

        def at(X, name, v):
            return xc[name], v + X.layer * first_adds[name]
        outs = sem("outs")
        ln = Signals("ln")
        ms = Signals("self")
        per = dict(qkv_pe=12, qkv_out=12, sq=4, ss=4, nm=4, qk_ready=4, qkt_pe=8, qt_out=4, kt_out=4, qm=4, s_pe=4, s_out=4, e_out=4,
                   pt_pe=16, pt_out=16, av_pe=4, ao=4, aot_pe=4, aot_a=2, aot_d=2, y_pe=4, x_att=4)
        fs = Signals("ff")
        ws = Signals("selfw")
        es = Signals("moe")
        mi = {0: Signals("in0"), 1: Signals("in1")}
        spill = sem("spill")

        block = top.enter_context(nc.Block())

        @block.sync
        def _(sp):
            s = xs[0]
            sp.dma_start(x_st, a["x"].rearrange("b n d -> n b d")).then_inc(s["x_in"], 16)
            for dst, src in ((lnw2, a["L0_xattn_ln_l_w"]), (lnb2, a["L0_xattn_ln_l_b"]), (qsc, a["L0_xattn_q_scale"]),
                             (ksc, a["L0_xattn_k_scale"]), (lnw[:, :], a["L0_xattn_ln_x_w"]), (lnb[:, :], a["L0_xattn_ln_x_b"])):
                sp.dma_start(dst, src.rearrange("(o n) -> o n", o=1).partition_broadcast(P)).then_inc(s["x_in"], 16)
            sp.dma_start(wq_st, a["L0_xattn_Wq"].rearrange("(k p) n -> p k n", p=P)).then_inc(s["w_in"], 16)
            sp.dma_start(kvw, a["L0_xattn_Wkv"].rearrange("(k p) n -> p k n", p=P)).then_inc(s["w_in"], 16)

            def context(X, s):
                ctx = a["ctx_1024"].rearrange("b s d -> (b s) d")
                with sp.Fori(0, B) as b:
                    row = sp.snap(b * S)
                    sp.wait_ge(*at(X, "ao_done", b + 1))
                    if X.layer == 0:
                        sp.wait_ge(s["w_split"], X.splits)

                    def load(i, rep):
                        tile = ctx[bass.ds(sp.snap(row + i * P), P), :]
                        if rep >= 2:
                            if X.layer == 0:
                                sp.wait_ge(s["z_norm"], b * CT + i - 1)
                            else:
                                sp.wait_ge(*at(X, "t_done", b * CT + i - 1))
                        sp.dma_start(xin[rep % 2], tile).then_inc(xc[f"x_ld{rep % 2}"], 16)
                    load(0, 0)
                    load(1, 1)
                    with sp.Fori(1, CT // 2) as j:
                        load(j * 2, 2)
                        load(j * 2 + 1, 3)

            def row(v):
                return v.rearrange("(o n) -> o n", o=1).partition_broadcast(P)

            def native(w):
                return w.rearrange("(t p) n -> p t n", p=P)

            m = mi[0]
            context(X0, s)
            sp.wait_ge(*at(X0, "v_done", B * X0.NT))
            sp.dma_start(wo_st, a["L0_xattn_Wo"].rearrange("(k p) n -> p k n", p=P)).then_inc(s["wo_in"], 16)
            sp.dma_start(x_res, a["x"].rearrange("b n d -> n b d")).then_inc(s["wo_in"], 16)
            sp.wait_ge(s["z_ready"], B * CT * 2)
            sp.dma_start(lnw[:, :], row(a["L0_xattn_ln_o_w"])).then_inc(s["wo_in"], 16)
            sp.dma_start(lnb[:, :], row(a["L0_xattn_ln_o_b"])).then_inc(s["wo_in"], 16)
            sp.dma_start(Wqkv[:, :, :], native(a["L0_attn_W_qkv"])).then_inc(m["w_in"], 16)
            sp.wait_ge(*at(X0, "ao_done", B + 1))
            sp.dma_start(bqkv[:, :], row(a["L0_attn_b_qkv"])).then_inc(m["p_in"], 16)
            sp.dma_start(bproj[:, :], row(a["L0_attn_b_proj"])).then_inc(m["p_in"], 16)
            sp.dma_start(gains[:, 0, :], row(a["L0_attn_qn_w"])).then_inc(m["p_in"], 16)
            sp.dma_start(gains[:, 1, :], row(a["L0_attn_kn_w"])).then_inc(m["p_in"], 16)
            sp.dma_start(Wp[:, :, :], native(a["L0_attn_W_proj"])).then_inc(m["wp_in"], 16)
            for n, w in enumerate(("L0_ffn_W_r", "L0_ffn_W_k", "L0_ffn_W_v")):
                sp.dma_start(wst[:, n], native(a[w])).then_inc(fs["w_in"], 16)
            for n, w in enumerate(("L0_ffn_mu_r", "L0_ffn_mu_k")):
                sp.dma_start(mu[:, n, :], a[w].rearrange("(k p) -> p k", p=P), allow_slow_non_contiguous=True).then_inc(fs["w_in"], 16)
            s = xs[1]
            sp.wait_ge(fs["wt"], 3 * KT)
            for n, w in enumerate(("L1_xattn_wq", "L1_xattn_wk", "L1_xattn_wv")):
                sp.dma_start(wst[:, n], native(a[w])).then_inc(s["w_in"], 16)
            sp.wait_ge(fs["x_ff"], B)
            sp.dma_start(x_dram.rearrange("b n d -> n b d"), x[:, :, :]).then_inc(spill, 16)
            sp.wait_ge(spill, 16)
            context(X1, s)
            sp.wait_ge(*at(X1, "v_done", B * X1.NT))
            sp.dma_start(wo_st, native(a["L1_xattn_wo"])).then_inc(s["wo_in"], 16)
            sp.dma_start(x_res, x_dram.rearrange("b n d -> n b d")).then_inc(s["wo_in"], 16)
            for n, w in enumerate(("L1_attn_wq", "L1_attn_wk", "L1_attn_wv")):
                sp.dma_start(qkv_st[:, n], native(a[w])).then_inc(ws["w_in"], 16)
            m = mi[1]
            sp.wait_ge(*at(X1, "ao_done", B + 1))
            sp.dma_start(wffT[:, 0], native(a["L1_attn_wproj"])).then_inc(ws["wp_in"], 16)
            sp.dma_start(gains[:, 0, :], row(a["L1_attn_g_rms"])).then_inc(m["p_in"], 16)
            sp.dma_start(gains[:, 1, :], row(a["L1_attn_g_rms"])).then_inc(m["p_in"], 16)
            sp.dma_start(rope_t[:, :, :], a["rope"]).then_inc(m["p_in"], 16)
            sp.wait_ge(es["ring_free"], 1)
            sp.dma_start(gwn[:, :], a["L1_ffn_gate_w"]).then_inc(es["g_in"], 16)
            sp.dma_start(b1n[:, :], a["L1_ffn_b1"].rearrange("e (f p) -> (e f) p", p=P)).then_inc(es["g_in"], 16)
            sp.wait_ge(es["table"], 1)
            blocks = sp.value_load(tab[0:1, TMAX:TMAX + 1], min_val=1, max_val=TMAX)
            w1 = a["L1_ffn_w1"].rearrange("e (k p) f -> e p k f", p=P)
            w2 = a["L1_ffn_w2"].rearrange("e (f p) n -> e p f n", p=P)
            with sp.Fori(0, blocks) as t:
                e = sp.value_load(tab[0:1, bass.ds(t, 1)], min_val=0, max_val=E - 1)
                for c in range(CH):
                    sp.wait_ge(es["ring_free"], t * CH + c + 1)
                    sp.dma_start(w1r[:, c], w1[e, :, :, c * 512:(c + 1) * 512]).then_inc(es[f"w1_in{c}"], 16)
                    sp.dma_start(w2r[:, c], w2[e, :, c * KT:(c + 1) * KT, :]).then_inc(es[f"w2_in{c}"], 16)
                sp.wait_ge(es["y_out"], t + 1)
                sp.dma_start(b2r[:, :], a["L1_ffn_b2"][e, :].rearrange("(o n) -> o n", o=1).partition_broadcast(P)).then_inc(es["b2_in"], 16)
            sp.wait_ge(es["x_moe"], blocks * B)
            sp.dma_start(out.rearrange("b n d -> n b d"), x[:, :, :]).then_inc(outs, 16)
            sp.wait_ge(outs, 16)

        @block.gpsimd
        def _(pool):
            pool.memset(ident[:, :], 0.0).then_inc(s_c, 1)
            pool.memset(rmask[4][:, :], 1.0).then_inc(s_c, 1)
            pool.memset(rmask[2][:, :], 1.0).then_inc(s_c, 1)
            pool.memset(eps[:, :], LN_EPS).then_inc(s_c, 1)
            pool.memset(zT[:, :, :, :], 0.0).then_inc(s_c, 1)
            pool.wait_ge(s_c, 5)
            pool.affine_select(out=ident[:, :], in_=ident[:, :], compare_op=ALU.not_equal, fill=1.0, base=0,
                               pattern=[[-1, P]], channel_multiplier=1).then_inc(s_c, 1)
            n = 6
            for hpg in (4, 2):
                w = P // hpg
                m = rmask[hpg][:, :]
                pool.affine_select(out=m, in_=m, compare_op=ALU.is_ge, fill=0.0, base=0,
                                   pattern=[[-w, hpg]], channel_multiplier=1).then_inc(s_c, 1)
                n += 1
                pool.wait_ge(s_c, n)
                pool.affine_select(out=m, in_=m, compare_op=ALU.is_ge, fill=0.0, base=w - 1,
                                   pattern=[[w, hpg]], channel_multiplier=-1).then_inc(s_c, 1)
                n += 1
            pool.wait_ge(s_c, n)

            s = xs[0]
            with pool.Fori(0, B) as b:
                with pool.Fori(0, CT // 2) as j:
                    for u in (0, 1):
                        i = b * CT + j * 2 + u
                        pool.wait_ge(s["z_norm"], i + 1)
                        pool.tensor_tensor(zt[u], zt[u], lnw[:, :], ALU.mult).then_inc(s["z_ready"], 1)
                        pool.wait_ge(s["z_ready"], i * 2 + 1)
                        pool.tensor_tensor(zt[u], zt[u], lnb[:, :], ALU.add).then_inc(s["z_ready"], 1)
            pool.wait_ge(s["wo_in"], 64)
            for b in range(B):
                pool.tensor_tensor(x_res[:, b, :], x_res[:, b, :], lnb[:, :], ALU.add).then_inc(s["res"], 1)
            pool.wait_ge(mi[0]["p_in"], 64)
            pool.wait_ge(ln["z"], B)
            for b in range(B):
                pool.tensor_tensor(x[:, b, :], x[:, b, :], bproj[:, :], ALU.add).then_inc(ms["x_bias"], 1)
            for layer in (0, 1):
                for b in range(B):
                    pool.wait_ge(ms["qt_out"], layer * per["qt_out"] + b + 1)
                    if b >= 2:
                        pool.wait_ge(ms["s_pe"], layer * per["s_pe"] + b - 1)
                    Qm4 = Qm[:, b % 2].rearrange("p (g j) n -> p g j n", g=GROUPS)
                    for j in range(HEADS // GROUPS):
                        i = pool.tensor_scalar(Qm4[:, :, j, :], QT[:, :, b * N:(b + 1) * N], rmask[4][:, j:j + 1], None, ALU.mult)
                    i.then_inc(ms["qm"], 1)
            pool.wait_ge(es["ring_free"], 1)
            pool.memset(ones[:, :], 1.0).then_inc(es["c"], 1)
            pool.memset(upper[:, :], 1.0).then_inc(es["c"], 1)
            pool.iota(slots[:, :], [[1, P]], base=0, channel_multiplier=0, allow_small_or_imprecise_dtypes=True).then_inc(es["c"], 1)
            pool.iota(order[:, :], [[-1, E]], base=E, channel_multiplier=0, allow_small_or_imprecise_dtypes=True).then_inc(es["c"], 1)
            pool.iota(turns[:, :], [[1, TMAX]], base=0, channel_multiplier=0, allow_small_or_imprecise_dtypes=True).then_inc(es["c"], 1)
            pool.wait_ge(es["c"], 5)
            pool.affine_select(out=upper[:, :], in_=upper[:, :], compare_op=ALU.is_gt, fill=0.0, base=0,
                               pattern=[[1, P]], channel_multiplier=-1).then_inc(es["c"], 1)

        @block.scalar
        def _(act):
            def deviation(s, base=0):
                act.wait_ge(s["v"], base + 1)
                act.activation(sd[:, :], mv[:, :, 1], ACT.Sqrt, bias=eps[:, :]).then_inc(s["sd"], 1)

            s = xs[0]
            act.wait_ge(s_c, 10)
            act.wait_ge(s["w_in"], 32)
            act.activation(WKh[:, :, :], kvw[:, :, 0:D], ACT.Copy).then_inc(s["w_split"], 1)
            act.activation(WVh[:, :, :], kvw[:, :, D:2 * D], ACT.Copy).then_inc(s["w_split"], 1)
            deviation(s)
            deviation(s, 1)
            for b in (0, 2):
                act.wait_ge(s["zt_pe"], b + 1)
                act.activation(zT[:, :, b, 1:N + 1], bank(b).rearrange("p (k n) -> p k n", k=KT), ACT.Copy).then_inc(s["zt_ready"], 1)
            for b in range(B):
                act.wait_ge(s["q_pe"], b + 1)
                act.activation(y_st[:, b, :], bank(4 + b), ACT.Square).then_inc(s["q_sq"], 1)
            act.wait_ge(s["q_ss"], 1)
            act.activation(nrm, ssb, ACT.Sqrt).then_inc(s["q_nm"], 1)
            for b in (0, 2):
                act.wait_ge(s["qt_pe"], b + 1)
                act.activation(QT[:, :, b * N:(b + 1) * N], bank(b).rearrange("p (k n) -> p k n", k=KT), ACT.Copy).then_inc(s["qt_ready"], 1)

            def attend(X, s, scale):
                masks = a["mask_BxS2_bk0"].rearrange("b s -> (b s)").bitcast(u8)
                with act.Fori(0, B) as b:
                    act.wait_ge(*at(X, "ao_done", b + 1))
                    if X.layer == 0:
                        act.dma_start(mask8[:, :], masks[bass.ds(b * S, S)].rearrange("(o n) -> o n", o=1).partition_broadcast(P)).then_inc(s["mask_in"], 16)

                    def step(i, rep):
                        t = rep + 1
                        if 0 <= t < X.NT:
                            if t == CT:
                                if rep >= 1:
                                    act.wait_ge(*at(X, "v_done", b * X.NT + i))
                                act.activation(zh[:, t % 2], zT[:, :, b, 1:N + 1], ACT.Copy).then_inc(xc["zh_ready"], 1)
                            else:
                                act.wait_ge(*at(X, "t_done", b * CT + i + 2))
                                if rep >= 1:
                                    act.wait_ge(*at(X, "v_done", b * X.NT + i))
                                act.activation(zh[:, t % 2], bank(t % 2).rearrange("p (k n) -> p k n", k=KT), ACT.Copy).then_inc(xc["zh_ready"], 1)
                        if X.layer == 0 and 0 <= rep + 2 < CT:
                            act.wait_ge(s["st_ready"], b * CT + i + 3)
                            act.activation(xsd[:, rep % 2:rep % 2 + 1], xmv[:, rep % 2, 1:2], ACT.Sqrt, bias=eps[:, :]).then_inc(s["sd_ready"], 1)
                        if 0 <= rep < X.NT:
                            p = rep % 2
                            act.wait_ge(*at(X, "k_done", b * X.NT + i + 1))
                            if X.layer == 0:
                                act.activation(ksq, bank(2 + p), ACT.Square).then_inc(s["sq_ready"], 1)
                                act.wait_ge(s["ss_ready"], b * X.NT + i + 1)
                                act.activation(knm[:, :], kss[:, :], ACT.Sqrt).then_inc(s["nm_ready"], 1)
                            else:
                                if rep >= 2:
                                    act.wait_ge(*at(X, "kt_done", b * X.NT + i - 1))
                                act.activation(kn[p], bank(2 + p), ACT.Copy).then_inc(xc["kn_ready"], 1)
                            act.wait_ge(*at(X, "v_done", b * X.NT + i + 1))
                            act.activation(Vt[:, i, :], bank(4 + p), ACT.Copy).then_inc(xc["v_ready"], 1)
                        if 0 <= rep - 1 < X.NT:
                            p = (rep - 1) % 2
                            act.wait_ge(*at(X, "kt_done", b * X.NT + i))
                            act.activation(KTh[:, :, bass.ts(i - 1, P)], bank(6 + p).rearrange("p (k n) -> p k n", k=KT), ACT.Copy).then_inc(xc["kh_ready"], 1)
                    tile_steps(act, X.NT, step)

                    def copy(hn, q, first):
                        act.wait_ge(*at(X, "pt_done", hn * X.NQ + q + 1))
                        if not first:
                            act.wait_ge(*at(X, "av_done", hn * X.NQ if q == 0 and X.NQ == 5 else (hn - 1) * X.NQ + q + 1))
                        act.activation(PT[:, q, :], bank(X.turned_bank(q)), ACT.Copy).then_inc(xc["ev_a"], 1)

                    def head(g, u, first):
                        hn = b * X.H + g * X.hpg + u
                        if not first:
                            for q in X.by_act:
                                copy(hn - 1, q, isinstance(g, int) and g == 0 and u == 1)
                        p = u % 2
                        act.wait_ge(*at(X, "nb_ready", hn + 1))
                        act.activation(SMv[:, p, 0:X.keys], SMv[:, p, 0:X.keys], ACT.Exp, scale=scale, bias=nb[:, p:p + 1],
                                       accum_out=rs[:, p:p + 1]).then_inc(xc["exp_done"], 1)
                    head_steps(act, X.hpg, head)
                    for q in X.by_act:
                        copy(b * X.H + X.H - 1, q, False)
            attend(X0, s, 8.0)

            def project_out(s, bank0=0):
                for b in (0, 2):
                    act.wait_ge(s["aot_pe"], b + 1)
                    act.activation(zT[:, :, b, 1:N + 1], bank(bank0 + b).rearrange("p (k n) -> p k n", k=KT), ACT.Copy).then_inc(s["aot_ready"], 1)
            project_out(s)
            deviation(s, 2)

            def layer_norm(u, bank0=0):
                def turned(b):
                    act.wait_ge(ln["zt_pe"], u * B + b + 1)
                    act.activation(zT[:, :, b, 1:N + 1], bank(bank0 + b).rearrange("p (k n) -> p k n", k=KT), ACT.Copy).then_inc(ln["zt"], 1)
                for b in range(B):
                    if b == B - 1:
                        turned(0)
                    act.wait_ge(ln["v"], u * B + b + 1)
                    act.activation(sd[:, b:b + 1], mv[:, b, 1:2], ACT.Sqrt, bias=eps[:, :]).then_inc(ln["sd"], 1)
                for b in range(1, B):
                    turned(b)

            def self_attention(layer):
                def own(name, v):
                    return ms[name], v + layer * per[name]

                def out_of_bank(j):
                    act.wait_ge(*own("qkv_pe", j + 1))
                    act.activation(qkv[:, j // 3, (j % 3) * D:(j % 3 + 1) * D], bank((4 + j) % 8), ACT.Copy).then_inc(ms["qkv_out"], 1)

                def turned(b):
                    for w, (dst, done) in enumerate(((QT, "qt_out"), (KTm, "kt_out"))):
                        act.wait_ge(*own("qkt_pe", 2 * b + w + 1))
                        act.activation(dst[:, :, b * N:(b + 1) * N], bank(2 * b + w).rearrange("p (k n) -> p k n", k=KT), ACT.Copy).then_inc(ms[done], 1)
                for b in range(B):
                    if layer == 1:
                        out_of_bank(3 * b)
                        out_of_bank(3 * b + 1)
                    act.wait_ge(*own("qkv_out", 3 * b + 2))
                    if b:
                        act.wait_ge(*own("ss", b))
                    act.activation(hsq[:, :], qkv[:, b, 0:2 * D], ACT.Square).then_inc(ms["sq"], 1)
                    act.wait_ge(*own("ss", b + 1))
                    act.activation(hrs[:, b, :], hss[:, b, :], ACT.Sqrt).then_inc(ms["nm"], 1)
                    if layer == 1:
                        out_of_bank(3 * b + 2)
                    if b == B - 1:
                        turned(0)
                for b in range(1, B):
                    turned(b)
                for b in range(B):
                    act.wait_ge(*own("s_out", b + 1))
                    act.activation(Pm[:, :], Pm[:, :], ACT.Exp, bias=float(layer)).then_inc(ms["e_out"], 1)
                    for q in range(4):
                        act.wait_ge(*own("pt_pe", 4 * b + q + 1))
                        if b:
                            act.wait_ge(*own("av_pe", b))
                        act.activation(PTm[:, q * 512:(q + 1) * 512], bank(4 + (4 * b + q) % 3), ACT.Copy).then_inc(ms["pt_out"], 1)
                if layer == 0:
                    for j in range(3 * KT):
                        act.wait_ge(fs["wt_pe"], j + 1)
                        act.activation(wffT[:, j // KT, j % KT, :], bank(j % 4), ACT.Copy).then_inc(fs["wt"], 1)
                else:
                    for j in range(KT):
                        act.wait_ge(ws["p_tr"], j + 1)
                        act.activation(Wp[:, j, :], bank(j), ACT.Copy).then_inc(ws["p"], 1)
                for b in (0, 2):
                    act.wait_ge(*own("aot_pe", b + 1))
                    act.activation(zT[:, :, b, 1:N + 1], bank(4 + b).rearrange("p (k n) -> p k n", k=KT), ACT.Copy).then_inc(ms["aot_a"], 1)

            layer_norm(0)
            self_attention(0)
            layer_norm(1, 4)
            act.wait_ge(fs["om"], 1)
            act.wait_ge(ln["zt"], 2 * B)
            for n, dst in enumerate((xr, xk)):
                for k in range(KT):
                    act.activation(dst[:, k, :].rearrange("p (b n) -> p b n", b=B), zT[:, k, :, 0:N], ACT.Copy, scale=omu[:, n, k:k + 1]).then_inc(fs["prev"], 1)
            for b in range(B):
                act.wait_ge(fs["r_pe"], b + 1)
                act.activation(rgate[:, b, :], bank(b), ACT.Sigmoid).then_inc(fs["r_out"], 1)
            for n in range(KT):
                act.wait_ge(fs["k_pe"], n + 1)
                act.activation(kact[:, n, :], bank(4 + n), ACT.Relu).then_inc(fs["k_relu"], 1)
            s = xs[1]

            def weight(j):
                w, k = j // KT, j % KT
                if j == 2 * KT:
                    act.wait_ge(spill, 16)
                act.wait_ge(s["w_tr"], j + 1)
                act.activation((wqT, WVh, WKh)[w][:, k, :], bank(4 + k), ACT.Copy).then_inc(s["w_hi"], 1)
            layer_norm(2)
            for j in range(2 * KT):
                weight(j)
            for n in range(KT):
                act.wait_ge(s["qt_pe"], n + 1)
                act.activation(QT[:, n, :], bank(n), ACT.Copy).then_inc(s["qt_ready"], 1)
                weight(2 * KT + n)
            attend(X1, s, HD ** -0.5)
            act.wait_ge(*at(X1, "av_done", B * X1.H * X1.NQ))
            for k in range(KT):
                act.wait_ge(s["wo_tr"], k + 1)
                act.activation(wqT[:, k, :], bank(k), ACT.Copy).then_inc(s["wo_a"], 1)
            project_out(s, 4)
            for j in range(3 * KT):
                w, k = j // KT, j % KT
                act.wait_ge(ws["tr"], j + 1)
                act.activation(WqkvT[:, k, w * D:(w + 1) * D], bank(4 + k), ACT.Copy).then_inc(ws["a"], 1)
            layer_norm(3)
            self_attention(1)
            layer_norm(4, 4)
            act.wait_ge(ln["z"], 5 * B)
            act.activation(zmh[:, :, :], z[:, :, :], ACT.Copy).then_inc(es["zh"], 1)
            act.wait_ge(es["b_pe"], 1)
            act.activation(gwT[:, :, :], ps[:, 5, 0:KT * E].rearrange("p (k e) -> p k e", k=KT), ACT.Copy).then_inc(es["g_t"], 1)
            act.activation(b1T[:, :], ps[:, 5, P:2 * P], ACT.Copy).then_inc(es["g_t"], 1)
            act.wait_ge(es["ex_in"], 1)
            act.activation(ex[:, :, :], ex[:, :, :], ACT.Exp).then_inc(es["ex_out"], 1)
            act.wait_ge(es["table"], 1)
            blocks = act.value_load(tab[0:1, TMAX:TMAX + 1], min_val=1, max_val=TMAX)
            act.wait_ge(es["gather"], 1)
            act.activation(xeT[:, :, :], bank(0).rearrange("p (k n) -> p k n", k=KT), ACT.Copy).then_inc(es["xe"], 1)
            with act.Fori(0, blocks) as t:
                e = act.value_load(tab[0:1, bass.ds(t, 1)], min_val=0, max_val=E - 1)
                for c in range(CH):
                    act.wait_ge(es["up"], t * CH + c + 1)
                    for f in range(KT):
                        act.activation(hT[:, c % 2, f, :], ps[:, 2 + c % 2, f * P:(f + 1) * P], ACT.Relu,
                                       bias=b1T[:, bass.ds(e * FT + (c * KT + f), 1)]).then_inc(es["h"], 1)
                act.wait_ge(es["y_out"], t + 2)
                act.activation(yh[:, :], ysb[:, :], ACT.Copy).then_inc(es["yh"], 1)
                act.wait_ge(es["gather"], t + 2)
                act.activation(xeT[:, :, :], bank(0).rearrange("p (k n) -> p k n", k=KT), ACT.Copy).then_inc(es["xe"], 1)

        @block.vector
        def _(dve):
            def moments(s, src, base, rstd=rstd):
                for b in range(B):
                    dve.bn_stats(st[:, b, :], src(b))
                dve.drain()
                for b in range(B):
                    i = dve.bn_aggr(mv[:, b, :], st[:, b, :])
                i.then_inc(s["v"], 1)
                dve.wait_ge(s["sd"], base + 1)
                dve.reciprocal(rstd[:, :], sd[:, :])
                dve.drain()

            def normalise(s, src, dst, base):
                moments(s, src, base)
                for b in range(B):
                    i = dve.tensor_scalar(dst(b), src(b), mv[:, b, 0:1], rstd[:, b:b + 1], ALU.subtract, ALU.mult)
                    yield b, i

            s = xs[0]
            dve.wait_ge(s_c, 10)
            dve.wait_ge(s["x_in"], 7 * 16)
            for _b in normalise(s, lambda b: x_st[:, b, :], lambda b: z[:, b, :], 0):
                pass
            dve.drain()
            moments(s, lambda b: z[:, b, :], 1)
            for b in range(B):
                dve.scalar_tensor_tensor(z[:, b, :], z[:, b, :], mv[:, b, 0:1], lnw2, ALU.subtract, ALU.mult)
            dve.drain()
            for b in range(B):
                dve.scalar_tensor_tensor(z[:, b, :], z[:, b, :], rstd[:, b:b + 1], lnb2, ALU.mult, ALU.add).then_inc(s["ln_z"], 1)
            dve.wait_ge(s["w_in"], 32)
            dve.wait_ge(s["w_split"], 2)
            dve.tensor_tensor(WKl[:, :, :], kvw[:, :, 0:D], WKh[:, :, :].bitcast(f32), ALU.subtract).then_inc(s["w_split"], 1)
            dve.tensor_tensor(WVl[:, :, :], kvw[:, :, D:2 * D], WVh[:, :, :].bitcast(f32), ALU.subtract).then_inc(s["w_split"], 1)
            for b in (1, 3):
                dve.wait_ge(s["zt_pe"], b + 1)
                dve.tensor_copy(zT[:, :, b, 1:N + 1], bank(b).rearrange("p (k n) -> p k n", k=KT)).then_inc(s["zt_ready"], 1)
            dve.tensor_tensor(qsc, qsc, ksc, ALU.mult)
            dve.wait_ge(s["q_sq"], B)
            for b in range(B):
                i = dve.tensor_reduce(ssb[:, b, :], y_st[:, b, :].rearrange("p (h d) -> p h d", h=X0.H), AX.X, ALU.add)
            i.then_inc(s["q_ss"], 1)
            dve.wait_ge(s["q_nm"], 1)
            dve.tensor_scalar(nrm, nrm, 1e-12, None, ALU.max)
            dve.drain()
            dve.reciprocal(ssb, nrm)
            dve.drain()
            for b in range(B):
                q3 = z[:, b, :].rearrange("p (h d) -> p h d", h=X0.H)
                dve.tensor_tensor(q3, bank(4 + b).rearrange("p (h d) -> p h d", h=X0.H),
                                  ssb[:, b, :].unsqueeze(2).to_broadcast([P, X0.H, X0.d]), ALU.mult)
                dve.drain()
                dve.tensor_tensor(q3, q3, qsc.unsqueeze(1).to_broadcast([P, X0.H, X0.d]), ALU.mult).then_inc(s["q_ready"], 1)
            for b in (1, 3):
                dve.wait_ge(s["qt_pe"], b + 1)
                dve.tensor_copy(QT[:, :, b * N:(b + 1) * N], bank(b).rearrange("p (k n) -> p k n", k=KT)).then_inc(s["qt_ready"], 1)

            def attend(X, s, scale):
                dve.memset(pmax[:, 4:5], 0.0).then_inc(xc["ao_done"], 1)
                with dve.Fori(0, B) as b:
                    if X.layer == 0:
                        dve.wait_ge(s["mask_in"], b * 16 + 16)
                        dve.tensor_scalar(mbias[:, 0:S], mask8[:, :], -1.0, -NEG, ALU.add, ALU.mult)
                        dve.memset(mbias[:, S:X.keys], 0.0)

                    def step(i, rep):
                        if X.layer == 0 and 0 <= rep + 2 < CT:
                            p = rep % 2
                            dve.wait_ge(*at(X, f"x_ld{p}", b * (CT // 2 * 16) + (i - p + 2) * 8 + 16))
                            dve.bn_stats(xst[:, p, :], xin[p])
                            dve.drain()
                            dve.bn_aggr(xmv[:, p, :], xst[:, p, :]).then_inc(s["st_ready"], 1)
                        t = rep + 1
                        if 0 <= t < X.NT:
                            dve.wait_ge(*at(X, "zh_ready", b * X.NT + i + 2))
                            src = zT[:, :, b, 1:N + 1] if t == CT else bank(t % 2).rearrange("p (k n) -> p k n", k=KT)
                            dve.tensor_tensor(zl[:, t % 2], src, zh[:, t % 2].bitcast(f32), ALU.subtract).then_inc(xc["zl_ready"], 1)
                        if X.layer == 0 and 0 <= rep + 2 < CT:
                            dve.wait_ge(s["sd_ready"], b * CT + i + 3)
                            dve.reciprocal(xrs[:, p:p + 1], xsd[:, p:p + 1])
                            dve.drain()
                            if rep >= 0:
                                dve.wait_ge(*at(X, "t_done", b * CT + i + 1))
                            dve.tensor_scalar(zt[p], xin[p], xmv[:, p, 0:1], xrs[:, p:p + 1], ALU.subtract, ALU.mult).then_inc(s["z_norm"], 1)
                        if X.layer == 0 and 0 <= rep < X.NT:
                            p = rep % 2
                            dve.wait_ge(s["sq_ready"], b * X.NT + i + 1)
                            dve.tensor_reduce(kss[:, :], ksq.rearrange("p (h d) -> p h d", h=X.H), AX.X, ALU.add).then_inc(s["ss_ready"], 1)
                            dve.wait_ge(s["nm_ready"], b * X.NT + i + 1)
                            dve.tensor_scalar(knm[:, :], knm[:, :], 1e-12, None, ALU.max)
                            dve.drain()
                            dve.reciprocal(krn[:, :], knm[:, :])
                            dve.drain()
                            if rep >= 2:
                                dve.wait_ge(*at(X, "kt_done", b * X.NT + i - 1))
                            dve.tensor_tensor(kn[p].rearrange("p (h d) -> p h d", h=X.H), bank(2 + p).rearrange("p (h d) -> p h d", h=X.H),
                                              krn[:, :].unsqueeze(2).to_broadcast([P, X.H, X.d]), ALU.mult).then_inc(xc["kn_ready"], 1)
                        if 0 <= rep - 1 < X.NT:
                            p = (rep - 1) % 2
                            dve.wait_ge(*at(X, "kh_ready", b * X.NT + i))
                            dve.tensor_tensor(KTl[:, :, bass.ts(i - 1, P)], bank(6 + p).rearrange("p (k n) -> p k n", k=KT),
                                              KTh[:, :, bass.ts(i - 1, P)].bitcast(f32), ALU.subtract).then_inc(xc["kl_ready"], 1)
                    tile_steps(dve, X.NT, step)

                    def copy(hn, q, first):
                        w = P * len(X.quad(q))
                        dve.wait_ge(*at(X, "pt_done", hn * X.NQ + q + 1))
                        if q == 4:
                            dve.wait_ge(*at(X, "av_done", hn * X.NQ + 1))
                        elif not first:
                            dve.wait_ge(*at(X, "av_done", (hn - 1) * X.NQ + q + 1))
                        dve.tensor_copy(PT[:, q % 4, 0:w], bank(X.turned_bank(q), w)).then_inc(xc["ev_d"], 1)

                    def output(g, u):
                        h = g * X.hpg + u
                        p = u % 2
                        dve.wait_ge(*at(X, "av_done", (b * X.H + h + 1) * X.NQ))
                        dve.reciprocal(rinv[:, p:p + 1], rs[:, p:p + 1])
                        dve.drain()
                        dve.tensor_scalar(z[:, b, bass.ds(h * X.d, X.d)], ps[:, 7, u * P + u * X.d:u * P + (u + 1) * X.d],
                                          rinv[:, p:p + 1], None, ALU.mult).then_inc(xc["o_done"], 1)

                    def head(g, u, first):
                        hn = b * X.H + g * X.hpg + u
                        p = u % 2
                        second = isinstance(g, int) and g == 0 and u == 1
                        if not (first or second):
                            dve.wait_ge(*at(X, "s_done", hn * 2 - 2))
                        q = QT[:, g, bass.ts(b, N)]
                        row = rmask[X.hpg][:, u:u + 1]
                        dve.tensor_scalar(Qmh[:, p, :], q, row, None, ALU.mult)
                        dve.drain()
                        dve.scalar_tensor_tensor(Qml[:, p, :], q, row, Qmh[:, p, :].bitcast(f32), ALU.mult, ALU.subtract).then_inc(xc["qm_ready"], 1)
                        for k, (lo, hi) in enumerate(X.halves):
                            if k == 1 and X.NQ == 5 and not first:
                                copy(hn - 1, 1, second)
                            dve.wait_ge(*at(X, "s_done", hn * 2 + k + 1))
                            if k == 0 and not (first or second):
                                dve.wait_ge(*at(X, "pt_done", (hn - 1) * X.NQ))
                            src = ps[:, lo // 512:5, :].rearrange("p k n -> p (k n)")[:, 0:hi - lo]
                            m = pmax[:, 2 * p + k:2 * p + k + 1]
                            dve.memset(pmax[:, 4 + 2 * p + k:5 + 2 * p + k], 0.0)
                            if X.layer == 0:
                                dve.tensor_tensor_reduce(out=SMv[:, p, lo:hi], in0=src, in1=mbias[:, lo:hi], scale=1.0, scalar=-3.0e38,
                                                         op0=ALU.add, op1=ALU.max, accum_out=m).then_inc(xc["s_taken"], 1)
                            else:
                                dve.tensor_scalar(SMv[:, p, lo:hi], src, 1.0, None, ALU.mult, ALU.max, accum_out=m).then_inc(xc["s_taken"], 1)
                            if k == 0 and not (first or second):
                                output(*((g, u - 2) if u >= 2 else (g - 1, X.hpg + u - 2)))
                        dve.drain()
                        dve.tensor_scalar(nb[:, p:p + 1], pmax[:, 2 * p:2 * p + 1], pmax[:, 2 * p + 1:2 * p + 2], -scale, ALU.max, ALU.mult).then_inc(xc["nb_ready"], 1)
                        if not first:
                            for q in X.by_dve:
                                if q > 1 or X.NQ == 4:
                                    copy(hn - 1, q, second)
                    head_steps(dve, X.hpg, head)
                    output(GROUPS - 1, X.hpg - 2)
                    for q in X.by_dve:
                        copy(b * X.H + X.H - 1, q, False)
                    output(GROUPS - 1, X.hpg - 1)
                    dve.memset(pmax[:, 4:5], 0.0).then_inc(xc["ao_done"], 1)
            attend(X0, s, 8.0)

            def project_out(s, bank0=0):
                for b in (1, 3):
                    dve.wait_ge(s["aot_pe"], b + 1)
                    dve.tensor_copy(zT[:, :, b, 1:N + 1], bank(bank0 + b).rearrange("p (k n) -> p k n", k=KT)).then_inc(s["aot_ready"], 1)
            project_out(s)
            dve.wait_ge(s["y_pe"], B)
            dve.wait_ge(s["res"], B)
            moments(s, lambda b: bank(4 + b), 2, y_rstd)
            for b in range(B):
                dve.scalar_tensor_tensor(y_st[:, b, :], bank(4 + b), mv[:, b, 0:1], lnw[:, :], ALU.subtract, ALU.mult)
            dve.drain()

            def residual_norm(u, update):
                for b in range(B):
                    update(b)
                    dve.drain()
                    dve.bn_stats(st[:, b, :], x[:, b, :])
                    dve.drain()
                    dve.bn_aggr(mv[:, b, :], st[:, b, :]).then_inc(ln["v"], 1)
                    dve.wait_ge(ln["sd"], u * B + b + 1)
                    dve.reciprocal(rstd[:, b:b + 1], sd[:, b:b + 1])
                    dve.drain()
                    dve.tensor_scalar(z[:, b, :], x[:, b, :], mv[:, b, 0:1], rstd[:, b:b + 1], ALU.subtract, ALU.mult).then_inc(ln["z"], 1)

            def heads(t, h):
                return t.rearrange("p (h d) -> p h d", h=h)

            def self_attention(layer, eps_, shift):
                def own(name, v):
                    return ms[name], v + layer * per[name]
                scale = HD ** -0.5
                dve.wait_ge(mi[layer]["p_in"], (4 if layer == 0 else 3) * 16)
                if layer == 0:
                    dve.tensor_tensor(gains[:, 0, :], gains[:, 0, :], gains[:, 1, :], ALU.mult)
                else:
                    for half in (0, 1):
                        g = gains[:, 0, half * (HD // 2):(half + 1) * (HD // 2)]
                        dve.tensor_tensor(rope_g[:, 0, half, :], g, rope_t[:, 0, :], ALU.mult)
                        dve.tensor_tensor(rope_g[:, 1, 1 - half, :], g, rope_t[:, 2 - half, :], ALU.mult)

                def add_bias(j):
                    dve.wait_ge(*own("qkv_pe", j + 1))
                    cols = slice((j % 3) * D, (j % 3 + 1) * D)
                    dve.tensor_tensor(qkv[:, j // 3, cols], bank((4 + j) % 8), bqkv[:, cols], ALU.add).then_inc(ms["qkv_out"], 1)
                for b in range(B):
                    if layer == 0:
                        add_bias(3 * b)
                        add_bias(3 * b + 1)
                    dve.wait_ge(*own("sq", b + 1))
                    dve.tensor_reduce(hss[:, b, :], heads(hsq[:, :], 2 * HEADS), AX.X, ALU.add)
                    dve.drain()
                    dve.tensor_scalar(hss[:, b, :], hss[:, b, :], 1.0 / HD, eps_, ALU.mult, ALU.add).then_inc(ms["ss"], 1)
                    if layer == 0:
                        add_bias(3 * b + 2)
                    dve.wait_ge(*own("nm", b + 1))
                    dve.reciprocal(hss[:, b, :], hrs[:, b, :])
                    dve.drain()
                    t = qkv[:, b, 0:2 * D]
                    dve.tensor_tensor(heads(t, 2 * HEADS), heads(t, 2 * HEADS), hss[:, b, :].unsqueeze(2).to_broadcast([P, 2 * HEADS, HD]), ALU.mult)
                    dve.drain()
                    if layer == 0:
                        t = qkv[:, b, 0:D]
                        i = dve.tensor_tensor(heads(t, HEADS), heads(t, HEADS), gains[:, 0, :].unsqueeze(1).to_broadcast([P, HEADS, HD]), ALU.mult)
                    else:
                        u = t.rearrange("p (h a d) -> p h a d", h=2 * HEADS, a=2)
                        v = hrot[:, :].rearrange("p (h a d) -> p h a d", h=2 * HEADS, a=2)
                        for half in (0, 1):
                            dve.tensor_tensor(v[:, :, half, :], u[:, :, 1 - half, :], rope_g[:, 1, half, :].unsqueeze(1).to_broadcast([P, 2 * HEADS, HD // 2]), ALU.mult)
                        dve.drain()
                        dve.tensor_tensor(heads(t, 2 * HEADS), heads(t, 2 * HEADS),
                                          rope_g[:, 0].rearrange("p a d -> p (a d)").unsqueeze(1).to_broadcast([P, 2 * HEADS, HD]), ALU.mult)
                        dve.drain()
                        i = dve.tensor_tensor(t, t, hrot[:, :], ALU.add)
                    i.then_inc(ms["qk_ready"], 1)
                S3 = ps[:, 0:4, :].rearrange("p k n -> p (k n)").rearrange("p (h n) -> p h n", h=HEADS)
                P3 = Pm[:, :].rearrange("p (h n) -> p h n", h=HEADS)

                def shifted(b):
                    dve.wait_ge(*own("s_pe", b + 1))
                    dve.tensor_reduce(mx[:, :], S3, AX.X, ALU.max)
                    dve.drain()
                    dve.tensor_scalar(mx[:, :], mx[:, :], scale, shift, ALU.mult, ALU.add)
                    dve.drain()
                    if b:
                        dve.wait_ge(*own("pt_pe", 4 * b))
                    dve.scalar_tensor_tensor(P3, S3, scale, mx[:, :].unsqueeze(2).to_broadcast([P, HEADS, N]), ALU.mult, ALU.subtract).then_inc(ms["s_out"], 1)
                shifted(0)
                for b in range(B):
                    dve.wait_ge(*own("e_out", b + 1))
                    total = hsum[:, b % 2, :]
                    dve.tensor_reduce(total, P3, AX.X, ALU.add)
                    if b + 1 < B:
                        shifted(b + 1)
                    dve.drain()
                    dve.reciprocal(total, total)
                    dve.drain()
                    dve.wait_ge(*own("av_pe", b + 1))
                    dve.tensor_tensor(heads(z[:, b, :], HEADS), heads(bank(7), HEADS), total.unsqueeze(2).to_broadcast([P, HEADS, HD]), ALU.mult).then_inc(ms["ao"], 1)
                for b in (1, 3):
                    dve.wait_ge(*own("aot_pe", b + 1))
                    dve.tensor_copy(zT[:, :, b, 1:N + 1], bank(4 + b).rearrange("p (k n) -> p k n", k=KT)).then_inc(ms["aot_d"], 1)

            def attended(layer):
                def update(b):
                    if layer == 0 and b == 0:
                        dve.wait_ge(ms["x_bias"], B)
                    dve.wait_ge(ms["y_pe"], layer * per["y_pe"] + b + 1)
                    dve.tensor_tensor(x[:, b, :], x[:, b, :], bank(b), ALU.add).then_inc(ms["x_att"], 1)
                return update

            def first_sum(b):
                dve.scalar_tensor_tensor(x[:, b, :], y_st[:, b, :], y_rstd[:, b:b + 1], x_res[:, b, :], ALU.mult, ALU.add).then_inc(s["x_done"], 1)
            residual_norm(0, first_sum)
            self_attention(0, 1e-6, 0.0)
            dve.wait_ge(fs["w_in"], 80)
            dve.tensor_scalar(omu[:, :, :], mu[:, :, :], -1.0, 1.0, ALU.mult, ALU.add).then_inc(fs["om"], 1)
            residual_norm(1, attended(0))
            for n, dst in enumerate((xr, xk)):
                for k in range(KT):
                    to = dst[:, k, :].rearrange("p (b n) -> p b n", b=B)
                    dve.wait_ge(fs["prev"], n * KT + k + 1)
                    dve.scalar_tensor_tensor(to, zT[:, k, :, 1:N + 1], mu[:, n, k:k + 1], to, ALU.mult, ALU.add).then_inc(fs["mix"], 1)
            for n in range(KT):
                dve.wait_ge(fs["k_relu"], n + 1)
                dve.tensor_tensor(kact[:, n, :], kact[:, n, :], kact[:, n, :], ALU.mult).then_inc(fs["k_out"], 1)
            dve.wait_ge(fs["r_out"], B)

            def gated(b):
                dve.wait_ge(fs["v_pe"], b + 1)
                dve.tensor_tensor(rgate[:, b, :], rgate[:, b, :], bank(b), ALU.mult)
                dve.drain()
                dve.tensor_tensor(x[:, b, :], x[:, b, :], rgate[:, b, :], ALU.add).then_inc(fs["x_ff"], 1)
            residual_norm(2, gated)
            s = xs[1]
            for j in range(KT, 3 * KT):
                w, k = j // KT, j % KT
                hi, lo = ((WVh, WVl), (WKh, WKl))[w - 1]
                dve.wait_ge(s["w_hi"], j + 1)
                dve.tensor_tensor(lo[:, k, :], bank(4 + k), hi[:, k, :].bitcast(f32), ALU.subtract).then_inc(s["w_split"], 1)
            attend(X1, s, HD ** -0.5)
            project_out(s, 4)
            dve.wait_ge(s["wo_in"], 32)

            def second_sum(b):
                dve.wait_ge(s["y_pe"], b + 1)
                dve.tensor_tensor(x[:, b, :], bank(b), x_res[:, b, :], ALU.add).then_inc(s["x_done"], 1)
            residual_norm(3, second_sum)
            self_attention(1, 1e-5, 1.0)
            residual_norm(4, attended(1))
            dve.wait_ge(es["zh"], 1)
            dve.tensor_tensor(zml[:, :, :], z[:, :, :], zmh[:, :, :].bitcast(f32), ALU.subtract).then_inc(es["zl"], 1)
            dve.wait_ge(es["c"], 6)
            dve.wait_ge(es["logits"], 1)
            dve.tensor_copy(lg[:, :, :], ps[:, 4, 0:B * E].rearrange("p (b e) -> p b e", b=B))
            dve.drain()

            def wide(v):
                return v.unsqueeze(2).to_broadcast([P, B, E])

            def over(v):
                return v.unsqueeze(1).to_broadcast([P, B, E])
            dve.tensor_reduce(lm[:, :], lg[:, :, :], AX.X, ALU.max)
            dve.drain()
            dve.tensor_tensor(ex[:, :, :], lg[:, :, :], wide(lm[:, :]), ALU.subtract).then_inc(es["ex_in"], 1)
            dve.tensor_tensor(cand[:, :, :], lg[:, :, :], wide(lm[:, :]), ALU.is_equal)
            dve.drain()
            dve.tensor_tensor(cand[:, :, :], cand[:, :, :], over(order[:, :]), ALU.mult)
            dve.drain()
            dve.tensor_reduce(lm[:, :], cand[:, :, :], AX.X, ALU.max)
            dve.drain()
            dve.tensor_tensor(oh[:, :, :], cand[:, :, :], wide(lm[:, :]), ALU.is_equal).then_inc(es["oh"], 1)
            dve.wait_ge(es["ex_out"], 1)
            dve.tensor_reduce(gate[:, :], ex[:, :, :], AX.X, ALU.add)
            dve.drain()
            dve.reciprocal(gate[:, :], gate[:, :]).then_inc(es["y_out"], 1)
            dve.wait_ge(es["ranks"], 1)
            count = ps[:, 6, B * E:(B + 1) * E]
            dve.tensor_scalar(nblk[:, :], count, 0.0, None, ALU.is_gt)
            for j in range(1, T // P):
                dve.drain()
                dve.tensor_scalar(cmp8[:, :], count, float(j * P), None, ALU.is_gt)
                dve.drain()
                dve.tensor_tensor(nblk[:, :], nblk[:, :], cmp8[:, :], ALU.add)
            dve.drain()
            dve.tensor_copy(last[:, :], nblk[:, :])
            for j in range(1, E):
                dve.drain()
                dve.tensor_tensor(last[:, j:j + 1], last[:, j:j + 1], last[:, j - 1:j], ALU.add)
            dve.drain()
            dve.tensor_tensor(first[:, :], last[:, :], nblk[:, :], ALU.subtract)
            dve.tensor_tensor(cmpt[:, :, :], last[:, :].unsqueeze(1).to_broadcast([P, TMAX, E]), turns[:, :].unsqueeze(2).to_broadcast([P, TMAX, E]), ALU.is_le)
            dve.drain()
            dve.tensor_reduce(tabf[:, 0:TMAX], cmpt[:, :, :], AX.X, ALU.add)
            dve.tensor_scalar(first[:, :], first[:, :], float(P), None, ALU.mult)
            dve.tensor_copy(tabf[:, TMAX:TMAX + 1], last[:, E - 1:E])
            dve.drain()
            dve.tensor_scalar(tabf[:, 0:TMAX], tabf[:, 0:TMAX], float(E - 1), None, ALU.min)
            dve.drain()
            dve.tensor_copy(tab[:, :], tabf[:, :]).then_inc(es["table"], 1)
            dve.tensor_tensor(cand[:, :, :], ps[:, 6, 0:B * E].rearrange("p (b e) -> p b e", b=B), over(first[:, :]), ALU.add)
            dve.drain()
            dve.tensor_tensor(cand[:, :, :], cand[:, :, :], oh[:, :, :], ALU.mult)
            dve.drain()
            dve.tensor_reduce(pos[:, :], cand[:, :, :], AX.X, ALU.add)
            dve.drain()
            dve.wait_ge(es["table"], 1)
            blocks = dve.value_load(tab[0:1, TMAX:TMAX + 1], min_val=1, max_val=TMAX)

            def dispatch():
                for b in range(B):
                    i = dve.tensor_scalar(Dm[:, b, :], slots[:, :], pos[:, b:b + 1], None, ALU.is_equal)
                i.then_inc(es["dm"], 1)
                dve.drain()
                dve.tensor_scalar(pos[:, :], pos[:, :], -float(P), None, ALU.add)
                dve.drain()
            dispatch()
            with dve.Fori(0, blocks) as t:
                dve.wait_ge(es["dt_pe"], t + 1)
                dve.tensor_copy(DT[:, :, :], bank(1).rearrange("p (b n) -> p b n", b=B)).then_inc(es["dt"], 1)
                dispatch()
                dve.wait_ge(es["ring_free"], t * CH + 2 * CH)
                dve.wait_ge(es["b2_in"], t * 16 + 16)
                dve.tensor_tensor(ysb[:, :], bank(4), b2r[:, :], ALU.add).then_inc(es["y_out"], 1)
                dve.wait_ge(es["yh"], t + 1)
                dve.tensor_tensor(yl[:, :], ysb[:, :], yh[:, :].bitcast(f32), ALU.subtract).then_inc(es["yl"], 1)
                for b in range(B):
                    dve.wait_ge(es["mixed"], t * B + b + 1)
                    dve.scalar_tensor_tensor(x[:, b, :], bank(5 + b % 3), gate[:, b:b + 1], x[:, b, :], ALU.mult, ALU.add).then_inc(es["x_moe"], 1)

        @block.tensor
        def _(pe):
            def transpose4(dst, src):
                for k in range(KT):
                    i = pe.transpose(dst[:, k * P:(k + 1) * P], src[:, k * P:(k + 1) * P], ident[:, :])
                return i

            def product(dst, lhs, rhs):
                for k in range(KT):
                    i = pe.matmul(dst, lhs(k), rhs(k), start=(k == 0), stop=(k == KT - 1))
                return i

            s = xs[0]
            pe.wait_ge(s_c, 10)
            for b in range(B):
                pe.wait_ge(s["ln_z"], b + 1)
                transpose4(bank(b), z[:, b, :]).then_inc(s["zt_pe"], 1)
            pe.wait_ge(s["w_in"], 32)
            pe.wait_ge(s["zt_ready"], B)
            for b in range(B):
                product(bank(4 + b), lambda k: zT[:, k, b, 1:N + 1], lambda k: wq_st[:, k, :]).then_inc(s["q_pe"], 1)
            for b in range(B):
                pe.wait_ge(s["q_ready"], b + 1)
                transpose4(bank(b), z[:, b, :]).then_inc(s["qt_pe"], 1)

            def attend(X, s):
                pe.wait_ge(s["w_split"], X.splits)
                pe.wait_ge(s["qt_ready"], B)
                with pe.Fori(0, B) as b:
                    pe.wait_ge(*at(X, "ao_done", b + 1))

                    def step(i, rep):
                        t = rep + 1
                        if 0 <= t < CT:
                            if X.layer == 0:
                                pe.wait_ge(s["z_ready"], (b * CT + i + 2) * 2)
                                src = zt[t % 2]
                            else:
                                pe.wait_ge(*at(X, f"x_ld{t % 2}", b * (CT // 2 * 16) + (i + 1 - t % 2) * 8 + 16))
                                src = xin[t % 2]
                            if t >= 2:
                                pe.wait_ge(*at(X, "zl_ready", b * X.NT + i))
                            transpose4(bank(t % 2), src).then_inc(xc["t_done"], 1)
                        if 0 <= rep < X.NT:
                            p = rep % 2
                            n = b * X.NT + i
                            pe.wait_ge(*at(X, "zl_ready", n + 1))
                            if rep >= 2:
                                pe.wait_ge(*at(X, "kn_ready", n - 1))
                            for k in range(KT):
                                pe.matmul(bank(2 + p), zh[:, p, k, :], WKh[:, k, :], start=(k == 0), stop=False)
                                pe.matmul(bank(2 + p), zh[:, p, k, :], WKl[:, k, :], start=False, stop=False)
                                m = pe.matmul(bank(2 + p), zl[:, p, k, :], WKh[:, k, :], start=False, stop=(k == KT - 1))
                            m.then_inc(xc["k_done"], 1)
                            if rep >= 2:
                                pe.wait_ge(*at(X, "v_ready", n - 1))
                            for k in range(KT):
                                pe.matmul(bank(4 + p), zh[:, p, k, :], WVh[:, k, :], start=(k == 0), stop=False)
                                pe.matmul(bank(4 + p), zh[:, p, k, :], WVl[:, k, :], start=False, stop=False)
                                m = pe.matmul(bank(4 + p), zl[:, p, k, :], WVh[:, k, :], start=False, stop=(k == KT - 1))
                            m.then_inc(xc["v_done"], 1)
                        if 0 <= rep - 1 < X.NT:
                            p = (rep - 1) % 2
                            pe.wait_ge(*at(X, "kn_ready", b * X.NT + i))
                            if rep - 1 >= 2:
                                pe.wait_ge(*at(X, "kl_ready", b * X.NT + i - 2))
                            transpose4(bank(6 + p), kn[p]).then_inc(xc["kt_done"], 1)
                    tile_steps(pe, X.NT, step)
                    pe.wait_ge(*at(X, "kl_ready", b * X.NT + X.NT))
                    pe.wait_ge(*at(X, "v_ready", b * X.NT + X.NT))

                    def copied(hn, q):
                        if q in X.by_act:
                            pe.wait_ge(*at(X, "ev_a", hn * X.nA + X.by_act.index(q) + 1))
                        else:
                            pe.wait_ge(*at(X, "ev_d", hn * X.nD + X.by_dve.index(q) + 1))

                    def turn(h, u, q, first):
                        hn = b * X.H + h
                        if q == 0:
                            pe.wait_ge(*at(X, "exp_done", hn + 1))
                        back, r = X.before(q)
                        if not (first and back):
                            copied(hn - back, r)
                        for n, kt in enumerate(X.quad(q)):
                            i = pe.transpose(ps[:, X.turned_bank(q), n * P:(n + 1) * P], SMv[:, u % 2, kt * P:(kt + 1) * P], ident[:, :])
                        i.then_inc(xc["pt_done"], 1)

                    def add(g, u, q, first):
                        hn = b * X.H + g * X.hpg + u
                        if q == 0 and not first:
                            pe.wait_ge(*at(X, "o_done", hn))
                        copied(hn, q)
                        for n, kt in enumerate(X.quad(q)):
                            i = pe.matmul(bank(7)[:, u * P:(u + 1) * P], PT[:, q % 4, n * P:(n + 1) * P], Vt[:, kt, bass.ds(g * P, P)],
                                          start=(kt == 0), stop=(kt == X.NT - 1))
                        i.then_inc(xc["av_done"], 1)

                    def score(g, u, c, first):
                        hn = b * X.H + g * X.hpg + u
                        p = u % 2
                        k = c // 2 if c < 4 else 1
                        if c == 0:
                            pe.wait_ge(*at(X, "qm_ready", hn + 1))
                        if c in (0, 2) and not first:
                            pe.wait_ge(*at(X, "s_taken", hn * 2 - 1 + k))
                        lo = c * 512
                        w = min(512, X.keys - lo)
                        o = bank(c, w)
                        pe.matmul(o, Qmh[:, p, :], KTh[:, g, lo:lo + w], start=True, stop=False)
                        pe.matmul(o, Qmh[:, p, :], KTl[:, g, lo:lo + w], start=False, stop=False)
                        i = pe.matmul(o, Qml[:, p, :], KTh[:, g, lo:lo + w], start=False, stop=True)
                        if c == 1 or lo + w == X.keys:
                            i.then_inc(xc["s_done"], 1)

                    plan = ("S0 S1 T0 S2 T1 S3 T2 A0 T3 A1 A2 A3" if X.NQ == 4 else "S0 S1 T0 S2 T1 S3 S4 T2 A0 T3 A1 T4 A2 A3 A4").split()

                    def head(g, u, first):
                        gg, uu = (g, u - 1) if u else (g - 1, X.hpg - 1)
                        for what, q in plan:
                            q = int(q)
                            if what == "S":
                                score(g, u, q, first)
                            elif first:
                                continue
                            elif what == "T":
                                turn(gg * X.hpg + uu, uu, q, isinstance(g, int) and g == 0 and u == 1)
                            else:
                                add(gg, uu, q, isinstance(g, int) and g == 0 and u == 1)
                    head_steps(pe, X.hpg, head)
                    for what, q in plan:
                        if what == "T":
                            turn(X.H - 1, X.hpg - 1, int(q), False)
                        elif what == "A":
                            add(GROUPS - 1, X.hpg - 1, int(q), False)
            attend(X0, s)

            def project_out(s, wo):
                for b in range(B):
                    pe.wait_ge(*at(X0, "ao_done", B + 1))
                    transpose4(bank(b), z[:, b, :]).then_inc(s["aot_pe"], 1)
                pe.wait_ge(s["aot_ready"], B)
                for b in range(B):
                    product(bank(4 + b), lambda k: zT[:, k, b, 1:N + 1], lambda k: wo[:, k, :]).then_inc(s["y_pe"], 1)
            pe.wait_ge(s["wo_in"], 64)
            project_out(s, wo_st)

            def norm_turn(u, bs, bank0=0):
                for b in bs:
                    pe.wait_ge(ln["z"], u * B + b + 1)
                    transpose4(bank(bank0 + b), z[:, b, :]).then_inc(ln["zt_pe"], 1)

            def turn_weight(dst, w, k):
                for t in range(KT):
                    i = pe.transpose(dst[:, t * P:(t + 1) * P], w[:, t, k * P:(k + 1) * P], ident[:, :])
                return i

            def tokens(b):
                return lambda k: zT[:, k, b, 1:N + 1]

            def self_attention(layer):
                def own(name, v):
                    return ms[name], v + layer * per[name]
                w_in = Wqkv if layer == 0 else WqkvT
                u = 3 * layer

                def projections(b):
                    pe.wait_ge(ln["zt"], u * B + (b + 1 if b < 2 else B))
                    for j in range(3 * b, 3 * b + 3):
                        if j >= 8:
                            pe.wait_ge(*own("qkv_out", j - 7))
                        cols = slice((j % 3) * D, (j % 3 + 1) * D)
                        product(bank((4 + j) % 8), tokens(b), lambda k: w_in[:, k, cols]).then_inc(ms["qkv_pe"], 1)

                def turn(b):
                    pe.wait_ge(*own("qk_ready", b + 1))
                    pe.wait_ge(*own("qkv_out", 2 * b + 6))
                    transpose4(bank(2 * b), qkv[:, b, 0:D]).then_inc(ms["qkt_pe"], 1)
                    transpose4(bank(2 * b + 1), qkv[:, b, D:2 * D]).then_inc(ms["qkt_pe"], 1)

                def scores(b):
                    pe.wait_ge(*own("qm", b + 1))
                    pe.wait_ge(*own("kt_out", max(b + 1, 2)))
                    if b:
                        pe.wait_ge(*own("s_out", b))
                    for h in range(HEADS):
                        i = pe.matmul(ps[:, h // 4, (h % 4) * N:(h % 4 + 1) * N], Qm[:, b % 2, h, :], KTm[:, h // 4, b * N:(b + 1) * N], start=True, stop=True)
                    i.then_inc(ms["s_pe"], 1)

                norm_turn(u, (0, 1, 2))
                projections(0)
                norm_turn(u, (3,))
                projections(1)
                projections(2)
                turn(0)
                projections(3)
                turn(1)
                scores(0)
                turn(2)
                turn(3)
                for b in range(B):
                    if b + 1 < B:
                        scores(b + 1)
                    pe.wait_ge(*own("e_out", b + 1))
                    pe.wait_ge(*own("kt_out", B))
                    for q in range(4):
                        n = 4 * b + q
                        if n >= 3:
                            pe.wait_ge(*own("pt_out", n - 2))
                        for j in range(4):
                            h = 4 * q + j
                            i = pe.transpose(ps[:, 4 + n % 3, j * N:(j + 1) * N], Pm[:, h * N:(h + 1) * N], ident[:, :])
                        i.then_inc(ms["pt_pe"], 1)
                    if b:
                        pe.wait_ge(*own("ao", b))
                    for q in range(4):
                        pe.wait_ge(*own("pt_out", 4 * b + q + 1))
                        for j in range(4):
                            h = 4 * q + j
                            i = pe.matmul(ps[:, 7, h * HD:(h + 1) * HD], PTm[:, h * N:(h + 1) * N], qkv[:, b, 2 * D + h * HD:2 * D + (h + 1) * HD], start=True, stop=True)
                    i.then_inc(ms["av_pe"], 1)
                if layer == 0:
                    pe.wait_ge(fs["w_in"], 80)
                    for j in range(3 * KT):
                        if j >= 4:
                            pe.wait_ge(fs["wt"], j - 3)
                        turn_weight(bank(j % 4), wst[:, j // KT], j % KT).then_inc(fs["wt_pe"], 1)
                else:
                    pe.wait_ge(ws["wp_in"], 16)
                    for k in range(KT):
                        turn_weight(bank(k), wffT[:, 0], k).then_inc(ws["p_tr"], 1)
                for b in range(B):
                    pe.wait_ge(*own("ao", b + 1))
                    transpose4(bank(4 + b), z[:, b, :]).then_inc(ms["aot_pe"], 1)
                if layer == 0:
                    pe.wait_ge(mi[0]["wp_in"], 16)
                    pe.wait_ge(fs["wt"], 3 * KT)
                else:
                    pe.wait_ge(ws["p"], KT)
                for b in range(B):
                    pe.wait_ge(*own("aot_d" if b % 2 else "aot_a", b // 2 + 1))
                    product(bank(b), tokens(b), lambda k: Wp[:, k, :]).then_inc(ms["y_pe"], 1)

            pe.wait_ge(mi[0]["w_in"], 16)
            self_attention(0)
            norm_turn(1, range(B), 4)
            for b in range(B):
                for k in range(KT):
                    if b == 0:
                        pe.wait_ge(fs["mix"], k + 1)
                    i = pe.matmul(bank(b), xr[:, k, b * N:(b + 1) * N], wffT[:, 0, k, :], start=(k == 0), stop=(k == KT - 1))
                i.then_inc(fs["r_pe"], 1)
            pe.wait_ge(fs["mix"], 2 * KT)
            for n in range(KT):
                product(bank(4 + n), lambda k: wffT[:, 1, k, n * P:(n + 1) * P], lambda k: xk[:, k, :]).then_inc(fs["k_pe"], 1)
            pe.wait_ge(fs["r_out"], B)
            pe.wait_ge(fs["k_out"], KT)
            for b in range(B):
                product(bank(b), lambda k: kact[:, k, b * N:(b + 1) * N], lambda k: wffT[:, 2, k, :]).then_inc(fs["v_pe"], 1)

            s = xs[1]
            pe.wait_ge(s["w_in"], 48)

            def weight(j):
                w, k = j // KT, j % KT
                if j >= KT:
                    pe.wait_ge(s["w_hi"], j - 3)
                if j >= 2 * KT:
                    pe.wait_ge(s["w_split"], j - 7)
                turn_weight(bank(4 + k), wst[:, (0, 2, 1)[w]], k).then_inc(s["w_tr"], 1)
            for j in range(KT):
                weight(j)
            norm_turn(2, range(B))
            for j in range(KT, 2 * KT):
                weight(j)
            pe.wait_ge(s["w_hi"], KT)
            pe.wait_ge(ln["zt"], 3 * B)
            for n in range(KT):
                product(bank(n), lambda k: wqT[:, k, n * P:(n + 1) * P], lambda k: zT[:, k, :, 1:N + 1]).then_inc(s["qt_pe"], 1)
                weight(2 * KT + n)
            attend(X1, s)
            pe.wait_ge(s["wo_in"], 32)
            pe.wait_ge(*at(X1, "s_taken", 2 * B * X1.H))
            for k in range(KT):
                turn_weight(bank(k), wo_st, k).then_inc(s["wo_tr"], 1)
            for b in range(B):
                pe.wait_ge(*at(X1, "ao_done", B + 1))
                transpose4(bank(4 + b), z[:, b, :]).then_inc(s["aot_pe"], 1)
            pe.wait_ge(s["aot_ready"], B)
            pe.wait_ge(s["wo_a"], KT)
            for b in range(B):
                product(bank(b), tokens(b), lambda k: wqT[:, k, :]).then_inc(s["y_pe"], 1)
            pe.wait_ge(ws["w_in"], 48)
            for j in range(3 * KT):
                if j >= KT:
                    pe.wait_ge(ws["a"], j - 3)
                turn_weight(bank(4 + j % KT), qkv_st[:, j // KT], j % KT).then_inc(ws["tr"], 1)
            pe.wait_ge(ws["a"], 3 * KT)
            self_attention(1)
            norm_turn(4, range(B), 4)
            pe.wait_ge(ln["zt"], 5 * B)
            pe.wait_ge(es["zh"], 1)
            for c in range(CH):
                i = pe.transpose(ps[:, 7, 0:P], ident[:, :], ident[:, :])
                i.then_inc(es["ring_free"], 1)
            pe.wait_ge(es["g_in"], 32)
            for k in range(KT):
                pe.transpose(ps[:, 5, k * E:(k + 1) * E], gwn[:, k * P:(k + 1) * P], ident[0:E, 0:E])
            pe.transpose(ps[:, 5, P:2 * P], b1n[:, :], ident[:, :]).then_inc(es["b_pe"], 1)
            pe.wait_ge(es["g_t"], 2)
            for b in range(B):
                i = product(ps[:, 4, b * E:(b + 1) * E], tokens(b), lambda k: gwT[:, k, :])
            i.then_inc(es["logits"], 1)
            pe.wait_ge(es["c"], 6)
            pe.wait_ge(es["oh"], 1)
            for b in range(B + 1):
                o = ps[:, 6, b * E:(b + 1) * E]
                for j in range(b):
                    i = pe.matmul(o, ones[:, :], oh[:, j, :], start=(j == 0), stop=(j == b - 1 and b == B))
                if b < B:
                    i = pe.matmul(o, upper[:, :], oh[:, b, :], start=(b == 0), stop=True)
            i.then_inc(es["ranks"], 1)
            pe.wait_ge(es["table"], 1)
            blocks = pe.value_load(tab[0:1, TMAX:TMAX + 1], min_val=1, max_val=TMAX)
            pe.wait_ge(es["zl"], 1)

            def gather():
                for k in range(KT):
                    o = ps[:, 0, k * P:(k + 1) * P]
                    for b in range(B):
                        pe.matmul(o, zmh[:, b, k * P:(k + 1) * P], Dm[:, b, :], start=(b == 0), stop=False)
                        i = pe.matmul(o, zml[:, b, k * P:(k + 1) * P], Dm[:, b, :], start=False, stop=(b == B - 1))
                i.then_inc(es["gather"], 1)
            pe.wait_ge(es["dm"], 1)
            gather()
            with pe.Fori(0, blocks) as t:
                def up(c):
                    pe.wait_ge(es[f"w1_in{c}"], t * 16 + 16)
                    for f in range(KT):
                        i = product(ps[:, 2 + c % 2, f * P:(f + 1) * P], lambda k: w1r[:, c, k, f * P:(f + 1) * P], lambda k: xeT[:, k, :])
                    i.then_inc(es["up"], 1)

                def down(c):
                    pe.wait_ge(es[f"w2_in{c}"], t * 16 + 16)
                    pe.wait_ge(es["h"], t * FT + (c + 1) * KT)
                    for f in range(KT):
                        i = pe.matmul(bank(4), hT[:, c % 2, f, :], w2r[:, c, f, :], start=(c == 0 and f == 0), stop=(c == CH - 1 and f == KT - 1))
                    i.then_inc(es["ring_free"], 1)
                pe.wait_ge(es["xe"], t + 1)
                up(0)
                for b in range(B):
                    i = pe.transpose(ps[:, 1, b * P:(b + 1) * P], Dm[:, b, :].bitcast(f32), ident[:, :])
                i.then_inc(es["dt_pe"], 1)
                for c in range(1, CH):
                    up(c)
                    down(c - 1)
                down(CH - 1)
                pe.wait_ge(es["dm"], t + 2)
                gather()
                pe.wait_ge(es["dt"], t + 1)
                pe.wait_ge(es["yl"], t + 1)
                for b in range(B):
                    if b == 3:
                        pe.wait_ge(es["x_moe"], t * B + 1)
                    pe.matmul(bank(5 + b % 3), DT[:, b, :], yh[:, :], start=True, stop=False)
                    pe.matmul(bank(5 + b % 3), DT[:, b, :], yl[:, :], start=False, stop=True).then_inc(es["mixed"], 1)


def kernel(**inputs):
    import numpy as _np
    import concourse.bacc as _bacc
    from concourse import mybir as _mybir
    from concourse.bass_utils import run_bass_kernel_spmd as _run

    nc = _bacc.Bacc("TRN2", target_bir_lowering=False, num_devices=1)
    arrays, args = {}, {}
    for name, value in inputs.items():
        v = _np.ascontiguousarray(value)
        if v.dtype == _np.bool_:
            v = v.view(_np.int32)
        arrays[f"in_{name}"] = v
        args[name] = nc.dram_tensor(f"in_{name}", v.shape, _mybir.dt.from_np(v.dtype), kind="ExternalInput").ap()
    angles = _np.outer(_np.arange(N, dtype=_np.float32), (1.0 / 10000.0 ** (_np.arange(0, HD, 2, dtype=_np.float32) / HD)).astype(_np.float32))
    table = _np.stack([_np.cos(angles), _np.sin(angles), -_np.sin(angles)], axis=1).astype(_np.float32)
    bits = table.view(_np.uint32)
    table = ((bits + 0x7FFF + ((bits >> 16) & 1)) & _np.uint32(0xFFFF0000)).view(_np.float32)
    arrays["rope_table"] = table
    args["rope"] = nc.dram_tensor("rope_table", table.shape, _mybir.dt.float32, kind="ExternalInput").ap()
    res = nc.dram_tensor("out_x", (B, N, D), _mybir.dt.float32, kind="ExternalOutput").ap()
    perceiver(nc, args, res)
    r = _run(nc, [arrays], core_ids=[0])
    return r.results[0]["out_x"]
```

```python
import numpy as np
import concourse.bass as bass
from concourse import mybir
from contextlib import ExitStack

f32 = mybir.dt.float32
f32r = mybir.dt.float32r
bf16 = mybir.dt.bfloat16
u8 = mybir.dt.uint8
i32 = mybir.dt.int32
ALU = mybir.AluOpType
ACT = mybir.ActivationFunctionType
AX = mybir.AxisListType

P = 128
B, N, D = 4, 128, 512
S = 2048
KT = D // P
T = B * N
CT = S // P
LN_EPS = 1e-5
NEG = -1.0e30
GROUPS = D // P


class Cross:

    def __init__(self, layer, heads, latent_keys):
        self.layer, self.H = layer, heads
        self.d = D // heads
        self.hpg = heads // GROUPS
        self.NT = CT + (1 if latent_keys else 0)
        self.keys = self.NT * P
        self.halves = [(0, 1024), (1024, self.keys)]
        self.NQ = -(-self.NT // 4)
        self.by_act, self.by_dve = ((0, 1, 2, 3), ()) if self.NQ == 4 else ((0, 2), (1, 3, 4))
        self.nA, self.nD = len(self.by_act), len(self.by_dve)
        self.splits = 4 if layer == 0 else 8

    def turned_bank(self, q):
        return 4 + q % 3 if self.NQ == 4 else 5 + q % 2

    def before(self, q):
        n = 3 if self.NQ == 4 else 2
        if q >= n:
            return 0, q - n
        return 1, max(r for r in range(self.NQ) if self.turned_bank(r) == self.turned_bank(q))

    def quad(self, q):
        return range(4 * q, min(4 * q + 4, self.NT))


HEADS, HD = 16, 32
E, F = 8, 2048
CH = F // 512
FT = F // P
TMAX = T // P + E - 1
X0 = Cross(0, 8, True)
X1 = Cross(1, 16, False)


def tile_steps(eng, nt, body):
    body(0, 0)
    with eng.Fori(0, 6) as j:
        for u in (1, 2):
            body(j * 2 + u, u)
    for s in range(13, nt + 1):
        body(s, s)


def batch_steps(eng, lead, body):
    lead(0)
    with eng.Fori(0, B - 1) as b:
        body(b, False)
    body(B - 1, True)


def head_steps(eng, hpg, body):
    for u in range(hpg):
        body(0, u, u == 0)
    with eng.Fori(1, GROUPS) as g:
        for u in range(hpg):
            body(g, u, False)


def perceiver(nc, a, out):
    top = ExitStack()
    with top:
        def sb(name, shape, dt=f32, ctx=top):
            return ctx.enter_context(nc.sbuf_tensor(name, shape, dt))

        def sem(name):
            return top.enter_context(nc.semaphore(name))

        x_dram = nc.dram_tensor("x_spill", [B, N, D], f32).ap()

        z = sb("z", [P, B, D])
        zT = sb("zT", [P, KT, B, N + 1])
        QT = sb("QT", [P, GROUPS, T])
        ident = sb("ident", [P, P])
        rmask = {4: sb("rmask4", [P, 4]), 2: sb("rmask2", [P, 2])}
        eps = sb("eps", [P, 1])
        st = sb("st", [P, B, 6])
        mv = sb("mv", [P, B, 2])
        sd = sb("sd", [P, B])
        rstd = sb("rstd", [P, B])
        y_mv = sb("y_mv", [P, B, 2])
        y_sd = sb("y_sd", [P, B])
        y_rstd = sb("y_rstd", [P, B])
        ps = top.enter_context(nc.psum_tensor("ps", [P, 8, 512], f32))

        def bank(k, w=512):
            return ps[:, k, 0:w]

        cross = ExitStack()
        WKh = sb("WKh", [P, KT, D], f32r, cross)
        WKl = sb("WKl", [P, KT, D], f32r, cross)
        WVh = sb("WVh", [P, KT, D], f32r, cross)
        WVl = sb("WVl", [P, KT, D], f32r, cross)
        KTh = sb("KTh", [P, GROUPS, X0.keys], f32r, cross)
        KTl = sb("KTl", [P, GROUPS, X0.keys], f32r, cross)
        zhl = sb("zhl", [P, 2, 2, KT, P], f32r, cross)
        zh, zl = zhl[:, 0], zhl[:, 1]
        Qmh = sb("Qmh", [P, 2, P], f32r, cross)
        Qml = sb("Qml", [P, 2, P], f32r, cross)
        V = sb("V", [P, X0.NT * D], f32, cross)
        SM = sb("SM", [P, 2 * X0.keys], f32, cross)
        PT = sb("PT", [P, 4, 512], f32, cross)
        lnw = sb("lnw", [P, D], f32, cross)
        lnb = sb("lnb", [P, D], f32, cross)
        mask8 = sb("mask8", [P, S], u8, cross)
        mbias = sb("mbias", [P, X0.keys], bf16, cross)
        rs = sb("rs", [P, 2], f32, cross)
        rinv = sb("rinv", [P, 2], f32, cross)
        pmax = sb("pmax", [P, 8], f32, cross)
        nb = sb("nb", [P, 2], f32, cross)
        xst = sb("xst", [P, 2, 6], f32, cross)
        xmv = sb("xmv", [P, 2, 2], f32, cross)
        xsd = sb("xsd", [P, 2], f32, cross)
        xrs = sb("xrs", [P, 2], f32, cross)
        kss = sb("kss", [P, 8], f32, cross)
        knm = sb("knm", [P, 8], f32, cross)
        krn = sb("krn", [P, 8], f32, cross)
        cross.close()
        Vt = V[:, :].rearrange("p (t n) -> p t n", n=D)
        SMv = SM[:, :].rearrange("p (u n) -> p u n", u=2)
        tilebuf = SM[:, 0:8 * D].rearrange("p (t n) -> p t n", n=D)
        xin = [tilebuf[:, k, :] for k in (0, 1)]
        zt = [tilebuf[:, k, :] for k in (2, 3)]
        kn = [tilebuf[:, k, :] for k in (4, 5)]
        ksq = tilebuf[:, 6, :]
        kvw = SM[:, 0:KT * 1024].rearrange("p (k n) -> p k n", k=KT)
        def vbuf(k):
            return V[:, k * 2048:(k + 1) * 2048]
        wq_st = vbuf(0).rearrange("p (k n) -> p k n", k=KT)
        wqT = vbuf(1).rearrange("p (k n) -> p k n", k=KT)
        x_st = vbuf(2).rearrange("p (b n) -> p b n", b=B)
        lnw2 = V[:, 6144:6656]
        lnb2 = V[:, 6656:7168]
        qsc = V[:, 7168:7232]
        ksc = V[:, 7232:7296]
        y_st = vbuf(1).rearrange("p (b n) -> p b n", b=B)
        ssb = V[:, 7296:7296 + 32].rearrange("p (b h) -> p b h", b=B)
        nrm = V[:, 7328:7328 + 32].rearrange("p (b h) -> p b h", b=B)
        mid = ExitStack()
        x = sb("x", [P, B, D], f32, mid)
        Wqkv = sb("Wqkv", [P, KT, 3 * D], f32, mid)
        Wp = sb("Wp", [P, KT, D], f32, mid)
        wst = sb("wst", [P, 3, KT, D], f32, mid)
        wffT = sb("wffT", [P, 3, KT, D], f32, mid)
        qkv = sb("qkv", [P, B, 3 * D], f32, mid)
        Qm = sb("Qm", [P, 2, HEADS, N], f32, mid)
        KTm = sb("KTm", [P, GROUPS, T], f32, mid)
        Pm = sb("Pm", [P, HEADS * N], f32, mid)
        PTm = sb("PTm", [P, HEADS * N], f32, mid)
        bqkv = sb("bqkv", [P, 3 * D], f32, mid)
        bproj = sb("bproj", [P, D], f32, mid)
        gains = sb("gains", [P, 2, HD], f32, mid)
        rope_t = sb("rope_t", [P, 3, HD // 2], f32, mid)
        hss = sb("hss", [P, B, 2 * HEADS], f32, mid)
        hrs = sb("hrs", [P, B, 2 * HEADS], f32, mid)
        mx = sb("mx", [P, HEADS], f32, mid)
        hsum = sb("hsum", [P, 2, HEADS], f32, mid)
        mu = sb("mu", [P, 2, KT], f32, mid)
        omu = sb("omu", [P, 2, KT], f32, mid)
        hsq = sb("hsq", [P, 2 * D], f32, mid)
        hrot = sb("hrot", [P, 2 * D], f32, mid)
        rope_g = sb("rope_g", [P, 2, 2, HD // 2], f32, mid)
        b1n = sb("b1n", [P, P], f32, mid)
        b1T = sb("b1T", [P, P], f32, mid)
        gwn = sb("gwn", [E, D], f32, mid)
        gwT = sb("gwT", [P, KT, E], f32, mid)
        upper = sb("upper", [P, P], f32, mid)
        ones = sb("ones", [P, P], f32, mid)
        slots = sb("slots", [P, P], f32, mid)
        order = sb("order", [P, E], f32, mid)
        turns = sb("turns", [P, TMAX], f32, mid)
        mid.close()
        before = 4 * KT * D + 2 * GROUPS * X0.keys - (B * D + 10 * KT * D)
        assert 0 <= before <= B * 3 * D - KT * D
        wo_st = qkv[:, :, :].rearrange("p b n -> p (b n)")[:, before:before + KT * D].rearrange("p (k n) -> p k n", k=KT)
        WqkvT = wst[:, :, :, :].rearrange("p w k n -> p (w k n)").rearrange("p (k n) -> p k n", k=KT)
        qkv_st = Wqkv[:, :, :].rearrange("p k n -> p (k n)").rearrange("p (w k n) -> p w k n", w=3, k=KT)
        moe = ExitStack()
        sb("x_keep", [P, B, D], f32, moe)
        w1r = sb("w1r", [P, CH, KT, 512], f32, moe)
        w2r = sb("w2r", [P, CH, KT, 512], f32, moe)
        zmh = sb("zmh", [P, B, D], f32r, moe)
        zml = sb("zml", [P, B, D], f32r, moe)
        Dm = sb("Dm", [P, B, P], f32r, moe)
        DT = sb("DT", [P, B, P], f32r, moe)
        xeT = sb("xeT", [P, KT, P], f32, moe)
        hT = sb("hT", [P, 2, KT, P], f32, moe)
        ysb = sb("ysb", [P, D], f32, moe)
        yh = sb("yh", [P, D], f32r, moe)
        yl = sb("yl", [P, D], f32r, moe)
        b2r = sb("b2r", [P, D], f32, moe)
        lg = sb("lg", [P, B, E], f32, moe)
        lm = sb("lm", [P, B], f32, moe)
        oh = sb("oh", [P, B + 1, E], f32, moe)
        cand = sb("cand", [P, B, E], f32, moe)
        ex = sb("ex", [P, B, E], f32, moe)
        gate = sb("gate", [P, B], f32, moe)
        pos = sb("pos", [P, B], f32, moe)
        nblk = sb("nblk", [P, E], f32, moe)
        cmp8 = sb("cmp8", [P, E], f32, moe)
        last = sb("last", [P, E], f32, moe)
        first = sb("first", [P, E], f32, moe)
        cmpt = sb("cmpt", [P, TMAX, E], f32, moe)
        tabf = sb("tabf", [P, TMAX + 1], f32, moe)
        tab = sb("tab", [P, TMAX + 1], i32, moe)
        moe.close()
        ffbuf = qkv[:, :, :].rearrange("p b n -> p (b n)").rearrange("p (w k t) -> p w k t", w=3, k=KT)
        xr, xk, kact = (ffbuf[:, w] for w in range(3))
        rgate = Pm[:, :].rearrange("p (b n) -> p b n", b=B)

        s_c = sem("consts")

        class Signals(dict):

            def __init__(self, part):
                self.part = part

            def __missing__(self, name):
                self[name] = sem(f"{self.part}_{name}")
                return self[name]
        xs = {0: Signals("x0"), 1: Signals("x1")}
        xc = Signals("xc")
        tiles, heads_ = B * X0.NT, B * X0.H
        first_adds = dict(x_ld0=B * CT // 2 * 16, x_ld1=B * CT // 2 * 16, t_done=B * CT, zh_ready=tiles, zl_ready=tiles, k_done=tiles, v_done=tiles,
                          kn_ready=tiles, kt_done=tiles, kh_ready=tiles, kl_ready=tiles, v_ready=tiles, qm_ready=heads_, s_done=2 * heads_,
                          s_taken=2 * heads_, nb_ready=heads_, exp_done=heads_, pt_done=heads_ * X0.NQ, ev_a=heads_ * X0.nA, ev_d=heads_ * X0.nD,
                          av_done=heads_ * X0.NQ, o_done=heads_, ao_done=B + 1)

        def at(X, name, v):
            return xc[name], v + X.layer * first_adds[name]
        outs = sem("outs")
        ln = Signals("ln")
        ms = Signals("self")
        per = dict(qkv_pe=12, qkv_out=12, sq=4, ss=4, nm=4, qk_ready=4, qkt_pe=8, qt_out=4, kt_out=4, qm=4, s_pe=4, s_out=4, e_out=4,
                   pt_pe=16, pt_out=16, av_pe=4, ao=4, aot_pe=4, aot_a=2, aot_d=2, y_pe=4, x_att=4)
        fs = Signals("ff")
        ws = Signals("selfw")
        es = Signals("moe")
        mi = {0: Signals("in0"), 1: Signals("in1")}
        spill = sem("spill")

        block = top.enter_context(nc.Block())

        @block.sync
        def _(sp):
            s = xs[0]
            sp.dma_start(x_st, a["x"].rearrange("b n d -> n b d")).then_inc(s["x_in"], 16)
            for dst, src in ((lnw2, a["L0_xattn_ln_l_w"]), (lnb2, a["L0_xattn_ln_l_b"]), (qsc, a["L0_xattn_q_scale"]),
                             (ksc, a["L0_xattn_k_scale"]), (lnw[:, :], a["L0_xattn_ln_x_w"]), (lnb[:, :], a["L0_xattn_ln_x_b"])):
                sp.dma_start(dst, src.rearrange("(o n) -> o n", o=1).partition_broadcast(P)).then_inc(s["p_in"], 16)
            sp.dma_start(wq_st, a["L0_xattn_Wq"].rearrange("(k p) n -> p k n", p=P)).then_inc(s["w_in"], 16)
            sp.dma_start(kvw, a["L0_xattn_Wkv"].rearrange("(k p) n -> p k n", p=P)).then_inc(s["w_in"], 16)

            def context(X, s):
                ctx = a["ctx_1024"].rearrange("b s d -> (b s) d")
                if X.layer == 0:
                    sp.wait_ge(s["w_split"], X.splits)

                def entry(b):
                    row = b * S

                    def load(i, rep):
                        if rep >= 2:
                            if X.layer == 0:
                                sp.wait_ge(s["z_norm"], b * CT + i - 1)
                            else:
                                sp.wait_ge(*at(X, "t_done", b * CT + i - 1))
                        sp.dma_start(xin[rep % 2], ctx[bass.ds(row + i * P, P), :]).then_inc(xc[f"x_ld{rep % 2}"], 16)
                    load(0, 0)
                    load(1, 1)
                    with sp.Fori(1, CT // 2) as j:
                        load(j * 2, 2)
                        load(j * 2 + 1, 3)
                entry(0)
                with sp.Fori(1, B) as b:
                    sp.wait_ge(*at(X, "pt_done", (b * X.H - 1) * X.NQ))
                    entry(b)

            def row(v):
                return v.rearrange("(o n) -> o n", o=1).partition_broadcast(P)

            def native(w):
                return w.rearrange("(t p) n -> p t n", p=P)

            m = mi[0]
            context(X0, s)
            sp.wait_ge(*at(X0, "v_done", B * X0.NT))
            sp.dma_start(wo_st, a["L0_xattn_Wo"].rearrange("(k p) n -> p k n", p=P)).then_inc(s["wo_in"], 16)
            sp.dma_start(x[:, :, :], a["x"].rearrange("b n d -> n b d")).then_inc(s["wo_in"], 16)
            sp.wait_ge(s["z_ready"], B * CT * 2)
            sp.dma_start(lnw[:, :], row(a["L0_xattn_ln_o_w"])).then_inc(s["wo_in"], 16)
            sp.dma_start(lnb[:, :], row(a["L0_xattn_ln_o_b"])).then_inc(s["wo_in"], 16)
            sp.dma_start(Wqkv[:, :, :], native(a["L0_attn_W_qkv"])).then_inc(m["w_in"], 16)
            sp.wait_ge(*at(X0, "ao_done", B + 1))
            sp.dma_start(bqkv[:, :], row(a["L0_attn_b_qkv"])).then_inc(m["p_in"], 16)
            sp.dma_start(bproj[:, :], row(a["L0_attn_b_proj"])).then_inc(m["p_in"], 16)
            sp.dma_start(gains[:, 0, :], row(a["L0_attn_qn_w"])).then_inc(m["p_in"], 16)
            sp.dma_start(gains[:, 1, :], row(a["L0_attn_kn_w"])).then_inc(m["p_in"], 16)
            sp.dma_start(Wp[:, :, :], native(a["L0_attn_W_proj"])).then_inc(m["wp_in"], 16)
            for n, w in enumerate(("L0_ffn_W_r", "L0_ffn_W_k", "L0_ffn_W_v")):
                sp.dma_start(wst[:, n], native(a[w])).then_inc(fs["w_in"], 16)
            for n, w in enumerate(("L0_ffn_mu_r", "L0_ffn_mu_k")):
                sp.dma_start(mu[:, n, :], a[w].rearrange("(k p) -> p k", p=P), allow_slow_non_contiguous=True).then_inc(fs["w_in"], 16)
            s = xs[1]
            sp.wait_ge(fs["wt"], 3 * KT)
            for n, w in enumerate(("L1_xattn_wq", "L1_xattn_wk", "L1_xattn_wv")):
                sp.dma_start(wst[:, n], native(a[w])).then_inc(s["w_in"], 16)
            sp.wait_ge(fs["x_ff"], B)
            sp.dma_start(x_dram.rearrange("b n d -> n b d"), x[:, :, :]).then_inc(spill, 16)
            sp.wait_ge(spill, 16)
            context(X1, s)
            sp.wait_ge(*at(X1, "v_done", B * X1.NT))
            sp.dma_start(wo_st, native(a["L1_xattn_wo"])).then_inc(s["wo_in"], 16)
            sp.dma_start(x[:, :, :], x_dram.rearrange("b n d -> n b d")).then_inc(s["wo_in"], 16)
            for n, w in enumerate(("L1_attn_wq", "L1_attn_wk", "L1_attn_wv")):
                sp.dma_start(qkv_st[:, n], native(a[w])).then_inc(ws["w_in"], 16)
            m = mi[1]
            sp.wait_ge(*at(X1, "ao_done", B + 1))
            sp.dma_start(gwn[:, :], a["L1_ffn_gate_w"]).then_inc(es["g_in"], 16)
            sp.dma_start(b1n[:, :], a["L1_ffn_b1"].rearrange("e (f p) -> (e f) p", p=P)).then_inc(es["g_in"], 16)
            sp.dma_start(wffT[:, 0], native(a["L1_attn_wproj"])).then_inc(ws["wp_in"], 16)
            sp.dma_start(gains[:, 0, :], row(a["L1_attn_g_rms"])).then_inc(m["p_in"], 16)
            sp.dma_start(gains[:, 1, :], row(a["L1_attn_g_rms"])).then_inc(m["p_in"], 16)
            sp.dma_start(rope_t[:, :, :], a["rope"]).then_inc(m["p_in"], 16)
            sp.wait_ge(es["ring_free"], 1)
            sp.wait_ge(es["table"], 1)
            blocks = sp.value_load(tab[0:1, TMAX:TMAX + 1], min_val=1, max_val=TMAX)
            w1 = a["L1_ffn_w1"].rearrange("e (k p) f -> e p k f", p=P)
            w2 = a["L1_ffn_w2"].rearrange("e (f p) n -> e p f n", p=P)
            with sp.Fori(0, blocks) as t:
                e = sp.value_load(tab[0:1, bass.ds(t, 1)], min_val=0, max_val=E - 1)
                for c in range(CH):
                    sp.wait_ge(es["ring_free"], t * CH + c + 1)
                    sp.dma_start(w1r[:, c], w1[e, :, :, c * 512:(c + 1) * 512]).then_inc(es[f"w1_in{c}"], 16)
                    sp.dma_start(w2r[:, c], w2[e, :, c * KT:(c + 1) * KT, :]).then_inc(es[f"w2_in{c}"], 16)
                sp.wait_ge(es["y_out"], t + 1)
                sp.dma_start(b2r[:, :], a["L1_ffn_b2"][e, :].rearrange("(o n) -> o n", o=1).partition_broadcast(P)).then_inc(es["b2_in"], 16)
            sp.wait_ge(es["x_moe"], blocks * B)
            sp.dma_start(out.rearrange("b n d -> n b d"), x[:, :, :]).then_inc(outs, 16)
            sp.wait_ge(outs, 16)

        @block.gpsimd
        def _(pool):
            pool.memset(ident[:, :], 0.0).then_inc(s_c, 1)
            pool.memset(rmask[4][:, :], 1.0).then_inc(s_c, 1)
            pool.memset(rmask[2][:, :], 1.0).then_inc(s_c, 1)
            pool.memset(eps[:, :], LN_EPS).then_inc(s_c, 1)
            pool.memset(zT[:, :, :, :], 0.0).then_inc(s_c, 1)
            pool.wait_ge(s_c, 5)
            pool.affine_select(out=ident[:, :], in_=ident[:, :], compare_op=ALU.not_equal, fill=1.0, base=0,
                               pattern=[[-1, P]], channel_multiplier=1).then_inc(s_c, 1)
            n = 6
            for hpg in (4, 2):
                w = P // hpg
                m = rmask[hpg][:, :]
                pool.affine_select(out=m, in_=m, compare_op=ALU.is_ge, fill=0.0, base=0,
                                   pattern=[[-w, hpg]], channel_multiplier=1).then_inc(s_c, 1)
                n += 1
                pool.wait_ge(s_c, n)
                pool.affine_select(out=m, in_=m, compare_op=ALU.is_ge, fill=0.0, base=w - 1,
                                   pattern=[[w, hpg]], channel_multiplier=-1).then_inc(s_c, 1)
                n += 1
            pool.wait_ge(s_c, n)

            s = xs[0]
            with pool.Fori(0, B) as b:
                with pool.Fori(0, CT // 2) as j:
                    for u in (0, 1):
                        i = b * CT + j * 2 + u
                        pool.wait_ge(s["z_norm"], i + 1)
                        pool.tensor_tensor(zt[u], zt[u], lnw[:, :], ALU.mult).then_inc(s["z_ready"], 1)
                        pool.wait_ge(s["z_ready"], i * 2 + 1)
                        pool.tensor_tensor(zt[u], zt[u], lnb[:, :], ALU.add).then_inc(s["z_ready"], 1)
            pool.wait_ge(s["wo_in"], 64)
            for b in range(B):
                pool.tensor_tensor(x[:, b, :], x[:, b, :], lnb[:, :], ALU.add).then_inc(s["res"], 1)
            pool.wait_ge(mi[0]["p_in"], 64)
            pool.wait_ge(ln["z"], B)
            for b in range(B):
                pool.tensor_tensor(x[:, b, :], x[:, b, :], bproj[:, :], ALU.add).then_inc(ms["x_bias"], 1)
            pool.wait_ge(*at(X1, "ao_done", B + 1))
            pool.memset(ones[:, :], 1.0).then_inc(es["c"], 1)
            pool.memset(upper[:, :], 1.0).then_inc(es["c"], 1)
            pool.iota(slots[:, :], [[1, P]], base=0, channel_multiplier=0, allow_small_or_imprecise_dtypes=True).then_inc(es["c"], 1)
            pool.iota(order[:, :], [[-1, E]], base=E, channel_multiplier=0, allow_small_or_imprecise_dtypes=True).then_inc(es["c"], 1)
            pool.iota(turns[:, :], [[1, TMAX]], base=0, channel_multiplier=0, allow_small_or_imprecise_dtypes=True).then_inc(es["c"], 1)
            pool.wait_ge(es["c"], 5)
            pool.affine_select(out=upper[:, :], in_=upper[:, :], compare_op=ALU.is_gt, fill=0.0, base=0,
                               pattern=[[1, P]], channel_multiplier=-1).then_inc(es["c"], 1)

        @block.scalar
        def _(act):
            def deviation(s, base=0):
                act.wait_ge(s["v"], base + 1)
                act.activation(sd[:, :], mv[:, :, 1], ACT.Sqrt, bias=eps[:, :]).then_inc(s["sd"], 1)

            s = xs[0]
            act.wait_ge(s_c, 10)
            deviation(s)
            deviation(s, 1)
            act.wait_ge(s["w_in"], 32)
            act.activation(WKh[:, :, :], kvw[:, :, 0:D], ACT.Copy).then_inc(s["w_split"], 1)
            act.activation(WVh[:, :, :], kvw[:, :, D:2 * D], ACT.Copy).then_inc(s["w_split"], 1)
            for b in (0, 2):
                act.wait_ge(s["zt_pe"], b + 1)
                act.activation(zT[:, :, b, 1:N + 1], bank(b).rearrange("p (k n) -> p k n", k=KT), ACT.Copy).then_inc(s["zt_ready"], 1)
            def queries():
                for b in range(B):
                    act.wait_ge(s["q_pe"], b + 1)
                    act.activation(y_st[:, b, :], bank(4 + b), ACT.Square).then_inc(s["q_sq"], 1)
                    act.wait_ge(s["q_ss"], b + 1)
                    act.activation(nrm[:, b, :], ssb[:, b, :], ACT.Sqrt).then_inc(s["q_nm"], 1)
                for b in (0, 2):
                    act.wait_ge(s["qt_pe"], b + 1)
                    act.activation(QT[:, :, b * N:(b + 1) * N], bank(b).rearrange("p (k n) -> p k n", k=KT), ACT.Copy).then_inc(s["qt_ready"], 1)

            def attend(X, s, scale, before_tiles=lambda: None):
                masks = a["mask_BxS2_bk0"].rearrange("b s -> (b s)").bitcast(u8)

                def high(bb):
                    act.wait_ge(*at(X, "t_done", bb * CT + 1))
                    act.activation(zh[:, 0], bank(0).rearrange("p (k n) -> p k n", k=KT), ACT.Copy).then_inc(xc["zh_ready"], 1)

                def deviate(tile, p):
                    act.wait_ge(s["st_ready"], tile + 1)
                    act.activation(xsd[:, p:p + 1], xmv[:, p, 1:2], ACT.Sqrt, bias=eps[:, :]).then_inc(s["sd_ready"], 1)

                def load_mask(bb):
                    act.dma_start(mask8[:, :], masks[bass.ds(bb * S, S)].rearrange("(o n) -> o n", o=1).partition_broadcast(P)).then_inc(s["mask_in"], 16)

                def lead(bb):
                    if X.layer == 0:
                        load_mask(bb)
                        deviate(bb * CT, 0)
                        deviate(bb * CT + 1, 1)
                    before_tiles()
                    high(bb)

                def entry(b, is_last):
                    def step(i, rep):
                        if X.layer == 0 and rep + 2 < CT:
                            deviate(b * CT + i + 2, rep % 2)
                        t = rep + 1
                        if t < X.NT:
                            if t == CT:
                                act.wait_ge(*at(X, "v_done", b * X.NT + i))
                                act.activation(zh[:, t % 2], zT[:, :, b, 1:N + 1], ACT.Copy).then_inc(xc["zh_ready"], 1)
                            else:
                                act.wait_ge(*at(X, "t_done", b * CT + i + 2))
                                if rep >= 1:
                                    act.wait_ge(*at(X, "v_done", b * X.NT + i))
                                act.activation(zh[:, t % 2], bank(t % 2).rearrange("p (k n) -> p k n", k=KT), ACT.Copy).then_inc(xc["zh_ready"], 1)
                        if rep < X.NT:
                            p = rep % 2
                            act.wait_ge(*at(X, "k_done", b * X.NT + i + 1))
                            if X.layer == 0:
                                act.activation(ksq, bank(2 + p), ACT.Square).then_inc(s["sq_ready"], 1)
                                act.wait_ge(s["ss_ready"], b * X.NT + i + 1)
                                act.activation(knm[:, :], kss[:, :], ACT.Sqrt).then_inc(s["nm_ready"], 1)
                            else:
                                if rep >= 2:
                                    act.wait_ge(*at(X, "kt_done", b * X.NT + i - 1))
                                act.activation(kn[p], bank(2 + p), ACT.Copy).then_inc(xc["kn_ready"], 1)
                            act.wait_ge(*at(X, "v_done", b * X.NT + i + 1))
                            act.activation(Vt[:, i, :], bank(4 + p), ACT.Copy).then_inc(xc["v_ready"], 1)
                        if 0 <= rep - 1 < X.NT:
                            p = (rep - 1) % 2
                            act.wait_ge(*at(X, "kt_done", b * X.NT + i))
                            act.activation(KTh[:, :, bass.ts(i - 1, P)], bank(6 + p).rearrange("p (k n) -> p k n", k=KT), ACT.Copy).then_inc(xc["kh_ready"], 1)
                    tile_steps(act, X.NT, step)

                    def copy(hn, q, first):
                        act.wait_ge(*at(X, "pt_done", hn * X.NQ + q + 1))
                        if not first:
                            act.wait_ge(*at(X, "av_done", hn * X.NQ if q == 0 and X.NQ == 5 else (hn - 1) * X.NQ + q + 1))
                        act.activation(PT[:, q, :], bank(X.turned_bank(q)), ACT.Copy).then_inc(xc["ev_a"], 1)

                    def head(g, u, first):
                        hn = b * X.H + g * X.hpg + u
                        if not first:
                            for q in X.by_act:
                                copy(hn - 1, q, isinstance(g, int) and g == 0 and u == 1)
                        p = u % 2
                        act.wait_ge(*at(X, "nb_ready", hn + 1))
                        act.activation(SMv[:, p, 0:X.keys], SMv[:, p, 0:X.keys], ACT.Exp, scale=scale, bias=nb[:, p:p + 1],
                                       accum_out=rs[:, p:p + 1]).then_inc(xc["exp_done"], 1)
                    head_steps(act, X.hpg, head)
                    for n, q in enumerate(X.by_act):
                        copy(b * X.H + X.H - 1, q, False)
                        if n == 0 and X.layer == 0 and not is_last:
                            load_mask(b + 1)
                            deviate((b + 1) * CT, 0)
                            deviate((b + 1) * CT + 1, 1)
                    if not is_last:
                        high(b + 1)
                batch_steps(act, lead, entry)
            attend(X0, s, 8.0, queries)

            def project_out(s, bank0=0):
                for b in (0, 2):
                    act.wait_ge(s["aot_pe"], b + 1)
                    act.activation(zT[:, :, b, 1:N + 1], bank(bank0 + b).rearrange("p (k n) -> p k n", k=KT), ACT.Copy).then_inc(s["aot_ready"], 1)
            project_out(s)

            def layer_norm(u, bank0=0, ahead=lambda b: None, between=None):
                def turned(b):
                    act.wait_ge(ln["zt_pe"], u * B + b + 1)
                    act.activation(zT[:, :, b, 1:N + 1], bank(bank0 + b).rearrange("p (k n) -> p k n", k=KT), ACT.Copy).then_inc(ln["zt"], 1)
                for b in range(B):
                    if b == B - 1 and not between:
                        turned(0)
                    ahead(b)
                    act.wait_ge(ln["v"], u * B + b + 1)
                    act.activation(sd[:, b:b + 1], mv[:, b, 1:2], ACT.Sqrt, bias=eps[:, :]).then_inc(ln["sd"], 1)
                if between:
                    between()
                for b in range(0 if between else 1, B):
                    turned(b)

            def self_attention(layer):
                def own(name, v):
                    return ms[name], v + layer * per[name]

                def out_of_bank(j):
                    act.wait_ge(*own("qkv_pe", j + 1))
                    act.activation(qkv[:, j // 3, (j % 3) * D:(j % 3 + 1) * D], bank((4 + j) % 8), ACT.Copy).then_inc(ms["qkv_out"], 1)

                def turned(b):
                    for w, (dst, done) in enumerate(((QT, "qt_out"), (KTm, "kt_out"))):
                        act.wait_ge(*own("qkt_pe", 2 * b + w + 1))
                        act.activation(dst[:, :, b * N:(b + 1) * N], bank(2 * b + w).rearrange("p (k n) -> p k n", k=KT), ACT.Copy).then_inc(ms[done], 1)

                def masked_queries(b):
                    act.wait_ge(*own("qt_out", b + 1))
                    if b >= 2:
                        act.wait_ge(*own("s_pe", b - 1))
                    Qm4 = Qm[:, b % 2].rearrange("p (g j) n -> p g j n", g=GROUPS)
                    for j in range(HEADS // GROUPS):
                        i = act.activation(Qm4[:, :, j, :], QT[:, :, b * N:(b + 1) * N], ACT.Copy, scale=rmask[4][:, j:j + 1])
                    i.then_inc(ms["qm"], 1)
                for b in range(B):
                    if b == B - 1:
                        turned(0)
                        masked_queries(0)
                    if layer == 1:
                        out_of_bank(3 * b)
                        out_of_bank(3 * b + 1)
                    act.wait_ge(*own("qkv_out", 3 * b + 2))
                    if b:
                        act.wait_ge(*own("ss", b))
                    act.activation(hsq[:, :], qkv[:, b, 0:2 * D], ACT.Square).then_inc(ms["sq"], 1)
                    act.wait_ge(*own("ss", b + 1))
                    act.activation(hrs[:, b, :], hss[:, b, :], ACT.Sqrt).then_inc(ms["nm"], 1)
                    if layer == 1:
                        out_of_bank(3 * b + 2)
                for b in range(1, B):
                    turned(b)
                for b in range(B):
                    if b + 1 < B:
                        masked_queries(b + 1)
                    act.wait_ge(*own("s_out", b + 1))
                    act.activation(Pm[:, :], Pm[:, :], ACT.Exp, bias=float(layer)).then_inc(ms["e_out"], 1)
                    for q in range(4):
                        act.wait_ge(*own("pt_pe", 4 * b + q + 1))
                        if b:
                            act.wait_ge(*own("av_pe", b))
                        act.activation(PTm[:, q * 512:(q + 1) * 512], bank(4 + q % 2), ACT.Copy).then_inc(ms["pt_out"], 1)
                if layer == 0:
                    for j in range(3 * KT):
                        act.wait_ge(fs["wt_pe"], j + 1)
                        act.activation(wffT[:, j // KT, j % KT, :], bank(j % 4), ACT.Copy).then_inc(fs["wt"], 1)
                else:
                    for j in range(KT):
                        act.wait_ge(ws["p_tr"], j + 1)
                        act.activation(Wp[:, j, :], bank(j), ACT.Copy).then_inc(ws["p"], 1)
                for b in (0, 2):
                    act.wait_ge(*own("aot_pe", b + 1))
                    act.activation(zT[:, :, b, 1:N + 1], bank(4 + b).rearrange("p (k n) -> p k n", k=KT), ACT.Copy).then_inc(ms["aot_a"], 1)


            def output_deviation(b):
                act.wait_ge(s["y_v"], b + 1)
                act.activation(y_sd[:, b:b + 1], y_mv[:, b, 1:2], ACT.Sqrt, bias=eps[:, :]).then_inc(s["y_sd"], 1)
            layer_norm(0, 0, output_deviation)
            self_attention(0)
            layer_norm(1, 4)
            act.wait_ge(fs["om"], 1)
            act.wait_ge(ln["zt"], 2 * B)
            for n, dst in enumerate((xr, xk)):
                for k in range(KT):
                    act.activation(dst[:, k, :].rearrange("p (b n) -> p b n", b=B), zT[:, k, :, 0:N], ACT.Copy, scale=omu[:, n, k:k + 1]).then_inc(fs["prev"], 1)
            for b in range(B):
                act.wait_ge(fs["r_pe"], b + 1)
                act.activation(rgate[:, b, :], bank(b), ACT.Sigmoid).then_inc(fs["r_out"], 1)
            for n in range(KT):
                act.wait_ge(fs["k_pe"], n + 1)
                act.activation(kact[:, n, :], bank(4 + n), ACT.Relu).then_inc(fs["k_relu"], 1)
            s = xs[1]

            def weight(j):
                w, k = j // KT, j % KT
                if j == 2 * KT:
                    act.wait_ge(spill, 16)
                act.wait_ge(s["w_tr"], j + 1)
                act.activation((wqT, WVh, WKh)[w][:, k, :], bank(4 + k), ACT.Copy).then_inc(s["w_hi"], 1)
            layer_norm(2)
            for j in range(2 * KT):
                weight(j)
            for n in range(KT):
                act.wait_ge(s["qt_pe"], n + 1)
                act.activation(QT[:, n, :], bank(n), ACT.Copy).then_inc(s["qt_ready"], 1)
                weight(2 * KT + n)
            attend(X1, s, HD ** -0.5)
            act.wait_ge(*at(X1, "av_done", B * X1.H * X1.NQ))
            for k in range(KT):
                act.wait_ge(s["wo_tr"], k + 1)
                act.activation(wqT[:, k, :], bank(k), ACT.Copy).then_inc(s["wo_a"], 1)
            project_out(s, 4)

            def weights():
                for j in range(3 * KT):
                    w, k = j // KT, j % KT
                    act.wait_ge(ws["tr"], j + 1)
                    act.activation(WqkvT[:, k, w * D:(w + 1) * D], bank(4 + k), ACT.Copy).then_inc(ws["a"], 1)
                act.wait_ge(es["b_pe"], 1)
                act.activation(gwT[:, :, :], ps[:, 7, 0:KT * E].rearrange("p (k e) -> p k e", k=KT), ACT.Copy).then_inc(es["g_t"], 1)
                act.activation(b1T[:, :], ps[:, 7, P:2 * P], ACT.Copy).then_inc(es["g_t"], 1)
            layer_norm(3, between=weights)
            self_attention(1)
            layer_norm(4, 4)
            act.wait_ge(ln["z"], 5 * B)
            act.activation(zmh[:, :, :], z[:, :, :], ACT.Copy).then_inc(es["zh"], 1)
            act.wait_ge(es["ex_in"], 1)
            act.activation(ex[:, :, :], ex[:, :, :], ACT.Exp).then_inc(es["ex_out"], 1)
            act.wait_ge(es["table"], 1)
            blocks = act.value_load(tab[0:1, TMAX:TMAX + 1], min_val=1, max_val=TMAX)
            act.wait_ge(es["gather"], 1)
            act.activation(xeT[:, :, :], bank(0).rearrange("p (k n) -> p k n", k=KT), ACT.Copy).then_inc(es["xe"], 1)
            with act.Fori(0, blocks) as t:
                e = act.value_load(tab[0:1, bass.ds(t, 1)], min_val=0, max_val=E - 1)
                for c in range(CH):
                    act.wait_ge(es["up"], t * CH + c + 1)
                    for f in range(KT):
                        act.activation(hT[:, c % 2, f, :], ps[:, 2 + c % 2, f * P:(f + 1) * P], ACT.Relu,
                                       bias=b1T[:, bass.ds(e * FT + (c * KT + f), 1)]).then_inc(es["h"], 1)
                act.wait_ge(es["y_out"], t + 2)
                act.activation(yh[:, :], ysb[:, :], ACT.Copy).then_inc(es["yh"], 1)
                act.wait_ge(es["gather"], t + 2)
                act.activation(xeT[:, :, :], bank(0).rearrange("p (k n) -> p k n", k=KT), ACT.Copy).then_inc(es["xe"], 1)

        @block.vector
        def _(dve):
            def moments(s, src, base):
                for b in range(B):
                    dve.bn_stats(st[:, b, :], src(b))
                dve.drain()
                for b in range(B):
                    i = dve.bn_aggr(mv[:, b, :], st[:, b, :])
                i.then_inc(s["v"], 1)
                dve.wait_ge(s["sd"], base + 1)
                dve.reciprocal(rstd[:, :], sd[:, :])
                dve.drain()

            def normalise(s, src, dst, base):
                moments(s, src, base)
                for b in range(B):
                    i = dve.tensor_scalar(dst(b), src(b), mv[:, b, 0:1], rstd[:, b:b + 1], ALU.subtract, ALU.mult)
                    yield b, i

            s = xs[0]
            dve.wait_ge(s_c, 10)
            dve.wait_ge(s["x_in"], 16)
            for _b in normalise(s, lambda b: x_st[:, b, :], lambda b: z[:, b, :], 0):
                pass
            dve.drain()
            moments(s, lambda b: z[:, b, :], 1)
            dve.wait_ge(s["p_in"], 6 * 16)
            for b in range(B):
                dve.scalar_tensor_tensor(z[:, b, :], z[:, b, :], mv[:, b, 0:1], lnw2, ALU.subtract, ALU.mult)
            dve.drain()
            for b in range(B):
                dve.scalar_tensor_tensor(z[:, b, :], z[:, b, :], rstd[:, b:b + 1], lnb2, ALU.mult, ALU.add).then_inc(s["ln_z"], 1)
            for b in (1, 3):
                dve.wait_ge(s["zt_pe"], b + 1)
                dve.tensor_copy(zT[:, :, b, 1:N + 1], bank(b).rearrange("p (k n) -> p k n", k=KT)).then_inc(s["zt_ready"], 1)
            dve.wait_ge(s["w_in"], 32)
            dve.wait_ge(s["w_split"], 2)
            dve.tensor_tensor(WKl[:, :, :], kvw[:, :, 0:D], WKh[:, :, :].bitcast(f32), ALU.subtract).then_inc(s["w_split"], 1)
            dve.tensor_tensor(WVl[:, :, :], kvw[:, :, D:2 * D], WVh[:, :, :].bitcast(f32), ALU.subtract).then_inc(s["w_split"], 1)
            def queries():
                dve.tensor_tensor(qsc, qsc, ksc, ALU.mult)
                for b in range(B):
                    dve.wait_ge(s["q_sq"], b + 1)
                    dve.tensor_reduce(ssb[:, b, :], y_st[:, b, :].rearrange("p (h d) -> p h d", h=X0.H), AX.X, ALU.add).then_inc(s["q_ss"], 1)
                    dve.wait_ge(s["q_nm"], b + 1)
                    dve.tensor_scalar(nrm[:, b, :], nrm[:, b, :], 1e-12, None, ALU.max)
                    dve.drain()
                    dve.reciprocal(ssb[:, b, :], nrm[:, b, :])
                    dve.drain()
                    q3 = z[:, b, :].rearrange("p (h d) -> p h d", h=X0.H)
                    dve.tensor_tensor(q3, bank(4 + b).rearrange("p (h d) -> p h d", h=X0.H),
                                      ssb[:, b, :].unsqueeze(2).to_broadcast([P, X0.H, X0.d]), ALU.mult)
                    dve.drain()
                    dve.tensor_tensor(q3, q3, qsc.unsqueeze(1).to_broadcast([P, X0.H, X0.d]), ALU.mult).then_inc(s["q_ready"], 1)
                for b in (1, 3):
                    dve.wait_ge(s["qt_pe"], b + 1)
                    dve.tensor_copy(QT[:, :, b * N:(b + 1) * N], bank(b).rearrange("p (k n) -> p k n", k=KT)).then_inc(s["qt_ready"], 1)

            def attend(X, s, scale, before_tiles=lambda: None):
                dve.memset(pmax[:, 4:5], 0.0).then_inc(xc["ao_done"], 1)

                def stats(load, tile, p):
                    dve.wait_ge(*at(X, f"x_ld{p}", load))
                    dve.bn_stats(xst[:, p, :], xin[p])
                    dve.drain()
                    dve.bn_aggr(xmv[:, p, :], xst[:, p, :]).then_inc(s["st_ready"], 1)

                def norm(tile, p):
                    dve.tensor_scalar(zt[p], xin[p], xmv[:, p, 0:1], xrs[:, p:p + 1], ALU.subtract, ALU.mult).then_inc(s["z_norm"], 1)

                def inverse(tile, p):
                    dve.wait_ge(s["sd_ready"], tile + 1)
                    dve.reciprocal(xrs[:, p:p + 1], xsd[:, p:p + 1])
                    dve.drain()

                def low(bb):
                    dve.wait_ge(*at(X, "zh_ready", bb * X.NT + 1))
                    dve.tensor_tensor(zl[:, 0], bank(0).rearrange("p (k n) -> p k n", k=KT), zh[:, 0].bitcast(f32), ALU.subtract).then_inc(xc["zl_ready"], 1)

                def lead_stats(bb):
                    for p in (0, 1):
                        stats(bb * (CT // 2 * 16) + 16, bb * CT + p, p)

                def lead_norm(bb):
                    for p in (0, 1):
                        inverse(bb * CT + p, p)
                        norm(bb * CT + p, p)

                def lead(bb):
                    if X.layer == 0:
                        lead_stats(bb)
                        lead_norm(bb)
                    before_tiles()
                    low(bb)

                def entry(b, is_last):
                    def masked_queries(g, u):
                        p = u % 2
                        q = QT[:, g, bass.ts(b, N)]
                        row = rmask[X.hpg][:, u:u + 1]
                        dve.tensor_scalar(Qmh[:, p, :], q, row, None, ALU.mult)
                        dve.drain()
                        dve.scalar_tensor_tensor(Qml[:, p, :], q, row, Qmh[:, p, :].bitcast(f32), ALU.mult, ALU.subtract).then_inc(xc["qm_ready"], 1)

                    def step(i, rep):
                        if rep == X.NT:
                            masked_queries(0, 0)
                            masked_queries(0, 1)
                        p = rep % 2
                        if X.layer == 0 and rep + 2 < CT:
                            stats(b * (CT // 2 * 16) + (i - p + 2) * 8 + 16, b * CT + i + 2, p)
                            inverse(b * CT + i + 2, p)
                            dve.wait_ge(*at(X, "t_done", b * CT + i + 1))
                            norm(b * CT + i + 2, p)
                        t = rep + 1
                        if t < X.NT:
                            dve.wait_ge(*at(X, "zh_ready", b * X.NT + i + 2))
                            src = zT[:, :, b, 1:N + 1] if t == CT else bank(t % 2).rearrange("p (k n) -> p k n", k=KT)
                            dve.tensor_tensor(zl[:, t % 2], src, zh[:, t % 2].bitcast(f32), ALU.subtract).then_inc(xc["zl_ready"], 1)
                        if X.layer == 0 and 0 <= rep < X.NT:
                            p = rep % 2
                            dve.wait_ge(s["sq_ready"], b * X.NT + i + 1)
                            dve.tensor_reduce(kss[:, :], ksq.rearrange("p (h d) -> p h d", h=X.H), AX.X, ALU.add).then_inc(s["ss_ready"], 1)
                            dve.wait_ge(s["nm_ready"], b * X.NT + i + 1)
                            dve.tensor_scalar(knm[:, :], knm[:, :], 1e-12, None, ALU.max)
                            dve.drain()
                            dve.reciprocal(krn[:, :], knm[:, :])
                            dve.drain()
                            if rep >= 2:
                                dve.wait_ge(*at(X, "kt_done", b * X.NT + i - 1))
                            dve.tensor_tensor(kn[p].rearrange("p (h d) -> p h d", h=X.H), bank(2 + p).rearrange("p (h d) -> p h d", h=X.H),
                                              krn[:, :].unsqueeze(2).to_broadcast([P, X.H, X.d]), ALU.mult).then_inc(xc["kn_ready"], 1)
                        if 0 <= rep - 1 < X.NT:
                            p = (rep - 1) % 2
                            dve.wait_ge(*at(X, "kh_ready", b * X.NT + i))
                            dve.tensor_tensor(KTl[:, :, bass.ts(i - 1, P)], bank(6 + p).rearrange("p (k n) -> p k n", k=KT),
                                              KTh[:, :, bass.ts(i - 1, P)].bitcast(f32), ALU.subtract).then_inc(xc["kl_ready"], 1)
                        if X.layer == 0 and rep == 13:
                            dve.wait_ge(s["mask_in"], b * 16 + 16)
                            dve.tensor_scalar(mbias[:, 0:S], mask8[:, :], -1.0, -NEG, ALU.add, ALU.mult)
                            dve.memset(mbias[:, S:X.keys], 0.0)
                    tile_steps(dve, X.NT, step)

                    def copy(hn, q, first):
                        w = P * len(X.quad(q))
                        dve.wait_ge(*at(X, "pt_done", hn * X.NQ + q + 1))
                        if q == 4:
                            dve.wait_ge(*at(X, "av_done", hn * X.NQ + 1))
                        elif not first:
                            dve.wait_ge(*at(X, "av_done", (hn - 1) * X.NQ + q + 1))
                        dve.tensor_copy(PT[:, q % 4, 0:w], bank(X.turned_bank(q), w)).then_inc(xc["ev_d"], 1)

                    def output(g, u):
                        h = g * X.hpg + u
                        p = u % 2
                        dve.wait_ge(*at(X, "av_done", (b * X.H + h + 1) * X.NQ))
                        dve.reciprocal(rinv[:, p:p + 1], rs[:, p:p + 1])
                        dve.drain()
                        dve.tensor_scalar(z[:, b, bass.ds(h * X.d, X.d)], ps[:, 7, u * P + u * X.d:u * P + (u + 1) * X.d],
                                          rinv[:, p:p + 1], None, ALU.mult).then_inc(xc["o_done"], 1)

                    def head(g, u, first):
                        hn = b * X.H + g * X.hpg + u
                        p = u % 2
                        second = isinstance(g, int) and g == 0 and u == 1
                        if not (first or second):
                            dve.wait_ge(*at(X, "s_done", hn * 2 - 2))
                            masked_queries(g, u)
                        for k, (lo, hi) in enumerate(X.halves):
                            if k == 1 and X.NQ == 5 and not first:
                                copy(hn - 1, 1, second)
                            dve.wait_ge(*at(X, "s_done", hn * 2 + k + 1))
                            if k == 0 and not (first or second):
                                dve.wait_ge(*at(X, "pt_done", (hn - 1) * X.NQ))
                            src = ps[:, lo // 512:5, :].rearrange("p k n -> p (k n)")[:, 0:hi - lo]
                            m = pmax[:, 2 * p + k:2 * p + k + 1]
                            dve.memset(pmax[:, 4 + 2 * p + k:5 + 2 * p + k], 0.0)
                            if X.layer == 0:
                                dve.tensor_tensor_reduce(out=SMv[:, p, lo:hi], in0=src, in1=mbias[:, lo:hi], scale=1.0, scalar=-3.0e38,
                                                         op0=ALU.add, op1=ALU.max, accum_out=m).then_inc(xc["s_taken"], 1)
                            else:
                                dve.tensor_scalar(SMv[:, p, lo:hi], src, 1.0, None, ALU.mult, ALU.max, accum_out=m).then_inc(xc["s_taken"], 1)
                            if k == 0 and not (first or second):
                                output(*((g, u - 2) if u >= 2 else (g - 1, X.hpg + u - 2)))
                        dve.drain()
                        dve.tensor_scalar(nb[:, p:p + 1], pmax[:, 2 * p:2 * p + 1], pmax[:, 2 * p + 1:2 * p + 2], -scale, ALU.max, ALU.mult).then_inc(xc["nb_ready"], 1)
                        if not first:
                            for q in X.by_dve:
                                if q > 1 or X.NQ == 4:
                                    copy(hn - 1, q, second)
                    head_steps(dve, X.hpg, head)
                    output(GROUPS - 1, X.hpg - 2)
                    if X.layer == 0 and not is_last:
                        lead_stats(b + 1)
                    for n, q in enumerate(X.by_dve):
                        copy(b * X.H + X.H - 1, q, False)
                        if n == 0 and X.layer == 0 and not is_last:
                            lead_norm(b + 1)
                    if not is_last:
                        low(b + 1)
                    output(GROUPS - 1, X.hpg - 1)
                    dve.memset(pmax[:, 4:5], 0.0).then_inc(xc["ao_done"], 1)
                batch_steps(dve, lead, entry)
            attend(X0, s, 8.0, queries)

            def project_out(s, bank0=0):
                for b in (1, 3):
                    dve.wait_ge(s["aot_pe"], b + 1)
                    dve.tensor_copy(zT[:, :, b, 1:N + 1], bank(bank0 + b).rearrange("p (k n) -> p k n", k=KT)).then_inc(s["aot_ready"], 1)
            project_out(s)
            dve.wait_ge(s["res"], B)

            def residual_norm(u, update):
                for b in range(B):
                    update(b)
                    dve.drain()
                    dve.bn_stats(st[:, b, :], x[:, b, :])
                    dve.drain()
                    dve.bn_aggr(mv[:, b, :], st[:, b, :]).then_inc(ln["v"], 1)
                    dve.wait_ge(ln["sd"], u * B + b + 1)
                    dve.reciprocal(rstd[:, b:b + 1], sd[:, b:b + 1])
                    dve.drain()
                    dve.tensor_scalar(z[:, b, :], x[:, b, :], mv[:, b, 0:1], rstd[:, b:b + 1], ALU.subtract, ALU.mult).then_inc(ln["z"], 1)

            def heads(t, h):
                return t.rearrange("p (h d) -> p h d", h=h)

            def self_attention(layer, eps_, shift):
                def own(name, v):
                    return ms[name], v + layer * per[name]
                scale = HD ** -0.5
                dve.wait_ge(mi[layer]["p_in"], (4 if layer == 0 else 3) * 16)
                if layer == 0:
                    dve.tensor_tensor(gains[:, 0, :], gains[:, 0, :], gains[:, 1, :], ALU.mult)
                else:
                    for half in (0, 1):
                        g = gains[:, 0, half * (HD // 2):(half + 1) * (HD // 2)]
                        dve.tensor_tensor(rope_g[:, 0, half, :], g, rope_t[:, 0, :], ALU.mult)
                        dve.tensor_tensor(rope_g[:, 1, 1 - half, :], g, rope_t[:, 2 - half, :], ALU.mult)

                def add_bias(j):
                    dve.wait_ge(*own("qkv_pe", j + 1))
                    cols = slice((j % 3) * D, (j % 3 + 1) * D)
                    dve.tensor_tensor(qkv[:, j // 3, cols], bank((4 + j) % 8), bqkv[:, cols], ALU.add).then_inc(ms["qkv_out"], 1)
                for b in range(B):
                    if layer == 0:
                        add_bias(3 * b)
                        add_bias(3 * b + 1)
                    dve.wait_ge(*own("sq", b + 1))
                    dve.tensor_reduce(hss[:, b, :], heads(hsq[:, :], 2 * HEADS), AX.X, ALU.add)
                    dve.drain()
                    dve.tensor_scalar(hss[:, b, :], hss[:, b, :], 1.0 / HD, eps_, ALU.mult, ALU.add).then_inc(ms["ss"], 1)
                    if layer == 0:
                        add_bias(3 * b + 2)
                    dve.wait_ge(*own("nm", b + 1))
                    dve.reciprocal(hss[:, b, :], hrs[:, b, :])
                    dve.drain()
                    t = qkv[:, b, 0:2 * D]
                    dve.tensor_tensor(heads(t, 2 * HEADS), heads(t, 2 * HEADS), hss[:, b, :].unsqueeze(2).to_broadcast([P, 2 * HEADS, HD]), ALU.mult)
                    dve.drain()
                    if layer == 0:
                        t = qkv[:, b, 0:D]
                        i = dve.tensor_tensor(heads(t, HEADS), heads(t, HEADS), gains[:, 0, :].unsqueeze(1).to_broadcast([P, HEADS, HD]), ALU.mult)
                    else:
                        u = t.rearrange("p (h a d) -> p h a d", h=2 * HEADS, a=2)
                        v = hrot[:, :].rearrange("p (h a d) -> p h a d", h=2 * HEADS, a=2)
                        for half in (0, 1):
                            dve.tensor_tensor(v[:, :, half, :], u[:, :, 1 - half, :], rope_g[:, 1, half, :].unsqueeze(1).to_broadcast([P, 2 * HEADS, HD // 2]), ALU.mult)
                        dve.drain()
                        dve.tensor_tensor(heads(t, 2 * HEADS), heads(t, 2 * HEADS),
                                          rope_g[:, 0].rearrange("p a d -> p (a d)").unsqueeze(1).to_broadcast([P, 2 * HEADS, HD]), ALU.mult)
                        dve.drain()
                        i = dve.tensor_tensor(t, t, hrot[:, :], ALU.add)
                    i.then_inc(ms["qk_ready"], 1)
                S3 = ps[:, 0:4, :].rearrange("p k n -> p (k n)").rearrange("p (h n) -> p h n", h=HEADS)
                P3 = Pm[:, :].rearrange("p (h n) -> p h n", h=HEADS)

                def shifted(b):
                    dve.wait_ge(*own("s_pe", b + 1))
                    dve.tensor_reduce(mx[:, :], S3, AX.X, ALU.max)
                    dve.drain()
                    dve.tensor_scalar(mx[:, :], mx[:, :], scale, shift, ALU.mult, ALU.add)
                    dve.drain()
                    if b:
                        dve.wait_ge(*own("pt_pe", 4 * b))
                    dve.scalar_tensor_tensor(P3, S3, scale, mx[:, :].unsqueeze(2).to_broadcast([P, HEADS, N]), ALU.mult, ALU.subtract).then_inc(ms["s_out"], 1)
                shifted(0)
                for b in range(B):
                    dve.wait_ge(*own("e_out", b + 1))
                    total = hsum[:, b % 2, :]
                    dve.tensor_reduce(total, P3, AX.X, ALU.add)
                    if b + 1 < B:
                        shifted(b + 1)
                    dve.drain()
                    dve.reciprocal(total, total)
                    dve.drain()
                    dve.wait_ge(*own("av_pe", b + 1))
                    for w in (0, 1):
                        own_cols = ps[:, 6:8, :].rearrange("p k n -> p (k n)").rearrange("p (g u v d) -> p g u v d", u=2, v=2, d=HD)[:, :, w, w, :]
                        i = dve.tensor_tensor(z[:, b, :].rearrange("p (g u d) -> p g u d", u=2, d=HD)[:, :, w, :], own_cols,
                                              total.rearrange("p (g u) -> p g u", u=2)[:, :, w].unsqueeze(2).to_broadcast([P, HEADS // 2, HD]), ALU.mult)
                    i.then_inc(ms["ao"], 1)
                for b in (1, 3):
                    dve.wait_ge(*own("aot_pe", b + 1))
                    dve.tensor_copy(zT[:, :, b, 1:N + 1], bank(4 + b).rearrange("p (k n) -> p k n", k=KT)).then_inc(ms["aot_d"], 1)

            def attended(layer):
                def update(b):
                    if layer == 0 and b == 0:
                        dve.wait_ge(ms["x_bias"], B)
                    dve.wait_ge(ms["y_pe"], layer * per["y_pe"] + b + 1)
                    dve.tensor_tensor(x[:, b, :], x[:, b, :], bank(b), ALU.add).then_inc(ms["x_att"], 1)
                return update

            def first_sum(b):
                dve.wait_ge(s["y_pe"], b + 1)
                dve.bn_stats(st[:, b, :], bank(4 + b))
                dve.drain()
                dve.bn_aggr(y_mv[:, b, :], st[:, b, :]).then_inc(s["y_v"], 1)
                dve.wait_ge(s["y_sd"], b + 1)
                dve.reciprocal(y_rstd[:, b:b + 1], y_sd[:, b:b + 1])
                dve.scalar_tensor_tensor(y_st[:, b, :], bank(4 + b), y_mv[:, b, 0:1], lnw[:, :], ALU.subtract, ALU.mult)
                dve.drain()
                dve.scalar_tensor_tensor(x[:, b, :], y_st[:, b, :], y_rstd[:, b:b + 1], x[:, b, :], ALU.mult, ALU.add).then_inc(s["x_done"], 1)
            residual_norm(0, first_sum)
            self_attention(0, 1e-6, 0.0)
            dve.wait_ge(fs["w_in"], 80)
            dve.tensor_scalar(omu[:, :, :], mu[:, :, :], -1.0, 1.0, ALU.mult, ALU.add).then_inc(fs["om"], 1)
            residual_norm(1, attended(0))
            for n, dst in enumerate((xr, xk)):
                for k in range(KT):
                    to = dst[:, k, :].rearrange("p (b n) -> p b n", b=B)
                    dve.wait_ge(fs["prev"], n * KT + k + 1)
                    dve.scalar_tensor_tensor(to, zT[:, k, :, 1:N + 1], mu[:, n, k:k + 1], to, ALU.mult, ALU.add).then_inc(fs["mix"], 1)
            for n in range(KT):
                dve.wait_ge(fs["k_relu"], n + 1)
                dve.tensor_tensor(kact[:, n, :], kact[:, n, :], kact[:, n, :], ALU.mult).then_inc(fs["k_out"], 1)
            dve.wait_ge(fs["r_out"], B)

            def gated(b):
                dve.wait_ge(fs["v_pe"], b + 1)
                dve.tensor_tensor(rgate[:, b, :], rgate[:, b, :], bank(b), ALU.mult)
                dve.drain()
                dve.tensor_tensor(x[:, b, :], x[:, b, :], rgate[:, b, :], ALU.add).then_inc(fs["x_ff"], 1)
            residual_norm(2, gated)
            s = xs[1]
            for j in range(KT, 3 * KT):
                w, k = j // KT, j % KT
                hi, lo = ((WVh, WVl), (WKh, WKl))[w - 1]
                dve.wait_ge(s["w_hi"], j + 1)
                dve.tensor_tensor(lo[:, k, :], bank(4 + k), hi[:, k, :].bitcast(f32), ALU.subtract).then_inc(s["w_split"], 1)
            attend(X1, s, HD ** -0.5)
            project_out(s, 4)
            dve.wait_ge(s["wo_in"], 32)

            def second_sum(b):
                dve.wait_ge(s["y_pe"], b + 1)
                dve.tensor_tensor(x[:, b, :], bank(b), x[:, b, :], ALU.add).then_inc(s["x_done"], 1)
            residual_norm(3, second_sum)
            self_attention(1, 1e-5, 1.0)
            residual_norm(4, attended(1))
            dve.memset(oh[:, B, :], 0.0)
            dve.wait_ge(es["zh"], 1)
            dve.tensor_tensor(zml[:, :, :], z[:, :, :], zmh[:, :, :].bitcast(f32), ALU.subtract).then_inc(es["zl"], 1)
            dve.wait_ge(es["c"], 6)
            dve.wait_ge(es["logits"], 1)
            dve.tensor_copy(lg[:, :, :], ps[:, 4, 0:B * E].rearrange("p (b e) -> p b e", b=B))
            dve.drain()

            def wide(v):
                return v.unsqueeze(2).to_broadcast([P, B, E])

            def over(v):
                return v.unsqueeze(1).to_broadcast([P, B, E])
            dve.tensor_reduce(lm[:, :], lg[:, :, :], AX.X, ALU.max)
            dve.drain()
            dve.tensor_tensor(ex[:, :, :], lg[:, :, :], wide(lm[:, :]), ALU.subtract).then_inc(es["ex_in"], 1)
            dve.tensor_tensor(cand[:, :, :], lg[:, :, :], wide(lm[:, :]), ALU.is_equal)
            dve.drain()
            dve.tensor_tensor(cand[:, :, :], cand[:, :, :], over(order[:, :]), ALU.mult)
            dve.drain()
            dve.tensor_reduce(lm[:, :], cand[:, :, :], AX.X, ALU.max)
            dve.drain()
            dve.tensor_tensor(oh[:, 0:B, :], cand[:, :, :], wide(lm[:, :]), ALU.is_equal).then_inc(es["oh"], 1)
            dve.wait_ge(es["ex_out"], 1)
            dve.tensor_reduce(gate[:, :], ex[:, :, :], AX.X, ALU.add)
            dve.drain()
            dve.reciprocal(gate[:, :], gate[:, :]).then_inc(es["y_out"], 1)
            dve.wait_ge(es["ranks"], 1)
            count = ps[:, 6, B * E:(B + 1) * E]
            dve.tensor_scalar(nblk[:, :], count, 0.0, None, ALU.is_gt)
            for j in range(1, T // P):
                dve.drain()
                dve.tensor_scalar(cmp8[:, :], count, float(j * P), None, ALU.is_gt)
                dve.drain()
                dve.tensor_tensor(nblk[:, :], nblk[:, :], cmp8[:, :], ALU.add)
            dve.drain()
            dve.tensor_copy(last[:, :], nblk[:, :])
            for j in range(1, E):
                dve.drain()
                dve.tensor_tensor(last[:, j:j + 1], last[:, j:j + 1], last[:, j - 1:j], ALU.add)
            dve.drain()
            dve.tensor_tensor(first[:, :], last[:, :], nblk[:, :], ALU.subtract)
            dve.tensor_tensor(cmpt[:, :, :], last[:, :].unsqueeze(1).to_broadcast([P, TMAX, E]), turns[:, :].unsqueeze(2).to_broadcast([P, TMAX, E]), ALU.is_le)
            dve.drain()
            dve.tensor_reduce(tabf[:, 0:TMAX], cmpt[:, :, :], AX.X, ALU.add)
            dve.tensor_scalar(first[:, :], first[:, :], float(P), None, ALU.mult)
            dve.tensor_copy(tabf[:, TMAX:TMAX + 1], last[:, E - 1:E])
            dve.drain()
            dve.tensor_scalar(tabf[:, 0:TMAX], tabf[:, 0:TMAX], float(E - 1), None, ALU.min)
            dve.drain()
            dve.tensor_copy(tab[:, :], tabf[:, :]).then_inc(es["table"], 1)
            dve.tensor_tensor(cand[:, :, :], ps[:, 6, 0:B * E].rearrange("p (b e) -> p b e", b=B), over(first[:, :]), ALU.add)
            dve.drain()
            dve.tensor_tensor(cand[:, :, :], cand[:, :, :], oh[:, 0:B, :], ALU.mult)
            dve.drain()
            dve.tensor_reduce(pos[:, :], cand[:, :, :], AX.X, ALU.add)
            dve.drain()
            dve.wait_ge(es["table"], 1)
            blocks = dve.value_load(tab[0:1, TMAX:TMAX + 1], min_val=1, max_val=TMAX)

            def dispatch():
                for b in range(B):
                    i = dve.tensor_scalar(Dm[:, b, :], slots[:, :], pos[:, b:b + 1], None, ALU.is_equal)
                i.then_inc(es["dm"], 1)
                dve.drain()
                dve.tensor_scalar(pos[:, :], pos[:, :], -float(P), None, ALU.add)
                dve.drain()
            dispatch()
            with dve.Fori(0, blocks) as t:
                dve.wait_ge(es["dt_pe"], t + 1)
                dve.tensor_copy(DT[:, :, :], bank(1).rearrange("p (b n) -> p b n", b=B)).then_inc(es["dt"], 1)
                dispatch()
                dve.wait_ge(es["ring_free"], t * CH + 2 * CH)
                dve.wait_ge(es["b2_in"], t * 16 + 16)
                dve.tensor_tensor(ysb[:, :], bank(4), b2r[:, :], ALU.add).then_inc(es["y_out"], 1)
                dve.wait_ge(es["yh"], t + 1)
                dve.tensor_tensor(yl[:, :], ysb[:, :], yh[:, :].bitcast(f32), ALU.subtract).then_inc(es["yl"], 1)
                for b in range(B):
                    dve.wait_ge(es["mixed"], t * B + b + 1)
                    dve.scalar_tensor_tensor(x[:, b, :], bank(5 + b % 3), gate[:, b:b + 1], x[:, b, :], ALU.mult, ALU.add).then_inc(es["x_moe"], 1)

        @block.tensor
        def _(pe):
            def transpose4(dst, src):
                for k in range(KT):
                    i = pe.transpose(dst[:, k * P:(k + 1) * P], src[:, k * P:(k + 1) * P], ident[:, :])
                return i

            def product(dst, lhs, rhs):
                for k in range(KT):
                    i = pe.matmul(dst, lhs(k), rhs(k), start=(k == 0), stop=(k == KT - 1))
                return i

            s = xs[0]
            pe.wait_ge(s_c, 10)
            for b in range(B):
                pe.wait_ge(s["ln_z"], b + 1)
                transpose4(bank(b), z[:, b, :]).then_inc(s["zt_pe"], 1)
            pe.wait_ge(s["w_in"], 32)
            pe.wait_ge(s["zt_ready"], B)
            for b in range(B):
                product(bank(4 + b), lambda k: zT[:, k, b, 1:N + 1], lambda k: wq_st[:, k, :]).then_inc(s["q_pe"], 1)
            for b in range(B):
                pe.wait_ge(s["q_ready"], b + 1)
                transpose4(bank(b), z[:, b, :]).then_inc(s["qt_pe"], 1)

            def attend(X, s):
                pe.wait_ge(s["w_split"], X.splits)
                pe.wait_ge(s["qt_ready"], B)

                def lead(bb):
                    if X.layer == 0:
                        pe.wait_ge(s["z_ready"], (bb * CT + 1) * 2)
                    else:
                        pe.wait_ge(*at(X, "x_ld0", bb * (CT // 2 * 16) + 16))
                    transpose4(bank(0), (zt if X.layer == 0 else xin)[0]).then_inc(xc["t_done"], 1)

                def entry(b, is_last):
                    def step(i, rep):
                        t = rep + 1
                        if t < CT:
                            if X.layer == 0:
                                pe.wait_ge(s["z_ready"], (b * CT + i + 2) * 2)
                                src = zt[t % 2]
                            else:
                                pe.wait_ge(*at(X, f"x_ld{t % 2}", b * (CT // 2 * 16) + (i + 1 - t % 2) * 8 + 16))
                                src = xin[t % 2]
                            if t >= 2:
                                pe.wait_ge(*at(X, "zl_ready", b * X.NT + i))
                            transpose4(bank(t % 2), src).then_inc(xc["t_done"], 1)
                        if 0 <= rep < X.NT:
                            p = rep % 2
                            n = b * X.NT + i
                            pe.wait_ge(*at(X, "zl_ready", n + 1))
                            if rep >= 2:
                                pe.wait_ge(*at(X, "kn_ready", n - 1))
                            for k in range(KT):
                                pe.matmul(bank(2 + p), zh[:, p, k, :], WKh[:, k, :], start=(k == 0), stop=False)
                                pe.matmul(bank(2 + p), zh[:, p, k, :], WKl[:, k, :], start=False, stop=False)
                                m = pe.matmul(bank(2 + p), zl[:, p, k, :], WKh[:, k, :], start=False, stop=(k == KT - 1))
                            m.then_inc(xc["k_done"], 1)
                            if rep >= 2:
                                pe.wait_ge(*at(X, "v_ready", n - 1))
                            for k in range(KT):
                                pe.matmul(bank(4 + p), zh[:, p, k, :], WVh[:, k, :], start=(k == 0), stop=False)
                                pe.matmul(bank(4 + p), zh[:, p, k, :], WVl[:, k, :], start=False, stop=False)
                                m = pe.matmul(bank(4 + p), zl[:, p, k, :], WVh[:, k, :], start=False, stop=(k == KT - 1))
                            m.then_inc(xc["v_done"], 1)
                        if 0 <= rep - 1 < X.NT:
                            p = (rep - 1) % 2
                            pe.wait_ge(*at(X, "kn_ready", b * X.NT + i))
                            if rep - 1 >= 2:
                                pe.wait_ge(*at(X, "kl_ready", b * X.NT + i - 2))
                            if rep == 2:
                                pe.wait_ge(*at(X, "ao_done", b + 1))
                            transpose4(bank(6 + p), kn[p]).then_inc(xc["kt_done"], 1)
                    tile_steps(pe, X.NT, step)

                    def copied(hn, q):
                        if q in X.by_act:
                            pe.wait_ge(*at(X, "ev_a", hn * X.nA + X.by_act.index(q) + 1))
                        else:
                            pe.wait_ge(*at(X, "ev_d", hn * X.nD + X.by_dve.index(q) + 1))

                    def turn(h, u, q, first):
                        hn = b * X.H + h
                        if q == 0:
                            pe.wait_ge(*at(X, "exp_done", hn + 1))
                        back, r = X.before(q)
                        if not (first and back):
                            copied(hn - back, r)
                        for n, kt in enumerate(X.quad(q)):
                            i = pe.transpose(ps[:, X.turned_bank(q), n * P:(n + 1) * P], SMv[:, u % 2, kt * P:(kt + 1) * P], ident[:, :])
                        i.then_inc(xc["pt_done"], 1)

                    def add(g, u, q, first):
                        hn = b * X.H + g * X.hpg + u
                        if q == 0 and first:
                            pe.wait_ge(*at(X, "v_ready", (b + 1) * X.NT))
                        elif q == 0:
                            pe.wait_ge(*at(X, "o_done", hn))
                        copied(hn, q)
                        for n, kt in enumerate(X.quad(q)):
                            i = pe.matmul(bank(7)[:, u * P:(u + 1) * P], PT[:, q % 4, n * P:(n + 1) * P], Vt[:, kt, bass.ds(g * P, P)],
                                          start=(kt == 0), stop=(kt == X.NT - 1))
                        i.then_inc(xc["av_done"], 1)

                    def score(g, u, c, first):
                        hn = b * X.H + g * X.hpg + u
                        p = u % 2
                        k = c // 2 if c < 4 else 1
                        if c == 0:
                            pe.wait_ge(*at(X, "qm_ready", hn + 1))
                        if c in (0, 2) and not first:
                            pe.wait_ge(*at(X, "s_taken", hn * 2 - 1 + k))
                        if c == 2 and first:
                            pe.wait_ge(*at(X, "kl_ready", (b + 1) * X.NT))
                        lo = c * 512
                        w = min(512, X.keys - lo)
                        o = bank(c, w)
                        pe.matmul(o, Qmh[:, p, :], KTh[:, g, lo:lo + w], start=True, stop=False)
                        pe.matmul(o, Qmh[:, p, :], KTl[:, g, lo:lo + w], start=False, stop=False)
                        i = pe.matmul(o, Qml[:, p, :], KTh[:, g, lo:lo + w], start=False, stop=True)
                        if c == 1 or lo + w == X.keys:
                            i.then_inc(xc["s_done"], 1)

                    plan = ("S0 S1 T0 S2 T1 S3 T2 A0 T3 A1 A2 A3" if X.NQ == 4 else "S0 S1 T0 S2 T1 S3 S4 T2 A0 T3 A1 T4 A2 A3 A4").split()

                    def head(g, u, first):
                        gg, uu = (g, u - 1) if u else (g - 1, X.hpg - 1)
                        second = isinstance(g, int) and g == 0 and u == 1
                        for what, q in sorted(plan, key=lambda w: w[0] != "S") if second else plan:
                            q = int(q)
                            if what == "S":
                                score(g, u, q, first)
                            elif first:
                                continue
                            elif what == "T":
                                turn(gg * X.hpg + uu, uu, q, second)
                            else:
                                add(gg, uu, q, second)
                    head_steps(pe, X.hpg, head)
                    for what, q in plan:
                        if what == "T":
                            turn(X.H - 1, X.hpg - 1, int(q), False)
                        elif what == "A":
                            add(GROUPS - 1, X.hpg - 1, int(q), False)
                    if not is_last:
                        lead(b + 1)
                batch_steps(pe, lead, entry)
            attend(X0, s)

            def project_out(s, wo):
                for b in range(B):
                    pe.wait_ge(*at(X0, "ao_done", B + 1))
                    transpose4(bank(b), z[:, b, :]).then_inc(s["aot_pe"], 1)
                pe.wait_ge(s["aot_ready"], B)
                for b in range(B):
                    product(bank(4 + b), lambda k: zT[:, k, b, 1:N + 1], lambda k: wo[:, k, :]).then_inc(s["y_pe"], 1)
            pe.wait_ge(s["wo_in"], 64)
            project_out(s, wo_st)

            def norm_turn(u, bs, bank0=0):
                for b in bs:
                    pe.wait_ge(ln["z"], u * B + b + 1)
                    transpose4(bank(bank0 + b), z[:, b, :]).then_inc(ln["zt_pe"], 1)

            def turn_weight(dst, w, k):
                for t in range(KT):
                    i = pe.transpose(dst[:, t * P:(t + 1) * P], w[:, t, k * P:(k + 1) * P], ident[:, :])
                return i

            def tokens(b):
                return lambda k: zT[:, k, b, 1:N + 1]

            def self_attention(layer):
                def own(name, v):
                    return ms[name], v + layer * per[name]
                w_in = Wqkv if layer == 0 else WqkvT
                u = 3 * layer

                def projections(b):
                    pe.wait_ge(ln["zt"], u * B + (b + 1 if b < 2 else B))
                    for j in range(3 * b, 3 * b + 3):
                        if j >= 8:
                            pe.wait_ge(*own("qkv_out", j - 7))
                        cols = slice((j % 3) * D, (j % 3 + 1) * D)
                        product(bank((4 + j) % 8), tokens(b), lambda k: w_in[:, k, cols]).then_inc(ms["qkv_pe"], 1)

                def turn(b):
                    pe.wait_ge(*own("qk_ready", b + 1))
                    pe.wait_ge(*own("qkv_out", 2 * b + 6))
                    transpose4(bank(2 * b), qkv[:, b, 0:D]).then_inc(ms["qkt_pe"], 1)
                    transpose4(bank(2 * b + 1), qkv[:, b, D:2 * D]).then_inc(ms["qkt_pe"], 1)

                def scores(b):
                    pe.wait_ge(*own("qm", b + 1))
                    pe.wait_ge(*own("kt_out", max(b + 1, 2)))
                    if b:
                        pe.wait_ge(*own("s_out", b))
                    for h in range(HEADS):
                        i = pe.matmul(ps[:, h // 4, (h % 4) * N:(h % 4 + 1) * N], Qm[:, b % 2, h, :], KTm[:, h // 4, b * N:(b + 1) * N], start=True, stop=True)
                    i.then_inc(ms["s_pe"], 1)

                norm_turn(u, (0, 1, 2))
                projections(0)
                norm_turn(u, (3,))
                if layer == 1:
                    pe.wait_ge(es["g_t"], 2)
                projections(1)
                projections(2)
                turn(0)
                projections(3)
                turn(1)
                scores(0)
                turn(2)
                turn(3)
                for b in range(B):
                    if b + 1 < B:
                        scores(b + 1)
                    pe.wait_ge(*own("e_out", b + 1))
                    pe.wait_ge(*own("kt_out", B))
                    for q in range(4):
                        n = 4 * b + q
                        if n >= 2:
                            pe.wait_ge(*own("pt_out", n - 1))
                        for j in range(4):
                            h = 4 * q + j
                            i = pe.transpose(ps[:, 4 + n % 2, j * N:(j + 1) * N], Pm[:, h * N:(h + 1) * N], ident[:, :])
                        i.then_inc(ms["pt_pe"], 1)
                    if b:
                        pe.wait_ge(*own("ao", b))
                    for q in range(4):
                        pe.wait_ge(*own("pt_out", 4 * b + q + 1))
                        for j in range(4):
                            h = 4 * q + j
                            pair = 2 * D + h // 2 * 2 * HD
                            i = pe.matmul(ps[:, 6 + h // 8, h % 8 * 2 * HD:(h % 8 + 1) * 2 * HD], PTm[:, h * N:(h + 1) * N], qkv[:, b, pair:pair + 2 * HD],
                                          start=True, stop=True)
                    i.then_inc(ms["av_pe"], 1)
                if layer == 0:
                    pe.wait_ge(fs["w_in"], 80)
                    for j in range(3 * KT):
                        if j >= 4:
                            pe.wait_ge(fs["wt"], j - 3)
                        turn_weight(bank(j % 4), wst[:, j // KT], j % KT).then_inc(fs["wt_pe"], 1)
                else:
                    pe.wait_ge(ws["wp_in"], 16)
                    for k in range(KT):
                        turn_weight(bank(k), wffT[:, 0], k).then_inc(ws["p_tr"], 1)
                for b in range(B):
                    pe.wait_ge(*own("ao", b + 1 if b < 2 else B))
                    transpose4(bank(4 + b), z[:, b, :]).then_inc(ms["aot_pe"], 1)
                if layer == 0:
                    pe.wait_ge(mi[0]["wp_in"], 16)
                    pe.wait_ge(fs["wt"], 3 * KT)
                else:
                    pe.wait_ge(ws["p"], KT)
                for b in range(B):
                    pe.wait_ge(*own("aot_d" if b % 2 else "aot_a", b // 2 + 1))
                    product(bank(b), tokens(b), lambda k: Wp[:, k, :]).then_inc(ms["y_pe"], 1)

            pe.wait_ge(mi[0]["w_in"], 16)
            self_attention(0)
            norm_turn(1, range(B), 4)
            for b in range(B):
                for k in range(KT):
                    if b == 0:
                        pe.wait_ge(fs["mix"], k + 1)
                    i = pe.matmul(bank(b), xr[:, k, b * N:(b + 1) * N], wffT[:, 0, k, :], start=(k == 0), stop=(k == KT - 1))
                i.then_inc(fs["r_pe"], 1)
            pe.wait_ge(fs["mix"], 2 * KT)
            for n in range(KT):
                product(bank(4 + n), lambda k: wffT[:, 1, k, n * P:(n + 1) * P], lambda k: xk[:, k, :]).then_inc(fs["k_pe"], 1)
            pe.wait_ge(fs["r_out"], B)
            pe.wait_ge(fs["k_out"], KT)
            for b in range(B):
                product(bank(b), lambda k: kact[:, k, b * N:(b + 1) * N], lambda k: wffT[:, 2, k, :]).then_inc(fs["v_pe"], 1)

            s = xs[1]
            pe.wait_ge(s["w_in"], 48)

            def weight(j):
                w, k = j // KT, j % KT
                if j >= KT:
                    pe.wait_ge(s["w_hi"], j - 3)
                if j >= 2 * KT:
                    pe.wait_ge(s["w_split"], j - 7)
                turn_weight(bank(4 + k), wst[:, (0, 2, 1)[w]], k).then_inc(s["w_tr"], 1)
            for j in range(KT):
                weight(j)
            norm_turn(2, range(B))
            for j in range(KT, 2 * KT):
                weight(j)
            pe.wait_ge(s["w_hi"], KT)
            pe.wait_ge(ln["zt"], 3 * B)
            for n in range(KT):
                product(bank(n), lambda k: wqT[:, k, n * P:(n + 1) * P], lambda k: zT[:, k, :, 1:N + 1]).then_inc(s["qt_pe"], 1)
                weight(2 * KT + n)
            attend(X1, s)
            pe.wait_ge(s["wo_in"], 32)
            pe.wait_ge(*at(X1, "s_taken", 2 * B * X1.H))
            for k in range(KT):
                turn_weight(bank(k), wo_st, k).then_inc(s["wo_tr"], 1)
            for b in range(B):
                pe.wait_ge(*at(X1, "ao_done", B + 1))
                transpose4(bank(4 + b), z[:, b, :]).then_inc(s["aot_pe"], 1)
            pe.wait_ge(s["aot_ready"], B)
            pe.wait_ge(s["wo_a"], KT)
            for b in range(B):
                product(bank(b), tokens(b), lambda k: wqT[:, k, :]).then_inc(s["y_pe"], 1)
            pe.wait_ge(ws["w_in"], 48)
            for j in range(3 * KT):
                if j >= KT:
                    pe.wait_ge(ws["a"], j - 3)
                turn_weight(bank(4 + j % KT), qkv_st[:, j // KT], j % KT).then_inc(ws["tr"], 1)
            pe.wait_ge(ws["a"], 3 * KT)
            pe.wait_ge(es["g_in"], 32)
            for k in range(KT):
                pe.transpose(ps[:, 7, k * E:(k + 1) * E], gwn[:, k * P:(k + 1) * P], ident[0:E, 0:E])
            pe.transpose(ps[:, 7, P:2 * P], b1n[:, :], ident[:, :]).then_inc(es["b_pe"], 1)
            self_attention(1)

            def logits(b):
                pe.wait_ge(ln["zt"], 4 * B + b + 1)
                return product(ps[:, 4, b * E:(b + 1) * E], tokens(b), lambda k: gwT[:, k, :])
            norm_turn(4, (0, 1, 2), 4)
            logits(0)
            logits(1)
            norm_turn(4, (3,), 4)
            logits(2)
            logits(3).then_inc(es["logits"], 1)
            pe.wait_ge(es["zh"], 1)
            for c in range(CH):
                i = pe.transpose(ps[:, 7, 0:P], ident[:, :], ident[:, :])
                i.then_inc(es["ring_free"], 1)
            pe.wait_ge(es["c"], 6)
            pe.wait_ge(es["oh"], 1)
            o = ps[:, 6, 0:(B + 1) * E]
            pe.matmul(o, upper[:, :], oh[:, :, :].rearrange("p b e -> p (b e)"), start=True, stop=False)
            for j in range(B):
                i = pe.matmul(o[:, (j + 1) * E:].rearrange("p (b e) -> p b e", e=E), ones[:, :], oh[:, j:j + 1, :].to_broadcast([P, B - j, E]), start=False, stop=(j == B - 1))
            i.then_inc(es["ranks"], 1)
            pe.wait_ge(es["table"], 1)
            blocks = pe.value_load(tab[0:1, TMAX:TMAX + 1], min_val=1, max_val=TMAX)
            pe.wait_ge(es["zl"], 1)

            def gather():
                for k in range(KT):
                    o = ps[:, 0, k * P:(k + 1) * P]
                    for b in range(B):
                        pe.matmul(o, zmh[:, b, k * P:(k + 1) * P], Dm[:, b, :], start=(b == 0), stop=False)
                        i = pe.matmul(o, zml[:, b, k * P:(k + 1) * P], Dm[:, b, :], start=False, stop=(b == B - 1))
                i.then_inc(es["gather"], 1)
            pe.wait_ge(es["dm"], 1)
            gather()
            with pe.Fori(0, blocks) as t:
                def up(c):
                    pe.wait_ge(es[f"w1_in{c}"], t * 16 + 16)
                    for f in range(KT):
                        i = product(ps[:, 2 + c % 2, f * P:(f + 1) * P], lambda k: w1r[:, c, k, f * P:(f + 1) * P], lambda k: xeT[:, k, :])
                    i.then_inc(es["up"], 1)

                def down(c):
                    pe.wait_ge(es[f"w2_in{c}"], t * 16 + 16)
                    pe.wait_ge(es["h"], t * FT + (c + 1) * KT)
                    for f in range(KT):
                        i = pe.matmul(bank(4), hT[:, c % 2, f, :], w2r[:, c, f, :], start=(c == 0 and f == 0), stop=(c == CH - 1 and f == KT - 1))
                    i.then_inc(es["ring_free"], 1)
                pe.wait_ge(es["xe"], t + 1)
                up(0)
                for b in range(B):
                    i = pe.transpose(ps[:, 1, b * P:(b + 1) * P], Dm[:, b, :].bitcast(f32), ident[:, :])
                i.then_inc(es["dt_pe"], 1)
                for c in range(1, CH):
                    up(c)
                    down(c - 1)
                down(CH - 1)
                pe.wait_ge(es["dm"], t + 2)
                gather()
                pe.wait_ge(es["dt"], t + 1)
                pe.wait_ge(es["yl"], t + 1)
                for b in range(B):
                    if b == 3:
                        pe.wait_ge(es["x_moe"], t * B + 1)
                    pe.matmul(bank(5 + b % 3), DT[:, b, :], yh[:, :], start=True, stop=False)
                    pe.matmul(bank(5 + b % 3), DT[:, b, :], yl[:, :], start=False, stop=True).then_inc(es["mixed"], 1)


def kernel(**inputs):
    import numpy as _np
    import concourse.bacc as _bacc
    from concourse import mybir as _mybir
    from concourse.bass_utils import run_bass_kernel_spmd as _run

    nc = _bacc.Bacc("TRN2", target_bir_lowering=False, num_devices=1)
    arrays, args = {}, {}
    for name, value in inputs.items():
        v = _np.ascontiguousarray(value)
        if v.dtype == _np.bool_:
            v = v.view(_np.int32)
        arrays[f"in_{name}"] = v
        args[name] = nc.dram_tensor(f"in_{name}", v.shape, _mybir.dt.from_np(v.dtype), kind="ExternalInput").ap()
    angles = _np.outer(_np.arange(N, dtype=_np.float32), (1.0 / 10000.0 ** (_np.arange(0, HD, 2, dtype=_np.float32) / HD)).astype(_np.float32))
    table = _np.stack([_np.cos(angles), _np.sin(angles), -_np.sin(angles)], axis=1).astype(_np.float32)
    bits = table.view(_np.uint32)
    table = ((bits + 0x7FFF + ((bits >> 16) & 1)) & _np.uint32(0xFFFF0000)).view(_np.float32)
    arrays["rope_table"] = table
    args["rope"] = nc.dram_tensor("rope_table", table.shape, _mybir.dt.float32, kind="ExternalInput").ap()
    res = nc.dram_tensor("out_x", (B, N, D), _mybir.dt.float32, kind="ExternalOutput").ap()
    perceiver(nc, args, res)
    r = _run(nc, [arrays], core_ids=[0])
    return r.results[0]["out_x"]
```
